# Optimizing a Trainium2 kernel written in Bass

```python
import numpy as np
import jax
import jax.numpy as jnp

def _softmax(x, axis=-1):
    return jax.nn.softmax(x, axis=axis)

def _gelu(x):
    return jax.nn.gelu(x, approximate=True)

def _silu(x):
    return jax.nn.silu(x)

def _sigmoid(x):
    return jax.nn.sigmoid(x)

def _layernorm(x, axis=-1, eps=1e-05):
    m = jnp.mean(x, axis=axis, keepdims=True)
    v = jnp.var(x, axis=axis, keepdims=True)
    return (x - m) / jnp.sqrt(v + eps)

def _scatter_add(tgt, idx, src, axis=0):
    return tgt.at[idx].add(src)

def _segment_sum(src, seg, n):
    return jax.ops.segment_sum(src, seg, n)
kernel_name = 'mk_flamingo_gated_d2_seqx_r8_1cd242'

def setup_inputs(seed: int=0):
    np.random.seed(seed)
    _w = jnp.asarray

    def _rec_inputs():
        import jax
        import jax.numpy as jnp
        _rk = jax.random.key(seed)
        x = 7.22e-05 + 1 * jax.random.normal(jax.random.fold_in(_rk, 1), (32, 128, 128), jnp.float32)
        _lenS = 128 - jax.random.randint(jax.random.fold_in(_rk, 7), (32,), 0, max(1, 128 // 4) + 1, jnp.int32)
        _lenS2 = 77 - jax.random.randint(jax.random.fold_in(_rk, 8), (32,), 0, max(1, 77 // 4) + 1, jnp.int32)
        _ctx_1024P = jax.random.normal(jax.random.fold_in(_rk, 11), (32, 16, 128), jnp.float32)
        _ctx_1024c = jax.random.dirichlet(jax.random.fold_in(_rk, 511), 0.3 * jnp.ones((16,), jnp.float32), (32, 77))
        _ctx_1024t = jnp.einsum('bsk,bkd->bsd', _ctx_1024c, _ctx_1024P)
        _ctx_1024t = _ctx_1024t * jax.lax.rsqrt(jnp.mean(jnp.square(_ctx_1024t)) + 1e-12) * 0.953939
        ctx_1024 = 4.13588e-05 + 0.999923 * (_ctx_1024t + 0.3 * jax.random.normal(jax.random.fold_in(_rk, 611), (32, 77, 128), jnp.float32))
        _g = jax.random.normal(jax.random.fold_in(_rk, 9001), (2, 2), jnp.float32)
        _g = jnp.sign(_g) * jnp.maximum(jnp.abs(_g), 1.0) + (_g == 0) * 1.0
        g_xattn = _g[0]
        g_ffn = _g[1]
        return (x, ctx_1024, g_xattn, g_ffn)
    x, ctx_1024, g_xattn, g_ffn = _rec_inputs()

    def _L0_xattn_setup():
        import jax, jax.numpy as jnp
        import numpy as np
        DIM = 128
        HEADS = 16
        DIM_HEAD = 64
        INNER = HEADS * DIM_HEAD
        MLP = 512
        EPS = 1e-05

        def _layernorm(x, g, b):
            mu = jnp.mean(x, axis=-1, keepdims=True)
            var = jnp.mean(jnp.square(x - mu), axis=-1, keepdims=True)
            return (x - mu) * jax.lax.rsqrt(var + EPS) * g + b

        def _l2norm(x):
            n = jnp.sqrt(jnp.sum(jnp.square(x), axis=-1, keepdims=True))
            return x / jnp.maximum(n, 1e-12)

        def _split_heads(x, B, N):
            return x.reshape(B, N, HEADS, DIM_HEAD).transpose(0, 2, 1, 3)
        key = jax.random.key(seed)
        ks = jax.random.split(key, 16)
        B, N = (4, 256)
        s = 0.02
        return {'Q': jax.random.normal(ks[0], (B, N, DIM), jnp.float32), 'K': jax.random.normal(ks[1], (B, N, DIM), jnp.float32), 'V': jax.random.normal(ks[2], (B, N, DIM), jnp.float32), 'wq': jax.random.normal(ks[3], (DIM, INNER), jnp.float32) * s, 'wk': jax.random.normal(ks[4], (DIM, INNER), jnp.float32) * s, 'wv': jax.random.normal(ks[5], (DIM, INNER), jnp.float32) * s, 'wo': jax.random.normal(ks[6], (INNER, DIM), jnp.float32) * s, 'bo': jnp.zeros((DIM,), jnp.float32), 'w1': jax.random.normal(ks[7], (DIM, MLP), jnp.float32) * s, 'b1': jnp.zeros((MLP,), jnp.float32), 'w2': jax.random.normal(ks[8], (MLP, DIM), jnp.float32) * s, 'b2': jnp.zeros((DIM,), jnp.float32), 'ln1_g': jnp.ones((DIM,), jnp.float32), 'ln1_b': jnp.zeros((DIM,), jnp.float32), 'ln2_g': jnp.ones((DIM,), jnp.float32), 'ln2_b': jnp.zeros((DIM,), jnp.float32)}
    _L0_xattn_all = _L0_xattn_setup()
    _L0_xattn_in = {k: v for k, v in _L0_xattn_all.items() if k in ('wq', 'wk', 'wv', 'wo', 'bo', 'w1', 'b1', 'w2', 'b2', 'ln1_g', 'ln1_b', 'ln2_g', 'ln2_b')}
    del _L0_xattn_all

    def _L0_ffn_setup():
        import jax, jax.numpy as jnp
        import numpy as np
        H = 128
        I = 88
        E = 64
        TOP_K = 8
        NG = 8
        TOPK_GROUP = 4
        N_SHARED = 2
        ROUTED_SCALE = 2.5
        S_I = I * N_SHARED

        def _route(x, gate_w, gate_bias):
            T = x.shape[0]
            logits = x @ gate_w.T
            scores = jax.nn.sigmoid(logits)
            scores_for_choice = scores + gate_bias[None, :]
            grp = scores_for_choice.reshape(T, NG, E // NG)
            group_scores = jnp.sum(jax.lax.top_k(grp, 2)[0], axis=-1)
            _, gidx = jax.lax.top_k(group_scores, TOPK_GROUP)
            gmask = jnp.zeros((T, NG), dtype=scores.dtype).at[jnp.arange(T)[:, None], gidx].set(1.0)
            emask = jnp.repeat(gmask, E // NG, axis=1)
            masked = jnp.where(emask > 0, scores_for_choice, 0.0)
            _, topk_idx = jax.lax.top_k(masked, TOP_K)
            topk_w = jnp.take_along_axis(scores, topk_idx, axis=1)
            topk_w = topk_w / (jnp.sum(topk_w, axis=-1, keepdims=True) + 1e-20)
            topk_w = topk_w * ROUTED_SCALE
            rw = jnp.zeros((T, E), dtype=scores.dtype).at[jnp.arange(T)[:, None], topk_idx].add(topk_w)
            return rw

        def _mlp(x, gw, uw, dw):
            return jax.nn.silu(x @ gw.T) * (x @ uw.T) @ dw.T
        key = jax.random.key(seed)
        ks = jax.random.split(key, 10)
        sc = 0.02
        return {'hidden_states': jax.random.normal(ks[0], (1, 128, H), dtype=jnp.float32), 'gate_w': sc * jax.random.normal(ks[1], (E, H), dtype=jnp.float32), 'gate_bias': sc * jax.random.normal(ks[2], (E,), dtype=jnp.float32), 'Wg': sc * jax.random.normal(ks[3], (E, I, H), dtype=jnp.float32), 'Wu': sc * jax.random.normal(ks[4], (E, I, H), dtype=jnp.float32), 'Wd': sc * jax.random.normal(ks[5], (E, H, I), dtype=jnp.float32), 'Sg': sc * jax.random.normal(ks[6], (S_I, H), dtype=jnp.float32), 'Su': sc * jax.random.normal(ks[7], (S_I, H), dtype=jnp.float32), 'Sd': sc * jax.random.normal(ks[8], (H, S_I), dtype=jnp.float32)}
    _L0_ffn_all = _L0_ffn_setup()
    _L0_ffn_in = {k: v for k, v in _L0_ffn_all.items() if k in ('gate_w', 'gate_bias', 'Wg', 'Wu', 'Wd', 'Sg', 'Su', 'Sd')}
    del _L0_ffn_all

    def _L1_xattn_setup():
        import jax, jax.numpy as jnp
        import numpy as np
        DIM = 128
        SCALE_DIM = 4
        QK_DIM = DIM // SCALE_DIM
        B, S = (4, 512)
        key = jax.random.key(seed)
        ks = jax.random.split(key, 8)
        std = 1.0 / np.sqrt(DIM)
        return {'q': jax.random.normal(ks[0], (B, S, DIM), jnp.float32), 'k': jax.random.normal(ks[1], (B, S, DIM), jnp.float32), 'v': jax.random.normal(ks[2], (B, S, DIM), jnp.float32), 'Wq': jax.random.normal(ks[3], (QK_DIM, DIM), jnp.float32) * std, 'bq': jnp.zeros((QK_DIM,), jnp.float32), 'Wk': jax.random.normal(ks[4], (QK_DIM, DIM), jnp.float32) * std, 'bk': jnp.zeros((QK_DIM,), jnp.float32), 'Wv': jax.random.normal(ks[5], (DIM, DIM), jnp.float32) * std, 'bv': jnp.zeros((DIM,), jnp.float32)}
    _L1_xattn_all = _L1_xattn_setup()
    _L1_xattn_in = {k: v for k, v in _L1_xattn_all.items() if k in ('Wq', 'bq', 'Wk', 'bk', 'Wv', 'bv')}
    del _L1_xattn_all

    def _L1_ffn_setup():
        import jax, jax.numpy as jnp
        import numpy as np
        ALPHA = 1.702
        LIMIT = 7.0
        EPS = 1e-05
        E = 16
        K = 4

        def _swiglu(h):
            x_glu = jnp.minimum(h[..., ::2], LIMIT)
            x_lin = jnp.clip(h[..., 1::2], LIMIT, LIMIT)
            return x_glu * jax.nn.sigmoid(ALPHA * x_glu) * (x_lin + 1.0)
        key = jax.random.key(seed)
        ks = jax.random.split(key, 7)
        B, T, H, I = (1, 256, 128, 128)
        x = jax.random.normal(ks[0], (B, T, H), jnp.float32)
        scale = jnp.ones((H,), jnp.float32)
        gate_w = jax.random.normal(ks[1], (E, H), jnp.float32) * 0.02
        gate_b = jnp.zeros((E,), jnp.float32)
        mlp1_w = jax.random.normal(ks[2], (E, 2 * I, H), jnp.float32) * 0.02
        mlp1_b = jax.random.normal(ks[3], (E, 2 * I), jnp.float32) * 0.02
        mlp2_w = jax.random.normal(ks[4], (E, H, I), jnp.float32) * 0.02
        mlp2_b = jax.random.normal(ks[5], (E, H), jnp.float32) * 0.02
        return dict(x=x, scale=scale, gate_w=gate_w, gate_b=gate_b, mlp1_w=mlp1_w, mlp1_b=mlp1_b, mlp2_w=mlp2_w, mlp2_b=mlp2_b)
    _L1_ffn_all = _L1_ffn_setup()
    _L1_ffn_in = {k: v for k, v in _L1_ffn_all.items() if k in ('scale', 'gate_w', 'gate_b', 'mlp1_w', 'mlp1_b', 'mlp2_w', 'mlp2_b')}
    del _L1_ffn_all
    return {'x': x, 'ctx_1024': ctx_1024, 'g_xattn': g_xattn, 'g_ffn': g_ffn, 'L0_xattn_wq': _L0_xattn_in['wq'], 'L0_xattn_wk': _L0_xattn_in['wk'], 'L0_xattn_wv': _L0_xattn_in['wv'], 'L0_xattn_wo': _L0_xattn_in['wo'], 'L0_xattn_bo': _L0_xattn_in['bo'], 'L0_xattn_w1': _L0_xattn_in['w1'], 'L0_xattn_b1': _L0_xattn_in['b1'], 'L0_xattn_w2': _L0_xattn_in['w2'], 'L0_xattn_b2': _L0_xattn_in['b2'], 'L0_xattn_ln1_g': _L0_xattn_in['ln1_g'], 'L0_xattn_ln1_b': _L0_xattn_in['ln1_b'], 'L0_xattn_ln2_g': _L0_xattn_in['ln2_g'], 'L0_xattn_ln2_b': _L0_xattn_in['ln2_b'], 'L0_ffn_gate_w': _L0_ffn_in['gate_w'], 'L0_ffn_gate_bias': _L0_ffn_in['gate_bias'], 'L0_ffn_Wg': _L0_ffn_in['Wg'], 'L0_ffn_Wu': _L0_ffn_in['Wu'], 'L0_ffn_Wd': _L0_ffn_in['Wd'], 'L0_ffn_Sg': _L0_ffn_in['Sg'], 'L0_ffn_Su': _L0_ffn_in['Su'], 'L0_ffn_Sd': _L0_ffn_in['Sd'], 'L1_xattn_Wq': _L1_xattn_in['Wq'], 'L1_xattn_bq': _L1_xattn_in['bq'], 'L1_xattn_Wk': _L1_xattn_in['Wk'], 'L1_xattn_bk': _L1_xattn_in['bk'], 'L1_xattn_Wv': _L1_xattn_in['Wv'], 'L1_xattn_bv': _L1_xattn_in['bv'], 'L1_ffn_scale': _L1_ffn_in['scale'], 'L1_ffn_gate_w': _L1_ffn_in['gate_w'], 'L1_ffn_gate_b': _L1_ffn_in['gate_b'], 'L1_ffn_mlp1_w': _L1_ffn_in['mlp1_w'], 'L1_ffn_mlp1_b': _L1_ffn_in['mlp1_b'], 'L1_ffn_mlp2_w': _L1_ffn_in['mlp2_w'], 'L1_ffn_mlp2_b': _L1_ffn_in['mlp2_b']}

def reference(x, ctx_1024, g_xattn, g_ffn, L0_xattn_wq, L0_xattn_wk, L0_xattn_wv, L0_xattn_wo, L0_xattn_bo, L0_xattn_w1, L0_xattn_b1, L0_xattn_w2, L0_xattn_b2, L0_xattn_ln1_g, L0_xattn_ln1_b, L0_xattn_ln2_g, L0_xattn_ln2_b, L0_ffn_gate_w, L0_ffn_gate_bias, L0_ffn_Wg, L0_ffn_Wu, L0_ffn_Wd, L0_ffn_Sg, L0_ffn_Su, L0_ffn_Sd, L1_xattn_Wq, L1_xattn_bq, L1_xattn_Wk, L1_xattn_bk, L1_xattn_Wv, L1_xattn_bv, L1_ffn_scale, L1_ffn_gate_w, L1_ffn_gate_b, L1_ffn_mlp1_w, L1_ffn_mlp1_b, L1_ffn_mlp2_w, L1_ffn_mlp2_b):
    import jax
    import jax.numpy as jnp

    def _L0_xattn_ref(Q, K, V, wq, wk, wv, wo, bo, w1, b1, w2, b2, ln1_g, ln1_b, ln2_g, ln2_b):
        import jax, jax.numpy as jnp
        import numpy as np
        DIM = 128
        HEADS = 16
        DIM_HEAD = 64
        INNER = HEADS * DIM_HEAD
        MLP = 512
        EPS = 1e-05

        def _layernorm(x, g, b):
            mu = jnp.mean(x, axis=-1, keepdims=True)
            var = jnp.mean(jnp.square(x - mu), axis=-1, keepdims=True)
            return (x - mu) * jax.lax.rsqrt(var + EPS) * g + b

        def _l2norm(x):
            n = jnp.sqrt(jnp.sum(jnp.square(x), axis=-1, keepdims=True))
            return x / jnp.maximum(n, 1e-12)

        def _split_heads(x, B, N):
            return x.reshape(B, N, HEADS, DIM_HEAD).transpose(0, 2, 1, 3)
        B, Nq, _ = Q.shape
        Nk = K.shape[1]
        Qn = _layernorm(Q, ln1_g, ln1_b)
        Kn = _layernorm(K, ln1_g, ln1_b)
        Vn = _layernorm(V, ln1_g, ln1_b)
        q = _split_heads(Qn @ wq, B, Nq)
        k = _split_heads(Kn @ wk, B, Nk)
        v = _split_heads(Vn @ wv, B, Nk)
        qn = _l2norm(q)
        kn = _l2norm(k)
        attn = jnp.einsum('bhqd,bhkd->bhqk', qn, kn)
        out = jnp.einsum('bhqk,bhkd->bhqd', attn, v)
        out = out.transpose(0, 2, 1, 3).reshape(B, Nq, INNER)
        x = Q + out @ wo + bo
        xn = _layernorm(x, ln2_g, ln2_b)
        h = jax.nn.gelu(xn @ w1 + b1, approximate=False)
        return x + h @ w2 + b2

    def _L0_ffn_ref(hidden_states, gate_w, gate_bias, Wg, Wu, Wd, Sg, Su, Sd):
        import jax, jax.numpy as jnp
        import numpy as np
        H = 128
        I = 88
        E = 64
        TOP_K = 8
        NG = 8
        TOPK_GROUP = 4
        N_SHARED = 2
        ROUTED_SCALE = 2.5
        S_I = I * N_SHARED

        def _route(x, gate_w, gate_bias):
            T = x.shape[0]
            logits = x @ gate_w.T
            scores = jax.nn.sigmoid(logits)
            scores_for_choice = scores + gate_bias[None, :]
            grp = scores_for_choice.reshape(T, NG, E // NG)
            group_scores = jnp.sum(jax.lax.top_k(grp, 2)[0], axis=-1)
            _, gidx = jax.lax.top_k(group_scores, TOPK_GROUP)
            gmask = jnp.zeros((T, NG), dtype=scores.dtype).at[jnp.arange(T)[:, None], gidx].set(1.0)
            emask = jnp.repeat(gmask, E // NG, axis=1)
            masked = jnp.where(emask > 0, scores_for_choice, 0.0)
            _, topk_idx = jax.lax.top_k(masked, TOP_K)
            topk_w = jnp.take_along_axis(scores, topk_idx, axis=1)
            topk_w = topk_w / (jnp.sum(topk_w, axis=-1, keepdims=True) + 1e-20)
            topk_w = topk_w * ROUTED_SCALE
            rw = jnp.zeros((T, E), dtype=scores.dtype).at[jnp.arange(T)[:, None], topk_idx].add(topk_w)
            return rw

        def _mlp(x, gw, uw, dw):
            return jax.nn.silu(x @ gw.T) * (x @ uw.T) @ dw.T
        B, S, _ = hidden_states.shape
        x = hidden_states.reshape(B * S, H)
        rw = _route(x, gate_w, gate_bias)
        expert_out = jax.vmap(lambda gw_, uw_, dw_: _mlp(x, gw_, uw_, dw_))(Wg, Wu, Wd)
        routed = jnp.einsum('eth,te->th', expert_out, rw)
        shared = _mlp(x, Sg, Su, Sd)
        out = (routed + shared).reshape(B, S, H)
        return out

    def _L1_xattn_ref(q, k, v, Wq, bq, Wk, bk, Wv, bv):
        import jax, jax.numpy as jnp
        import numpy as np
        DIM = 128
        SCALE_DIM = 4
        QK_DIM = DIM // SCALE_DIM
        B, S = (4, 512)
        scale = jnp.asarray(np.sqrt(QK_DIM), q.dtype)
        qp = jnp.einsum('bsd,ed->bse', q, Wq) + bq
        kp = jnp.einsum('bsd,ed->bse', k, Wk) + bk
        vp = jnp.einsum('bsd,ed->bse', v, Wv) + bv
        z = jnp.einsum('bqe,bke->bqk', qp, kp)
        z = jax.nn.sigmoid(z / scale)
        return jnp.einsum('bqk,bkd->bqd', z, vp)

    def _L1_ffn_ref(x, scale, gate_w, gate_b, mlp1_w, mlp1_b, mlp2_w, mlp2_b):
        import jax, jax.numpy as jnp
        import numpy as np
        ALPHA = 1.702
        LIMIT = 7.0
        EPS = 1e-05
        E = 16
        K = 4

        def _swiglu(h):
            x_glu = jnp.minimum(h[..., ::2], LIMIT)
            x_lin = jnp.clip(h[..., 1::2], LIMIT, LIMIT)
            return x_glu * jax.nn.sigmoid(ALPHA * x_glu) * (x_lin + 1.0)
        t = x * jax.lax.rsqrt(jnp.mean(x * x, axis=-1, keepdims=True) + EPS) * scale
        g = jnp.einsum('bth,eh->bte', t, gate_w) + gate_b
        vals, idx = jax.lax.top_k(g, K)
        w = jax.nn.softmax(vals, axis=-1)
        route = jnp.sum(jax.nn.one_hot(idx, E, dtype=t.dtype) * w[..., None], axis=-2)
        route_e = jnp.moveaxis(route, -1, 0)

        def step(acc, p):
            w1, b1, w2, b2, r = p
            h = jnp.einsum('bth,ih->bti', t, w1) + b1
            s = _swiglu(h)
            y = jnp.einsum('bti,hi->bth', s, w2) + b2
            return (acc + r[..., None] * y, None)
        acc, _ = jax.lax.scan(step, jnp.zeros_like(x), (mlp1_w, mlp1_b, mlp2_w, mlp2_b, route_e))
        return x + acc
    x = x + jnp.tanh(g_xattn[0]) * _L0_xattn_ref(_layernorm(x, axis=-1), ctx_1024, ctx_1024, L0_xattn_wq, L0_xattn_wk, L0_xattn_wv, L0_xattn_wo, L0_xattn_bo, L0_xattn_w1, L0_xattn_b1, L0_xattn_w2, L0_xattn_b2, L0_xattn_ln1_g, L0_xattn_ln1_b, L0_xattn_ln2_g, L0_xattn_ln2_b)
    x = x + jnp.tanh(g_ffn[0]) * _L0_ffn_ref(_layernorm(x, axis=-1), L0_ffn_gate_w, L0_ffn_gate_bias, L0_ffn_Wg, L0_ffn_Wu, L0_ffn_Wd, L0_ffn_Sg, L0_ffn_Su, L0_ffn_Sd)
    x = x + jnp.tanh(g_xattn[1]) * _L1_xattn_ref(_layernorm(x, axis=-1), ctx_1024, ctx_1024, L1_xattn_Wq, L1_xattn_bq, L1_xattn_Wk, L1_xattn_bk, L1_xattn_Wv, L1_xattn_bv)
    x = x + jnp.tanh(g_ffn[1]) * _L1_ffn_ref(_layernorm(x, axis=-1), L1_ffn_scale, L1_ffn_gate_w, L1_ffn_gate_b, L1_ffn_mlp1_w, L1_ffn_mlp1_b, L1_ffn_mlp2_w, L1_ffn_mlp2_b)
    return x

_drawn_inputs = setup_inputs


def setup_inputs(seed=0):
    import zlib

    import numpy as np

    out = dict(_drawn_inputs(seed))
    spreads = {'g_ffn': (-1.0, 0.6),
     'L0_xattn_bo': (0.0, 0.68),
     'L0_xattn_b1': (0.0, 0.8),
     'L0_xattn_b2': (0.0, 0.8),
     'L0_xattn_ln1_g': (1.0, 0.6),
     'L0_xattn_ln1_b': (0.0, 0.561),
     'L0_xattn_ln2_g': (1.0, 0.6),
     'L0_xattn_ln2_b': (0.0, 0.8),
     'L1_xattn_bq': (0.0, 0.32),
     'L1_xattn_bk': (0.0, 0.1),
     'L1_xattn_bv': (0.0, 0.1),
     'L1_ffn_scale': (1.0, 0.6),
     'L1_ffn_gate_b': (0.0, 0.8)}
    factors = {'L0_xattn_w1': 8.0,
     'L0_xattn_w2': 7.704,
     'L0_ffn_gate_w': 8.0,
     'L0_ffn_gate_bias': 8.0,
     'L0_ffn_Wg': 8.0,
     'L0_ffn_Wu': 8.0,
     'L0_ffn_Wd': 8.0,
     'L0_ffn_Sg': 8.0,
     'L0_ffn_Su': 8.0,
     'L0_ffn_Sd': 8.0,
     'L1_ffn_gate_w': 8.0,
     'L1_ffn_mlp1_w': 8.0,
     'L1_ffn_mlp1_b': 8.0,
     'L1_ffn_mlp2_w': 8.0,
     'L1_ffn_mlp2_b': 64.0}
    for name, (base, spread) in spreads.items():
        noise = np.random.default_rng([zlib.crc32(name.encode()), seed]).standard_normal(out[name].shape)
        drawn = base * np.exp(spread * noise) if base else spread * noise
        out[name] = jnp.asarray(drawn.astype(out[name].dtype))
    for name, factor in factors.items():
        out[name] = (out[name] * factor).astype(out[name].dtype)
    return out
```

```python
import math
from contextlib import ExitStack

import numpy as np

import concourse.bass as bass
from concourse import mybir

F32 = mybir.dt.float32
BF16 = mybir.dt.bfloat16
I32 = mybir.dt.int32
U32 = mybir.dt.uint32
ALU = mybir.AluOpType
ACT = mybir.ActivationFunctionType
AX_X = mybir.AxisListType.X

P = 128
D = 128
B = 32
NC_CTX = 77
H, DH = 16, 64
INNER = H * DH
MLP = 512
E, NG, EI = 64, 8, 88
TOPK, TOPG = 8, 4
E1, K1 = 16, 4
QK = 32
EPS = 1e-5
CHUNKS = 2
TC = B // CHUNKS
G = 4
GC = TC // G
SLOTS = TC * P * TOPK // P + E
SS = SLOTS // G
ROW = D + E
BIG = 65536.0
GONE = -1e30
LIMIT, ALPHA = 7.0, 1.702

V_LN1G, V_LN1B, V_LN2G, V_LN2B, V_B1, V_SCALE, V_BM1 = 0, 1, 2, 3, 4, 8, 9
V_BQ, V_BK, V_GATES, V_END = 25, 26, 27, 31
R_LN1G, R_LN1B, R_BO, R_B2, R_BV, R_GBIAS, R_GB1, R_END = 0, 128, 256, 384, 512, 640, 704, 720
C_ID, C_UP, C_LOW, C_STEP, C_SLOT, C_HOT, C_END = 0, 128, 256, 320, 336, 338, 338 + E1 * P


class Steps:

    def __init__(self, sem, eng):
        self.sem, self.eng, self.base, self.k = sem, eng, 0, 0

    def done(self, ins):
        ins.then_inc(self.sem, 1)
        self.k += 1

    def wait(self):
        self.eng.wait_ge(self.sem, self.base + self.k)

    def step(self, ins):
        self.done(ins)
        self.wait()

    def loop(self, lo, hi, body, per):
        start = self.base + self.k
        with self.eng.Fori(lo, hi) as i:
            self.base, self.k = (i - lo) * per + start, 0
            body(i)
            assert self.k == per, self.k
        self.base, self.k = start + (hi - lo) * per, 0


def build(nc, a):
    one = lambda i: bass.ds(i, 1)
    ctx = ExitStack()
    with ctx:
        def sb(name, shape, dt=F32):
            return ctx.enter_context(nc.sbuf_tensor("sb_" + name, shape, dt))

        def sem(name):
            return ctx.enter_context(nc.semaphore(name))

        X = sb("X", [P, B, D])
        Yf = sb("Y", [P, B * D])
        Y = Yf[:, :].rearrange("p (b d) -> p b d", b=B)
        XR = sb("XR", [P, TC, ROW])
        WGU = sb("WGU", [P, E, 2 * EI])
        RW_ = sb("RW", [P, E * D])
        WD = RW_[0:EI, :].rearrange("p (e d) -> p e d", e=E)
        CTX = RW_[0:NC_CTX, 0:B * D].rearrange("p (b d) -> p b d", b=B)
        WVT = RW_[0:DH, B * D:B * D + H * D].rearrange("p (h d) -> p h d", h=H)
        WO = RW_[0:DH, B * D + H * D:B * D + 2 * H * D].rearrange("p (h d) -> p h d", h=H)
        AW = sb("AW", [P, 4096])
        WQ, WK = AW[:, 0:1024], AW[:, 1024:2048]
        WH = AW[:, 2048:4096].rearrange("p (h d) -> p h d", h=H)
        A1 = sb("A1", [P, 7 * 1024])
        RT5 = sb("RT5", [P, 5 * 1024])
        W1 = sb("W1", [P, MLP])
        W2 = sb("W2", [P, MLP])
        VEC = sb("VEC", [P, V_END])
        ROWS = sb("ROWS", [P, R_END])
        CON = sb("CON", [P, C_HOT])
        TG = sb("TG", [P, 4])
        GWT = sb("GWT", [P, E])
        SGW = sb("SGW", [P, 4, EI])
        SDW = sb("SDW", [EI, 2, D])
        UPB = sb("UPB", [P, P], BF16)
        ONB = sb("ONB", [P, P], BF16)
        SELB = sb("SELB", [P, TC, E], BF16)
        CSB = sb("CSB", [P, TC, E], BF16)
        POS = sb("POS", [P, B * TOPK], U32)
        TE = sb("TE", [P, CHUNKS, 2], I32)
        TER = sb("TER", [1, CHUNKS * SLOTS], I32)
        ZT = sb("ZT", [P, G * D])
        BS = sb("BS", [P, TC, 6])
        BSC = sb("BSC", [P, TC, 6])
        ST = sb("ST", [P, 12, TC])
        N2 = sb("N2", [P, 2 * H])
        RN = sb("RN", [P, 2 * H])
        NT = sb("NT", [P, 4, E])
        PS = ctx.enter_context(nc.psum_tensor("PS", [P, 8, 512], F32))

        ID = CON[:, C_ID:C_ID + P]
        SQQ, SQK, QN, KN, QT, PB, GB = (A1[:, 1024 * i:1024 * (i + 1)] for i in range(7))
        ZC, VN = RT5[0:NC_CTX, 1024:1024 + D], RT5[0:NC_CTX, 1152:1152 + D]
        QNT, KNT = RT5[:, 1280:1280 + D], RT5[:, 1408:1408 + NC_CTX]
        ZERO = RT5[:, 0:ROW]
        HT = A1[:, 0:2048].rearrange("p (c n) -> p c n", c=4)
        XT = A1[:, 2048:2560]
        TMP = A1[:, 2560:3072]
        SIL = A1[0:EI, 3072:4096].rearrange("p (c n) -> p c n", c=2)
        SHH = A1[0:EI, 4096:5120].rearrange("p (c n) -> p c n", c=2)
        RS, RC, RA, RB, RK = (RT5[:, 1024 * i:1024 * (i + 1)] for i in range(5))
        XB = [A1[:, 768 * i:768 * (i + 1)].rearrange("p (t n) -> p t n", t=G) for i in range(4)]
        EXT = A1[:, 3072:3584]
        ESI = A1[:, 3584:3584 + G * EI].rearrange("p (t n) -> p t n", t=G)
        EH = A1[:, 4096:4096 + G * EI].rearrange("p (t n) -> p t n", t=G)
        EHT = [A1[0:EI, 4608 + 512 * i:5120 + 512 * i] for i in range(2)]
        YB = [A1[:, 5632 + 512 * i:6144 + 512 * i].rearrange("p (t n) -> p t n", t=G) for i in range(2)]
        W1E = RT5[:, 0:2048].rearrange("p (e n) -> p e n", e=E1)
        W2E = RT5[:, 2048:4096].rearrange("p (e n) -> p e n", e=E1)
        LW = RT5[:, 4096:5120]
        WQT, WKT, WVT1, GW1 = LW[:, 0:32], LW[:, 32:64], LW[:, 64:192], LW[:, 192:208]
        B2S = LW[0:48, 208:336]
        HOT = XR[0:48, :, :].rearrange("p t n -> p (t n)")[:, 0:E1 * P // 2].bitcast(BF16)
        HOTF = AW[0:48, 0:2048]
        GBUF = [Yf[:, 1024 * i:1024 * (i + 1)] for i in range(4)]
        CG = AW[0:NC_CTX, 0:512].rearrange("p (t n) -> p t n", t=G)
        CT = AW[:, 512:512 + G * NC_CTX]
        KP = AW[0:QK, 1024:1024 + G * NC_CTX]
        VP = AW[0:NC_CTX, 1536:2048].rearrange("p (t n) -> p t n", t=G)
        QP = AW[0:QK, 2048:2560]
        ZS = AW[0:NC_CTX, 2560:3072]
        TTT = AW[:, 3072:3584]
        HM = [A1[:, 512 * i:512 * (i + 1)] for i in range(2)]
        SG = [A1[:, 1024 + 512 * i:1536 + 512 * i] for i in range(2)]
        XTL = A1[:, 2048:2560]
        SX = [A1[:, 3072 + 512 * i:3584 + 512 * i] for i in range(2)]
        AT = A1[:, 4096:4608]
        RTF = A1[0:48, 4608:5120]
        RTB = A1[0:48, 6656:6912].bitcast(BF16)
        RED = A1[:, 5120:5632]
        GR = A1[:, 5632:6144]
        MR = A1[:, 6144:6656]
        HIB = A1[:, 6912:6944].bitcast(BF16).rearrange("p (t e) -> p t e", t=G)

        xs = [nc.dram_tensor(f"sorted_rows{c}", [SLOTS * P, ROW], F32).ap() for c in range(CHUNKS)]
        ys = [nc.dram_tensor(f"sorted_out{c}", [SLOTS * P, D], F32).ap() for c in range(CHUNKS)]
        te_d = nc.dram_tensor("slot_experts", [CHUNKS, SLOTS], I32).ap()

        ld_c, ld_x, ld_w, ld_m, ld_r, ld_wgu, ld_wd, ld_l, ld_hot = (sem(n) for n in (
            "ld_const", "ld_tokens", "ld_attn", "ld_mlp", "ld_route", "ld_wgu", "ld_wd", "ld_layer2", "ld_hot"))
        zeroed = sem("zeroed")
        dstep, astep = sem("dve_step"), sem("act_step")
        gates, wh_mm, wh_ok = sem("gates"), sem("wh_mm"), sem("wh_ok")
        cbf = sem("const_bf16")
        a_z, a_vn, a_t, a_qk, a_q, a_k, a_sq, a_n2, a_rt, a_qn, a_kn = (sem("attn_" + n) for n in (
            "z", "vn", "zT", "zT_out", "q", "k", "squares", "sums", "roots", "qn", "kn"))
        a_qt, a_qte, a_p, a_pe, a_g, a_ge, a_o, a_y = (sem("attn_" + n) for n in (
            "qT", "qT_out", "p", "p_out", "g", "g_out", "o", "y"))
        m_z, m_t, m_te, m_h, m_he, m_o, m_x = (sem("mlp_" + n) for n in (
            "z", "zT", "zT_out", "h", "gelu", "o", "x"))
        r_z, r_zc, r_t, r_te, r_l, r_le, r_gu, r_si, r_h, r_o, r_x = (sem("rt_" + n) for n in (
            "z", "z_row", "zT", "zT_out", "logit", "logit_out", "gu", "silu", "h", "o", "x"))
        t_s, t_sel, t_rank, t_pos, t_te, t_ted, t_ter, t_rw = (sem("tab_" + n) for n in (
            "sigmoid", "chosen", "ranks", "pos", "slots", "slots_dram", "slots_row", "rows"))
        p_cp, p_sc = sem("pool_copy"), [sem(f"scatter{i}") for i in range(2)]
        e_ld = [sem(f"ex_load{i}") for i in range(4)]
        e_t, e_te, e_gu, e_si, e_h, e_ht, e_hte, e_y, e_ye = (sem("ex_" + n) for n in (
            "xT", "xT_out", "gu", "silu", "h", "hT", "hT_out", "y", "y_out"))
        e_st = [sem(f"ex_store{i}") for i in range(2)]
        l_g = [sem(f"l2_gather{i}") for i in range(4)]
        l_red, l_cg, l_fin, l_out = sem("l2_reduced"), sem("l2_ctx"), sem("l2_final"), sem("l2_stored")
        l_dve = sem("l2_hot")
        l_h, l_hm, l_sg, l_sx, l_bc, l_y = (sem("l2_" + n) for n in ("h", "hmin", "glu", "weighted", "bcast", "y"))
        n_z, n_t, n_te, n_q, n_qe, n_ct, n_cte, n_kv, n_kpe, n_vpe, n_s, n_se, n_sh, n_o = (sem("l2f_" + n) for n in (
            "z", "zT", "zT_out", "q", "q_out", "ctxT", "ctxT_out", "kv", "k_out", "v_out", "scores", "tanh",
            "sigmoid", "o"))
        n_z2, n_t2, n_t2e, n_g, n_d, n_de, n_r, n_rt, n_rte, n_acce, n_f = (sem("l2r_" + n) for n in (
            "z", "zT", "zT_out", "gate", "diff", "silu", "weights", "wT", "wT_out", "sum_out", "sumT"))

        block = ctx.enter_context(nc.Block())

        def bank(n, k=1, p0=0, p1=P):
            return PS[p0:p1, n:n + k, :].rearrange("p a n -> p (a n)")

        gu_bank = [PS[:, 1 + 2 * u:3 + 2 * u, :].rearrange("p a (c n) -> p (a c) n", c=2) for u in range(2)]

        def chunk_tiles(c):
            return c * TC, (c + 1) * TC

        NGR = B // G

        def t3(x, n=G):
            return x.rearrange("p (t e) -> p t e", t=n)

        GL = GR[:, 0:80].rearrange("p (t e) -> p t e", t=G)
        GM8 = GR[:, 80:112].rearrange("p (t e) -> p t e", t=G)
        GO = GR[:, 112:192].rearrange("p (t e) -> p t e", t=G)
        GD, GSA, GSB, GSEL = (GR[:, 192 + 64 * i:256 + 64 * i] for i in range(4))
        GSUM = GR[:, 448:452]
        R48 = MR[:, 0:192].rearrange("p (t j e) -> p t j e", t=G, j=3)

        def layer2_act(act):
            def front(g):
                act.wait_ge(n_t, g + 1)
                nc.scalar.activation(XTL, bank(0), ACT.Copy).then_inc(n_te, 1)
                act.wait_ge(n_ct, g + 1)
                nc.scalar.activation(CT, bank(7)[:, 0:G * NC_CTX], ACT.Copy).then_inc(n_cte, 1)
                act.wait_ge(n_q, g + 1)
                nc.scalar.activation(QP, bank(6, 1, 0, QK), ACT.Identity, bias=VEC[0:QK, V_BQ:V_BQ + 1]).then_inc(n_qe, 1)
                act.wait_ge(n_kv, g + 1)
                nc.scalar.activation(KP, bank(0, 1, 0, QK)[:, 0:G * NC_CTX], ACT.Identity,
                                     bias=VEC[0:QK, V_BK:V_BK + 1]).then_inc(n_kpe, 1)
                act.wait_ge(n_s, g + 1)
                nc.scalar.activation(ZS, bank(7, 1, 0, NC_CTX), ACT.Tanh, scale=0.5 / math.sqrt(QK)).then_inc(n_se, 1)
                act.wait_ge(n_t2, g + 1)
                nc.scalar.activation(TTT, bank(6), ACT.Identity, scale=VEC[:, V_SCALE:V_SCALE + 1]).then_inc(n_t2e, 1)
                act.wait_ge(n_d, g + 1)
                nc.scalar.activation(GSA, GD, ACT.Silu)
                nc.scalar.activation(GSB, GD, ACT.Silu, scale=-1.0).then_inc(n_de, 1)
                act.wait_ge(n_rt, g + 1)
                nc.scalar.activation(RTF, bank(0, 1, 0, 48), ACT.Copy)
                nc.scalar.activation(RTB, bank(0, 1, 0, 48), ACT.Copy).then_inc(n_rte, 1)

            def experts(g):
                for e in range(E1):
                    act.wait_ge(l_hm, g * E1 + (e + 3))
                    act.wait_ge(l_sx, g * E1 + (e + 1))
                    nc.scalar.activation(SG[e % 2], HM[e % 2], ACT.Silu, scale=ALPHA).then_inc(l_sg, 1)
                act.wait_ge(l_y, g * E1 + (E1 + 2))
                nc.scalar.activation(AT, bank(5), ACT.Copy).then_inc(n_acce, 1)

            act.sem_inc(l_sg, 2)
            with act.Fori(0, NGR) as g:
                front(g)
                experts(g)

        def layer2_dve(dve, S, rsqrt, mean_rstd, second_norm):
            v = nc.vector
            dve.wait_ge(ld_hot, 16)
            v.tensor_copy(HOT, HOTF).then_inc(l_dve, 1)
            dve.wait_ge(ld_l, 16 * 7)
            dve.sem_inc(l_fin, 1)
            dve.sem_inc(l_hm, 2)
            dve.sem_inc(l_sx, 2)
            for i in range(2):
                dve.wait_ge(e_st[i], 16 * (SS // 2) * CHUNKS)
            S.done(v.memset(GL[:, :, E1:E1 + 4], GONE))
            q4 = [ST[:, i, 0:G] for i in range(9)]
            mean, rstd, var, both, t1, t2 = q4[:6]

            def settle():
                v.memset(NT[:, 2, 0:1], 0.0)

            def stats(tiles, rms):
                settle()
                for t in range(G):
                    ins = v.bn_stats(BS[:, t, :], X[:, tiles * G + t, :])
                S.step(ins)
                mean_rstd(BS[:, 0:G, :], mean, rstd, var, t1)
                if rms:
                    second_norm(var, rstd, both, t1, t2)

            def front(g):
                tiles = bass.ds(g * G, G)
                for t in range(G):
                    dve.wait_ge(l_g[t], g * (16 * TOPK) + 16 * TOPK)
                    v.tensor_reduce(RED[:, t * D:(t + 1) * D], GBUF[t].rearrange("p (k d) -> p d k", k=TOPK),
                                    AX_X, ALU.add).then_inc(l_red, 1)
                dve.wait_ge(l_red, g * G + G)
                S.step(v.scalar_tensor_tensor(X[:, tiles, :], t3(RED), TG[:, 1:2], X[:, tiles, :], ALU.mult, ALU.add))
                stats(g, False)
                for t in range(G):
                    ins = v.tensor_scalar(ZT[:, t * D:(t + 1) * D], X[:, g * G + t, :], mean[:, t:t + 1],
                                          rstd[:, t:t + 1], ALU.subtract, ALU.mult)
                ins.then_inc(n_z, 1)
                dve.wait_ge(n_kv, g + 1)
                v.tensor_tensor(VP, bank(6, 1, 0, NC_CTX).rearrange("p (t n) -> p t n", t=G),
                                ROWS[0:NC_CTX, R_BV:R_BV + D].unsqueeze(1).to_broadcast([NC_CTX, G, D]),
                                ALU.add).then_inc(n_vpe, 1)
                dve.wait_ge(n_se, g + 1)
                v.tensor_scalar(ZS, ZS, 0.5, 0.5, ALU.mult, ALU.add).then_inc(n_sh, 1)
                dve.wait_ge(n_o, g + 1)
                S.step(v.scalar_tensor_tensor(X[:, tiles, :], t3(bank(0)), TG[:, 2:3], X[:, tiles, :],
                                              ALU.mult, ALU.add))
                stats(g, True)
                for t in range(G):
                    ins = v.tensor_scalar(ZT[:, t * D:(t + 1) * D], X[:, g * G + t, :], mean[:, t:t + 1],
                                          both[:, t:t + 1], ALU.subtract, ALU.mult)
                ins.then_inc(n_z2, 1)
                S.step(v.tensor_scalar(t1, rstd, TG[:, 3:4], None, ALU.mult))
                S.done(v.tensor_tensor(t2, t1, mean, ALU.mult))
                S.step(v.tensor_scalar(t1, t1, 1.0, None, ALU.add))
                for t in range(G):
                    ins = v.tensor_scalar(X[:, g * G + t, :], X[:, g * G + t, :], t1[:, t:t + 1], t2[:, t:t + 1],
                                          ALU.mult, ALU.subtract)
                S.done(ins)
                dve.wait_ge(n_g, g + 1)
                S.step(v.tensor_tensor(GL[:, :, 0:E1], t3(bank(7)[:, 0:G * E1]),
                                       ROWS[:, R_GB1:R_GB1 + E1].unsqueeze(1).to_broadcast([P, G, E1]), ALU.add))
                settle()
                for t in range(G):
                    ins = v.max(GM8[:, t, :], GL[:, t, 0:E1])
                S.step(ins)
                S.step(v.tensor_tensor(t3(GD), GL[:, :, 0:E1], GM8[:, :, 0:1].to_broadcast([P, G, E1]), ALU.subtract))
                v.tensor_scalar(GD, GD, -1.0, None, ALU.add).then_inc(n_d, 1)
                S.step(v.memset(GM8[:, :, K1:8], GONE))
                settle()
                for t in range(G):
                    ins = v.match_replace(GO[:, t, :], GM8[:, t, :], GL[:, t, :], 2 * GONE)
                S.step(ins)
                S.done(v.tensor_scalar(t3(GSEL), GO[:, :, 0:E1], 2 * GONE, None, ALU.is_equal))
                dve.wait_ge(n_de, g + 1)
                S.step(v.reciprocal(GSB, GSB))
                S.step(v.tensor_tensor(GSA, GSA, GSB, ALU.mult))
                S.step(v.tensor_tensor(GSA, GSA, GSEL, ALU.mult))
                S.step(v.tensor_reduce(GSUM, t3(GSA), AX_X, ALU.add))
                S.step(v.reciprocal(GSUM, GSUM))
                S.step(v.tensor_tensor(t3(GSA), t3(GSA), GSUM.unsqueeze(2).to_broadcast([P, G, E1]), ALU.mult))
                S.step(v.tensor_copy(HIB, t3(GSA)))
                S.step(v.tensor_copy(R48[:, :, 0, :], HIB))
                S.step(v.tensor_tensor(t3(GSA), t3(GSA), R48[:, :, 0, :], ALU.subtract))
                S.step(v.tensor_copy(HIB, t3(GSA)))
                S.step(v.tensor_copy(R48[:, :, 1, :], HIB))
                v.tensor_tensor(R48[:, :, 2, :], t3(GSA), R48[:, :, 1, :], ALU.subtract).then_inc(n_r, 1)

            def experts(g):
                for e in range(E1 + 2):
                    if e < E1:
                        dve.wait_ge(l_h, g * E1 + (e + 1))
                        dve.wait_ge(l_sg, g * E1 + (e + 1))
                        v.tensor_scalar(HM[e % 2], bank(1 + e % 2), VEC[:, V_BM1 + e:V_BM1 + e + 1], LIMIT,
                                        ALU.add, ALU.min).then_inc(l_hm, 1)
                    if e >= 2:
                        k = e - 2
                        dve.wait_ge(l_sg, g * E1 + (k + 3))
                        dve.wait_ge(l_bc, g * E1 + (k + 1))
                        dve.wait_ge(l_y, g * E1 + (k + 1))
                        v.scalar_tensor_tensor(SX[k % 2], SG[k % 2], (LIMIT + 1.0) / ALPHA, bank(3 + k % 2),
                                               ALU.mult, ALU.mult).then_inc(l_sx, 1)
                dve.wait_ge(n_f, g + 1)
                tiles = bass.ds(g * G, G)
                v.scalar_tensor_tensor(X[:, tiles, :], t3(bank(5)), TG[:, 3:4], X[:, tiles, :], ALU.mult,
                                       ALU.add).then_inc(l_fin, 1)

            FRONT = 77

            def body(g):
                front(g)
                experts(g)
            S.loop(0, NGR, body, FRONT)

        def layer2_pe(pe):
            mm = nc.tensor.matmul
            pe.wait_ge(ld_l, 16 * 7)
            pe.wait_ge(l_dve, 1)
            pe.sem_inc(l_y, 2)
            def front(g):
                pe.wait_ge(n_z, g + 1)
                for t in range(G):
                    ins = nc.tensor.transpose(PS[:, 0, t * P:(t + 1) * P], ZT[:, t * D:(t + 1) * D], ID)
                ins.then_inc(n_t, 1)
                pe.wait_ge(l_cg, g * 16 + 16)
                for t in range(G):
                    ins = nc.tensor.transpose(PS[:, 7, t * NC_CTX:(t + 1) * NC_CTX], CG[:, t, :], ID[0:NC_CTX, 0:NC_CTX])
                ins.then_inc(n_ct, 1)
                pe.wait_ge(n_te, g + 1)
                mm(bank(6, 1, 0, QK), WQT, XTL, start=True, stop=True).then_inc(n_q, 1)
                pe.wait_ge(n_cte, g + 1)
                mm(bank(0, 1, 0, QK)[:, 0:G * NC_CTX], WKT, CT, start=True, stop=True)
                pe.wait_ge(n_qe, g + 1)
                for t in range(G):
                    ins = mm(PS[0:NC_CTX, 6, t * D:(t + 1) * D], CT[:, t * NC_CTX:(t + 1) * NC_CTX], WVT1,
                             start=True, stop=True)
                ins.then_inc(n_kv, 1)
                pe.wait_ge(n_kpe, g + 1)
                for t in range(G):
                    ins = mm(PS[0:NC_CTX, 7, t * P:(t + 1) * P], KP[:, t * NC_CTX:(t + 1) * NC_CTX],
                             QP[:, t * P:(t + 1) * P], start=True, stop=True)
                ins.then_inc(n_s, 1)
                pe.wait_ge(n_sh, g + 1)
                pe.wait_ge(n_vpe, g + 1)
                for t in range(G):
                    ins = mm(PS[:, 0, t * D:(t + 1) * D], ZS[:, t * P:(t + 1) * P], VP[:, t, :], start=True, stop=True)
                ins.then_inc(n_o, 1)
                pe.wait_ge(n_z2, g + 1)
                for t in range(G):
                    ins = nc.tensor.transpose(PS[:, 6, t * P:(t + 1) * P], ZT[:, t * D:(t + 1) * D], ID)
                ins.then_inc(n_t2, 1)
                pe.wait_ge(n_t2e, g + 1)
                for t in range(G):
                    ins = mm(PS[:, 7, t * E1:(t + 1) * E1], TTT[:, t * P:(t + 1) * P], GW1, start=True, stop=True)
                ins.then_inc(n_g, 1)
                pe.wait_ge(n_r, g + 1)
                nc.tensor.transpose(PS[:, 0, 0:P], MR[:, 0:P], ID)
                for t in range(G):
                    ins = nc.tensor.transpose(PS[0:48, 0, t * P:(t + 1) * P], MR[:, t * 48:(t + 1) * 48], ID)
                ins.then_inc(n_rt, 1)

            def experts(g):
                pe.wait_ge(l_fin, g + 1)
                pe.wait_ge(n_rte, g + 1)
                mm(bank(5), B2S, RTF, start=True, stop=False)
                for e in range(E1 + 3):
                    if e < E1:
                        pe.wait_ge(l_hm, g * E1 + (e + 1))
                        mm(bank(1 + e % 2), W1E[:, e, :], TTT, start=True, stop=True).then_inc(l_h, 1)
                    if 2 <= e < E1 + 2:
                        k = e - 2
                        pe.wait_ge(l_sx, g * E1 + (k + 1))
                        mm(bank(3 + k % 2), HOT[:, k * P:(k + 1) * P], RTB, start=True, stop=True).then_inc(l_bc, 1)
                    if e >= 3:
                        k = e - 3
                        pe.wait_ge(l_sx, g * E1 + (k + 3))
                        mm(bank(5), W2E[:, k, :], SX[k % 2], start=False, stop=(k == E1 - 1)).then_inc(l_y, 1)
                pe.wait_ge(n_acce, g + 1)
                for t in range(G):
                    ins = nc.tensor.transpose(PS[:, 5, t * P:(t + 1) * P], AT[:, t * P:(t + 1) * P], ID)
                ins.then_inc(n_f, 1)

            with pe.Fori(0, NGR) as g:
                front(g)
                experts(g)

        @block.sync
        def _(sp):
            for dst, name in ((CON, "con"), (VEC, "vec"), (ROWS, "rows")):
                sp.dma_start(dst[:], a[name]).then_inc(ld_c, 16)
            sp.dma_start(X[:, :, :], a["x"]).then_inc(ld_x, 16)
            sp.dma_start(CTX, a["ctx"]).then_inc(ld_x, 16)
            sp.dma_start(WVT, a["wvT"]).then_inc(ld_w, 16)
            sp.dma_start(WO, a["wo"]).then_inc(ld_w, 16)
            sp.dma_start(WQ, a["wq"]).then_inc(ld_w, 16)
            sp.dma_start(WK, a["wk"]).then_inc(ld_w, 16)
            sp.dma_start(W1[:], a["w1"]).then_inc(ld_m, 16)
            sp.dma_start(W2[:], a["w2"]).then_inc(ld_m, 16)
            sp.dma_start(GWT[:], a["gwT"]).then_inc(ld_r, 16)
            sp.dma_start(SGW[:, :, :], a["sgu"]).then_inc(ld_r, 16)
            sp.dma_start(SDW[:, :, :], a["sd"]).then_inc(ld_r, 16)
            sp.wait_ge(cbf, 1)
            for c in range(CHUNKS):
                z = ZERO.unsqueeze(1).to_broadcast([P, SLOTS, ROW])
                sp.dma_start(xs[c].rearrange("(s p) n -> p s n", p=P), z).then_inc(zeroed, 16)
            sp.dma_start(WGU[:, :, :], a["wgu"]).then_inc(ld_wgu, 16)

            for c in range(CHUNKS):
                sp.wait_ge(t_te, c + 1)
                sp.dma_start(te_d[c].rearrange("(p k) -> p k", k=2), TE[0:SLOTS // 2, c, :]).then_inc(t_ted, 16)
                sp.wait_ge(t_ted, 16 * (c + 1))
                sp.dma_start(TER[0:1, c * SLOTS:(c + 1) * SLOTS], te_d[c:c + 1, :]).then_inc(t_ter, 16)
            sp.wait_ge(a_y, B + 1)
            sp.dma_start(WD, a["wd"]).then_inc(ld_wd, 16)
            sp.wait_ge(t_rw, CHUNKS)
            for dst, name in ((W1E, "w1e"), (W2E, "w2e"), (WQT, "wqT1"), (WKT, "wkT1"), (WVT1, "wvT1"),
                              (GW1, "gw1"), (B2S, "b2s")):
                sp.dma_start(dst, a[name]).then_inc(ld_l, 16)
            sp.dma_start(HOTF, a["hot"]).then_inc(ld_hot, 16)

            def rows_of(t, step):
                return t[bass.ds(step * (G * P), G * P), :].rearrange("(t p) n -> p t n", p=P)

            for c in range(CHUNKS):
                o = c * SS
                for i in range(2):
                    sp.wait_ge(p_sc[i], 16 * TOPK * (TC // 2) * (c + 1))

                def load(i, r):
                    sp.dma_start(XB[r][:, :, :], rows_of(xs[c], i)).then_inc(e_ld[r], 16)

                def store(i, r):
                    sp.wait_ge(e_ye, o + i + 1)
                    sp.dma_start(rows_of(ys[c], i), YB[r % 2][:, :, :]).then_inc(e_st[r % 2], 16)

                if c == 0:
                    sp.wait_ge(r_x, B // G)
                for i in range(4):
                    if c:
                        sp.wait_ge(e_h, o - 4 + i + 2)
                    load(i, i)
                with sp.Fori(0, SS // 4 - 1) as q:
                    for r in range(4):
                        sp.wait_ge(e_h, q * 4 + (o + r + 2))
                        load(q * 4 + (r + 4), r)
                        store(q * 4 + r, r)
                for r in range(4):
                    store(SS - 4 + r, r)
            sp.wait_ge(l_dve, 1)
            sp.dma_start(CG[:, :, :], a["ctx"][:, 0:G, :]).then_inc(l_cg, 16)
            with sp.Fori(1, B // G) as g:
                sp.wait_ge(n_ct, g)
                sp.dma_start(CG[:, :, :], a["ctx"][:, bass.ds(g * G, G), :]).then_inc(l_cg, 16)
                sp.wait_ge(l_fin, g + 1)
                sp.dma_start(a["out"][:, bass.ds(g * G - G, G), :], X[:, bass.ds(g * G - G, G), :]).then_inc(l_out, 16)
            sp.wait_ge(l_fin, B // G + 1)
            sp.dma_start(a["out"][:, B - G:B, :], X[:, B - G:B, :]).then_inc(l_out, 16)
            sp.wait_ge(l_out, 16 * (B // G))

        @block.gpsimd
        def _(pool):
            def vn(b):
                pool.wait_ge(a_z, b + 1)
                nc.gpsimd.tensor_tensor(VN, ZC, ROWS[0:NC_CTX, R_LN1G:R_LN1G + D], ALU.mult).then_inc(p_cp, 1)
                pool.wait_ge(p_cp, b + 1)
                nc.gpsimd.tensor_tensor(VN, VN, ROWS[0:NC_CTX, R_LN1B:R_LN1B + D], ALU.add).then_inc(a_vn, 1)

            def attention(c):
                lo, hi = chunk_tiles(c)
                if c == 0:
                    vn(0)
                else:
                    pool.wait_ge(a_p, lo)
                    vn(lo)
                with pool.Fori(lo + 1, hi) as b:
                    pool.wait_ge(a_p, b)
                    vn(b)

            def rows(c):
                if c:
                    for i in range(2):
                        pool.wait_ge(p_sc[i], 16 * TOPK * (TC // 2) * c)
                with pool.Fori(c * GC, (c + 1) * GC) as g:
                    pool.wait_ge(r_z, g + 1)
                    dst = XR[:, bass.ds(g * G - c * TC, G), 0:D]
                    nc.gpsimd.tensor_copy(dst, ZT[:, :].rearrange("p (t d) -> p t d", t=G)).then_inc(r_zc, 1)

            def scatter(c):
                pool.wait_ge(t_rw, c + 1)
                pool.wait_ge(r_zc, (c + 1) * GC)
                pool.wait_ge(zeroed, 16 * CHUNKS)
                lo, _ = chunk_tiles(c)
                for t in range(TC):
                    b = lo + t
                    for k in range(TOPK):
                        pool.indirect_dma_start(
                            out=xs[c], in_=XR[:, t, :], in_offset=None,
                            out_offset=bass.IndirectOffsetOnAxis(ap=POS[:, b * TOPK + k:b * TOPK + k + 1], axis=0),
                        ).then_inc(p_sc[t % 2], 16)

            def gather(c):
                lo, hi = chunk_tiles(c)
                for i in range(2):
                    pool.wait_ge(e_st[i], 16 * (SS // 2) * (c + 1))
                for b in range(lo, hi):
                    r = b % 4
                    if b >= 4:
                        pool.wait_ge(l_red, b - 3)
                    for k in range(TOPK):
                        pool.indirect_dma_start(
                            out=GBUF[r][:, k * D:(k + 1) * D], out_offset=None, in_=ys[c],
                            in_offset=bass.IndirectOffsetOnAxis(ap=POS[:, b * TOPK + k:b * TOPK + k + 1], axis=0),
                        ).then_inc(l_g[r], 16)

            for c in range(CHUNKS):
                pool.wait_ge(ld_c, 48)
                attention(c)
                rows(c)
                scatter(c)
            for c in range(CHUNKS):
                gather(c)

        @block.scalar
        def _(act):
            S = Steps(astep, act)
            act.wait_ge(ld_c, 48)
            nc.scalar.activation(TG[:], VEC[:, V_GATES:V_GATES + 4], ACT.Tanh).then_inc(gates, 1)
            for i in range(4):
                act.wait_ge(wh_mm, i + 1)
                nc.scalar.activation(AW[:, 2048 + 512 * i:2560 + 512 * i], bank(1 + i), ACT.Copy).then_inc(wh_ok, 1)

            def attention(c):
                lo, hi = chunk_tiles(c)

                def qk_in(b):
                    act.wait_ge(a_t, b + 1)
                    nc.scalar.activation(QNT, PS[:, 0, 0:P], ACT.Identity,
                                         bias=VEC[:, V_LN1B:V_LN1B + 1], scale=VEC[:, V_LN1G:V_LN1G + 1])
                    nc.scalar.activation(KNT, PS[:, 0, P:P + NC_CTX], ACT.Identity,
                                         bias=VEC[:, V_LN1B:V_LN1B + 1],
                                         scale=VEC[:, V_LN1G:V_LN1G + 1]).then_inc(a_qk, 1)

                def q_sq(b):
                    act.wait_ge(a_q, b + 1)
                    nc.scalar.activation(SQQ, bank(1, 2), ACT.Square).then_inc(a_sq, 1)

                def k_sq(b):
                    act.wait_ge(a_k, b + 1)
                    nc.scalar.activation(SQK[0:NC_CTX, :], bank(3, 2, 0, NC_CTX), ACT.Square).then_inc(a_sq, 1)

                def roots(b):
                    act.wait_ge(a_n2, b + 1)
                    nc.scalar.activation(RN[:], N2[:], ACT.Sqrt).then_inc(a_rt, 1)

                def out2(ready, done, dst, b):
                    act.wait_ge(ready, b + 1)
                    nc.scalar.activation(dst, bank(5, 2), ACT.Copy).then_inc(done, 1)

                qk_in(lo)
                q_sq(lo)
                k_sq(lo)
                roots(lo)
                with act.Fori(lo, hi - 1) as b:
                    qk_in(b + 1)
                    out2(a_qt, a_qte, QT, b)
                    q_sq(b + 1)
                    out2(a_p, a_pe, PB, b)
                    k_sq(b + 1)
                    roots(b + 1)
                    out2(a_g, a_ge, GB, b)
                out2(a_qt, a_qte, QT, hi - 1)
                out2(a_p, a_pe, PB, hi - 1)
                out2(a_g, a_ge, GB, hi - 1)

            def mlp(c):
                lo, hi = c * GC, (c + 1) * GC

                def z_out(g):
                    act.wait_ge(m_t, g + 1)
                    nc.scalar.activation(XT, bank(0), ACT.Identity, bias=VEC[:, V_LN2B:V_LN2B + 1],
                                         scale=VEC[:, V_LN2G:V_LN2G + 1]).then_inc(m_te, 1)

                def gelu(g):
                    for n in range(4):
                        act.wait_ge(m_h, g * 4 + (n + 1))
                        nc.scalar.activation(HT[:, n, :], bank(1 + n), ACT.Gelu,
                                             bias=VEC[:, V_B1 + n:V_B1 + n + 1]).then_inc(m_he, 1)

                z_out(lo)
                gelu(lo)
                with act.Fori(lo, hi - 1) as g:
                    z_out(g + 1)
                    gelu(g + 1)

            def route(c):
                lo, hi = c * GC, (c + 1) * GC

                def z_out(g):
                    act.wait_ge(r_t, g + 1)
                    nc.scalar.activation(XT, bank(0), ACT.Copy).then_inc(r_te, 1)

                def silus(g):
                    for n in range(2):
                        act.wait_ge(r_gu, g * 2 + (n + 1))
                        nc.scalar.activation(SIL[:, n, :], bank(1 + 2 * n, 1, 0, EI), ACT.Silu).then_inc(r_si, 1)

                z_out(lo)
                silus(lo)
                with act.Fori(lo, hi - 1) as g:
                    z_out(g + 1)
                    silus(g + 1)
                act.wait_ge(r_le, (c + 1) * GC)
                nc.scalar.activation(RS, RS, ACT.Sigmoid).then_inc(t_s, 1)

            def experts(c):
                o = c * SS

                def x_out(i):
                    act.wait_ge(e_t, o + i + 1)
                    nc.scalar.activation(EXT, bank(0), ACT.Copy).then_inc(e_te, 1)

                def silu(i, u):
                    act.wait_ge(e_gu, o + i + 1)
                    act.wait_ge(e_h, o + i + 1)
                    nc.scalar.activation(ESI, gu_bank[u][:, :, 0:EI], ACT.Silu).then_inc(e_si, 1)

                def y_out(i, u, first=False):
                    act.wait_ge(e_y, o + i + 1)
                    if not first:
                        act.wait_ge(e_st[u], i * 8 + (16 * (o // 2) - 8 * u))
                    nc.scalar.activation(YB[u][:, :, :].rearrange("p t n -> p (t n)"), bank(6 + u),
                                         ACT.Copy).then_inc(e_ye, 1)

                x_out(0)
                silu(0, 0)
                x_out(1)
                silu(1, 1)
                x_out(2)

                def body(i, r, first=False):
                    silu(i + 1, (r + 1) % 2)
                    x_out(i + 2)
                    y_out(i - 1, (r - 1) % 2, first)

                body(1, 1, c == 0)
                body(2, 2, c == 0)
                with act.Fori(0, (SS - 8) // 4) as q:
                    for r in range(4):
                        body(q * 4 + (3 + r), 3 + r)
                i = 3 + (SS - 8)
                while i + 2 < SS:
                    body(i, i % 4)
                    i += 1
                silu(SS - 1, 1)
                y_out(SS - 3, 1)
                y_out(SS - 2, 0)
                y_out(SS - 1, 1)

            for c in range(CHUNKS):
                attention(c)
                mlp(c)
                route(c)
            for c in range(CHUNKS):
                experts(c)
            layer2_act(act)

        @block.vector
        def _(dve):
            v = nc.vector
            S = Steps(dstep, dve)
            v.memset(ZERO, 0.0)
            S.done(v.memset(N2[:], 1.0))
            S.done(v.memset(ONB[:], 1.0))
            S.done(v.memset(NT[:, 3, :], 1.0))
            dve.wait_ge(ld_c, 48)
            v.tensor_copy(UPB[:], CON[:, C_UP:C_UP + P]).then_inc(cbf, 1)
            dve.sem_inc(a_y, 1)
            dve.sem_inc(m_x, 1)
            dve.wait_ge(ld_x, 32)
            dve.wait_ge(gates, 1)

            def rsqrt(dst, src, tmp):
                S.step(v.tensor_scalar(tmp.bitcast(I32), src.bitcast(I32), 1, None, ALU.logical_shift_right))
                S.step(v.tensor_scalar(dst.bitcast(I32), tmp.bitcast(I32), -1, 0x5F3759DF, ALU.mult, ALU.add))
                for _ in range(3):
                    S.step(v.scalar_tensor_tensor(tmp, dst, -0.5, dst, ALU.mult, ALU.mult))
                    S.step(v.tensor_tensor(tmp, tmp, src, ALU.mult))
                    S.step(v.scalar_tensor_tensor(dst, tmp, 1.5, dst, ALU.add, ALU.mult))

            def mean_rstd(stats, mean, rstd, var, t1):
                f = lambda k: stats[:, :, k]
                S.step(v.tensor_tensor(mean, f(1), f(4), ALU.add))
                S.done(v.tensor_scalar(mean, mean, 0.5, None, ALU.mult))
                S.step(v.tensor_tensor(t1, f(1), f(4), ALU.subtract))
                S.done(v.tensor_tensor(var, f(2), f(5), ALU.add))
                S.step(v.scalar_tensor_tensor(t1, t1, 0.25, t1, ALU.mult, ALU.mult))
                S.step(v.scalar_tensor_tensor(var, var, 1.0 / D, t1, ALU.mult, ALU.add))
                S.step(v.tensor_scalar(var, var, EPS, None, ALU.add))
                rsqrt(rstd, var, t1)

            def second_norm(var, rstd, both, t1, t2):
                S.step(v.tensor_scalar(t2, var, -EPS, None, ALU.add))
                S.step(v.tensor_tensor(t2, t2, rstd, ALU.mult))
                S.step(v.tensor_tensor(t2, t2, rstd, ALU.mult))
                S.step(v.tensor_scalar(t2, t2, EPS, None, ALU.add))
                rsqrt(both, t2, t1)
                S.step(v.tensor_tensor(both, both, rstd, ALU.mult))

            def bn(src, dst, lo, n):
                with dve.Fori(0, n) as i:
                    v.bn_stats(dst[:, i, :], src[:, i + lo, :])
                S.done(v.memset(NT[:, 2, 0:1], 0.0))
                S.wait()

            mean, rstd, var, both, meanc, rstdc, t1, t2, varc = (ST[:, i, :] for i in range(9))

            def attention(c):
                lo, hi = chunk_tiles(c)
                bn(X, BS, lo, TC)
                with dve.Fori(0, TC) as i:
                    v.bn_stats(BSC[0:NC_CTX, i, :], CTX[:, i + lo, :])
                S.step(v.memset(NT[:, 2, 0:1], 0.0))
                mean_rstd(BS, mean, rstd, var, t1)
                second_norm(var, rstd, both, t1, t2)
                k = slice(0, NC_CTX)
                mean_rstd(BSC[k], meanc[k], rstdc[k], varc[k], t1[k])
                xc, yc = X[:, lo:hi, :], Y[:, lo:hi, :]
                sh = [P, TC, D]
                S.step(v.tensor_tensor(yc, xc, mean.unsqueeze(2).to_broadcast(sh), ALU.subtract))
                S.step(v.tensor_tensor(yc, yc, rstd.unsqueeze(2).to_broadcast(sh), ALU.mult))
                S.step(v.tensor_tensor(yc, yc, ROWS[:, R_BO:R_BO + D].unsqueeze(1).to_broadcast(sh), ALU.add))

                def z(b):
                    i = b - lo
                    v.tensor_scalar(ZT[:, 0:D], X[:, b, :], mean[:, one(i)], both[:, one(i)], ALU.subtract, ALU.mult)
                    v.tensor_scalar(ZC, CTX[:, b, :], meanc[k, one(i)], rstdc[k, one(i)],
                                    ALU.subtract, ALU.mult).then_inc(a_z, 1)

                def norms(b):
                    dve.wait_ge(a_sq, b * 2 + 1)
                    v.tensor_reduce(N2[:, 0:H], SQQ.rearrange("p (h d) -> p h d", h=H), AX_X, ALU.add)
                    dve.wait_ge(a_sq, b * 2 + 2)
                    v.tensor_reduce(N2[k, H:2 * H], SQK[k, :].rearrange("p (h d) -> p h d", h=H),
                                    AX_X, ALU.add).then_inc(a_n2, 1)
                    dve.wait_ge(a_rt, b + 1)
                    S.step(v.tensor_scalar(RN[:], RN[:], 1e-12, None, ALU.max))
                    S.step(v.reciprocal(RN[:], RN[:]))
                    v.tensor_tensor(QN.rearrange("p (h d) -> p h d", h=H),
                                    bank(1, 2).rearrange("p (h d) -> p h d", h=H),
                                    RN[:, 0:H].unsqueeze(2).to_broadcast([P, H, DH]), ALU.mult).then_inc(a_qn, 1)
                    v.tensor_tensor(KN[k, :].rearrange("p (h d) -> p h d", h=H),
                                    bank(3, 2, 0, NC_CTX).rearrange("p (h d) -> p h d", h=H),
                                    RN[k, H:2 * H].unsqueeze(2).to_broadcast([NC_CTX, H, DH]),
                                    ALU.mult).then_inc(a_kn, 1)

                def y(b):
                    dve.wait_ge(a_o, b + 1)
                    v.tensor_tensor(Y[:, b, :], bank(7)[:, 0:D], Y[:, b, :], ALU.add).then_inc(a_y, 1)

                def next_z(b):
                    dve.wait_ge(a_t, b)
                    dve.wait_ge(a_vn, b)
                    z(b)

                z(lo)
                norms(lo)
                next_z(lo + 1)

                def body(b):
                    norms(b + 1)
                    next_z(b + 2)
                    y(b)
                S.loop(lo, hi - 2, body, 2)
                norms(hi - 1)
                y(hi - 2)
                y(hi - 1)
                dve.wait_ge(a_y, hi + 1)

            def mlp(c):
                lo, hi = c * GC, (c + 1) * GC
                bn(Y, BS, c * TC, TC)
                mean_rstd(BS, mean, rstd, var, t1)

                def z(g):
                    for t in range(G):
                        i = (g - lo) * G + t
                        ins = v.tensor_scalar(ZT[:, t * D:(t + 1) * D], Y[:, g * G + t, :], mean[:, one(i)],
                                              rstd[:, one(i)], ALU.subtract, ALU.mult)
                    ins.then_inc(m_z, 1)

                def x(g):
                    dve.wait_ge(m_o, g + 1)
                    tiles = bass.ds(g * G, G)
                    tmp = TMP.rearrange("p (t d) -> p t d", t=G)
                    S.step(v.tensor_tensor(tmp, bank(5).rearrange("p (t d) -> p t d", t=G), Y[:, tiles, :], ALU.add))
                    S.step(v.tensor_tensor(tmp, tmp, ROWS[:, R_B2:R_B2 + D].unsqueeze(1).to_broadcast([P, G, D]),
                                           ALU.add))
                    v.scalar_tensor_tensor(X[:, tiles, :], tmp, TG[:, 0:1], X[:, tiles, :], ALU.mult,
                                           ALU.add).then_inc(m_x, 1)

                z(lo)
                dve.wait_ge(m_t, lo + 1)
                z(lo + 1)

                def body(g):
                    dve.wait_ge(m_t, g + 2)
                    z(g + 2)
                    x(g)
                S.loop(lo, hi - 2, body, 2)
                x(hi - 2)
                x(hi - 1)
                dve.wait_ge(m_x, hi + 1)

            def route(c):
                lo, hi = c * GC, (c + 1) * GC
                if c:
                    for i in range(2):
                        dve.wait_ge(p_sc[i], 16 * TOPK * (TC // 2) * c)
                else:
                    dve.wait_ge(zeroed, 16 * CHUNKS)
                bn(X, BS, c * TC, TC)
                mean_rstd(BS, mean, rstd, var, t1)

                def z(g):
                    for t in range(G):
                        i = (g - lo) * G + t
                        ins = v.tensor_scalar(ZT[:, t * D:(t + 1) * D], X[:, g * G + t, :], mean[:, one(i)],
                                              rstd[:, one(i)], ALU.subtract, ALU.mult)
                    ins.then_inc(r_z, 1)

                def rest(g):
                    dve.wait_ge(r_l, g + 1)
                    v.tensor_copy(RS.rearrange("p (g n) -> p g n", g=GC)[:, g - lo, :], bank(7)[:, 0:G * E],
                                  ).then_inc(r_le, 1)
                    for n in range(2):
                        dve.wait_ge(r_si, g * 2 + (n + 1))
                        v.tensor_tensor(SHH[:, n, :], SIL[:, n, :], bank(2 + 2 * n, 1, 0, EI), ALU.mult).then_inc(r_h, 1)
                    dve.wait_ge(r_o, g + 1)
                    v.scalar_tensor_tensor(X[:, bass.ds(g * G, G), :], bank(5).rearrange("p (t d) -> p t d", t=G),
                                           TG[:, 1:2], X[:, bass.ds(g * G, G), :], ALU.mult, ALU.add).then_inc(r_x, 1)

                z(lo)
                with dve.Fori(lo, hi - 1) as g:
                    dve.wait_ge(r_t, g + 1)
                    dve.wait_ge(r_zc, g + 1)
                    z(g + 1)
                    rest(g)
                rest(hi - 1)
                dve.wait_ge(r_zc, hi)
                tables(c)

            def tables(c):
                t3 = lambda x, n=TC: x.rearrange("p (t e) -> p t e", t=n)
                C = t3(RC)
                dve.wait_ge(t_s, c + 1)
                S.step(v.tensor_tensor(C, t3(RS), ROWS[:, R_GBIAS:R_GBIAS + E].unsqueeze(1).to_broadcast([P, TC, E]),
                                       ALU.add))
                c8 = RC.rearrange("p (n w) -> p n w", w=8)
                N = TC * NG
                hi0 = RA[:, 0:512].rearrange("p (n w) -> p n w", w=4)
                lo0 = RA[:, 512:1024].rearrange("p (n w) -> p n w", w=4)
                hi1 = RB[:, 0:256].rearrange("p (n w) -> p n w", w=2)
                lo1 = RB[:, 256:512].rearrange("p (n w) -> p n w", w=2)
                m1 = RB[:, 512:768].rearrange("p (n w) -> p n w", w=2)
                S.done(v.tensor_tensor(hi0, c8[:, :, 0:4], c8[:, :, 4:8], ALU.max))
                S.step(v.tensor_tensor(lo0, c8[:, :, 0:4], c8[:, :, 4:8], ALU.min))
                S.done(v.tensor_tensor(hi1, hi0[:, :, 0:2], hi0[:, :, 2:4], ALU.max))
                S.done(v.tensor_tensor(m1, hi0[:, :, 0:2], hi0[:, :, 2:4], ALU.min))
                S.step(v.tensor_tensor(lo1, lo0[:, :, 0:2], lo0[:, :, 2:4], ALU.max))
                S.step(v.tensor_tensor(lo1, lo1, m1, ALU.max))
                gs, gl, gm = RK[:, 0:N], RK[:, N:2 * N], RK[:, 2 * N:3 * N]
                S.done(v.tensor_tensor(gs, hi1[:, :, 0], hi1[:, :, 1], ALU.max))
                S.done(v.tensor_tensor(gm, hi1[:, :, 0], hi1[:, :, 1], ALU.min))
                S.step(v.tensor_tensor(gl, lo1[:, :, 0], lo1[:, :, 1], ALU.max))
                S.step(v.tensor_tensor(gl, gl, gm, ALU.max))
                S.step(v.tensor_tensor(gs, gs, gl, ALU.add))
                sh = [P, TC, NG, NG]
                g3 = gs.rearrange("p (t g) -> p t g", t=TC)
                mine, other = g3.unsqueeze(3).to_broadcast(sh), g3.unsqueeze(2).to_broadcast(sh)
                ra, rb = (x.rearrange("p (t g j) -> p t g j", t=TC, g=NG) for x in (RA, RB))
                S.done(v.tensor_tensor(ra, other, mine, ALU.is_gt))
                S.step(v.tensor_tensor(rb, other, mine, ALU.is_equal))
                low = CON[:, C_LOW:C_LOW + 64].unsqueeze(1).to_broadcast([P, TC, 64])
                S.step(v.tensor_tensor(t3(RB), t3(RB), low, ALU.mult))
                S.step(v.tensor_tensor(RA, RA, RB, ALU.add))
                S.step(v.tensor_reduce(gl, RA.rearrange("p (n j) -> p n j", j=NG), AX_X, ALU.add))
                S.step(v.tensor_scalar(gl, gl, TOPG - 0.5, None, ALU.is_lt))
                S.step(v.tensor_tensor(c8, c8, gl.unsqueeze(2).to_broadcast([P, N, 8]), ALU.mult))
                m8 = RK[:, 0:TC * 8].rearrange("p (t k) -> p t k", t=TC)
                A = t3(RA)
                for t in range(TC):
                    ins = v.max(m8[:, t, :], C[:, t, :])
                S.step(ins)
                for t in range(TC):
                    ins = v.match_replace(A[:, t, :], m8[:, t, :], C[:, t, :], GONE)
                S.step(ins)
                S.step(v.tensor_scalar(RB, RA, GONE, None, ALU.is_equal))
                v.tensor_copy(SELB[:, :, :], t3(RB)).then_inc(t_sel, 1)
                S.done(v.memset(CSB[:, 0, :], 0.0))
                sel3 = t3(RB)
                for t in range(1, TC):
                    S.wait()
                    S.done(v.tensor_tensor(CSB[:, t, :], CSB[:, t - 1, :], sel3[:, t - 1, :], ALU.add))
                S.wait()
                v.memset(NT[:, 2, 0:1], 0.0).then_inc(t_sel, 1)
                S.step(v.tensor_tensor(RS, RS, RB, ALU.mult))
                sm = RK[:, 512:512 + TC]
                S.step(v.tensor_reduce(sm, t3(RS), AX_X, ALU.add))
                S.step(v.tensor_scalar(sm, sm, 1e-20, None, ALU.add))
                S.step(v.reciprocal(sm, sm))
                S.step(v.tensor_scalar(sm, sm, 2.5, None, ALU.mult))
                S.done(v.tensor_tensor(XR[:, :, D:ROW], t3(RS), sm.unsqueeze(2).to_broadcast([P, TC, E]), ALU.mult))
                dve.wait_ge(t_rank, c + 1)
                nt, end, base = NT[:, 0, :], NT[:, 1, :], NT[:, 2, :]
                S.step(v.tensor_copy(end, bank(7)[:, 0:E]))
                sh = [P, E, TC]
                big = RC.rearrange("p (e j) -> p e j", e=E)
                S.step(v.tensor_tensor(big, end.unsqueeze(2).to_broadcast(sh),
                                       CON[:, C_STEP:C_STEP + TC].unsqueeze(1).to_broadcast(sh), ALU.is_gt))
                S.step(v.tensor_reduce(nt, big, AX_X, ALU.add))
                S.step(v.tensor_tensor_scan(end, NT[:, 3, :], nt, 0.0, ALU.mult, ALU.add))
                S.step(v.tensor_tensor(base, end, nt, ALU.subtract))
                S.step(v.tensor_scalar(base, base, float(P), None, ALU.mult))
                n = SLOTS // 2
                for j in range(2):
                    w = RC[0:n, 64 * j:64 * j + 64]
                    S.done(v.tensor_scalar(w, end[0:n], CON[0:n, C_SLOT + j:C_SLOT + j + 1], None, ALU.is_le))
                S.wait()
                S.step(v.tensor_reduce(NT[0:n, 0, 0:2], RC[0:n, 0:128].rearrange("p (j e) -> p j e", j=2), AX_X, ALU.add))
                v.tensor_scalar(TE[0:n, c, :], NT[0:n, 0, 0:2], E - 1.0, None, ALU.min).then_inc(t_te, 1)
                S.step(v.tensor_tensor(t3(RA), bank(5, 2).rearrange("p (t e) -> p t e", t=TC),
                                       base.unsqueeze(1).to_broadcast([P, TC, E]), ALU.add))
                S.step(v.tensor_scalar(RA, RA, -1.0, BIG, ALU.mult, ALU.add))
                S.step(v.tensor_tensor(RA, RA, RB, ALU.mult))
                for t in range(TC):
                    ins = v.max(m8[:, t, :], t3(RA)[:, t, :])
                S.step(ins)
                v.tensor_scalar(POS[:, c * TC * TOPK:(c + 1) * TC * TOPK], RK[:, 0:TC * 8], -1.0, BIG,
                                ALU.mult, ALU.add).then_inc(t_rw, 1)

            def experts(c):
                o = c * SS

                def h(i, r):
                    e = [dve.value_load(TER[0:1, one(i * G + (c * SLOTS + t))], min_val=0, max_val=E - 1)
                         for t in range(G)]
                    dve.wait_ge(e_si, o + i + 1)
                    dve.wait_ge(e_ht, o + i + 1)
                    for t in range(G):
                        ins = v.scalar_tensor_tensor(EH[:, t, :], ESI[:, t, :], XB[r][:, t, one(e[t] + D)],
                                                     gu_bank[r % 2][:, t, EI:2 * EI], ALU.mult, ALU.mult)
                    ins.then_inc(e_h, 1)

                def hT_out(i, r):
                    dve.wait_ge(e_ht, o + i + 2)
                    v.tensor_copy(EHT[r % 2], bank(5, 1, 0, EI)).then_inc(e_hte, 1)

                h(0, 0)

                def body(i, r):
                    hT_out(i, r)
                    h(i + 1, (r + 1) % 4)
                with dve.Fori(0, SS // 4 - 1) as q:
                    for r in range(4):
                        body(q * 4 + r, r)
                for i in range(SS - 4, SS - 1):
                    body(i, i % 4)
                hT_out(SS - 1, 3)

            for c in range(CHUNKS):
                attention(c)
                mlp(c)
                route(c)
            dve.sem_inc(e_h, 1)
            dve.wait_ge(t_ter, 16 * CHUNKS)
            for c in range(CHUNKS):
                experts(c)
            layer2_dve(dve, S, rsqrt, mean_rstd, second_norm)

        @block.tensor
        def _(pe):
            mm = nc.tensor.matmul
            pe.wait_ge(ld_c, 48)
            pe.wait_ge(ld_w, 64)
            for i in range(4):
                for j in range(4):
                    h = 4 * i + j
                    ins = mm(PS[:, 1 + i, j * D:(j + 1) * D], WVT[:, h, :], WO[:, h, :], start=True, stop=True)
                ins.then_inc(wh_mm, 1)
            pe.wait_ge(wh_ok, 4)

            def attention(c):
                lo, hi = chunk_tiles(c)

                def T(b):
                    pe.wait_ge(a_z, b + 1)
                    nc.tensor.transpose(PS[:, 0, 0:P], ZT[:, 0:D], ID)
                    nc.tensor.transpose(PS[:, 0, P:P + NC_CTX], ZC, ID[0:NC_CTX, 0:NC_CTX]).then_inc(a_t, 1)

                def q(b):
                    pe.wait_ge(a_qk, b + 1)
                    for j in range(2):
                        ins = mm(PS[:, 1 + j, :], QNT, WQ[:, 512 * j:512 * (j + 1)], start=True, stop=True)
                    ins.then_inc(a_q, 1)

                def k(b):
                    for j in range(2):
                        ins = mm(PS[0:NC_CTX, 3 + j, :], KNT, WK[:, 512 * j:512 * (j + 1)], start=True, stop=True)
                    ins.then_inc(a_k, 1)

                def qT(b):
                    pe.wait_ge(a_qn, b + 1)
                    for j in range(8):
                        ins = nc.tensor.transpose(bank(5, 2)[:, j * P:(j + 1) * P], QN[:, j * P:(j + 1) * P], ID)
                    ins.then_inc(a_qt, 1)

                def p(b):
                    pe.wait_ge(a_qte, b + 1)
                    pe.wait_ge(a_kn, b + 1)
                    pe.wait_ge(a_vn, b + 1)
                    for j in range(2):
                        ins = mm(PS[:, 5 + j, :], VN, KN[0:NC_CTX, 512 * j:512 * (j + 1)], start=True, stop=True)
                    ins.then_inc(a_p, 1)

                def g(b):
                    pe.wait_ge(a_pe, b + 1)
                    for h in range(H):
                        r = DH * (h % 2)
                        ins = mm(PS[r:r + DH, 5 + h // 8, (h // 2 % 4) * D:(h // 2 % 4 + 1) * D],
                                 PB[:, h * DH:(h + 1) * DH], WH[:, h, :], start=True, stop=True)
                    ins.then_inc(a_g, 1)

                def o(b):
                    pe.wait_ge(a_ge, b + 1)
                    pe.wait_ge(a_y, b + 1)
                    for j in range(8):
                        ins = mm(PS[:, 7, 0:D], QT[:, j * P:(j + 1) * P], GB[:, j * D:(j + 1) * D],
                                 start=(j == 0), stop=(j == 7))
                    ins.then_inc(a_o, 1)

                T(lo)
                q(lo)
                k(lo)
                with pe.Fori(lo, hi - 1) as b:
                    T(b + 1)
                    qT(b)
                    q(b + 1)
                    p(b)
                    k(b + 1)
                    g(b)
                    o(b)
                qT(hi - 1)
                p(hi - 1)
                g(hi - 1)
                o(hi - 1)

            def transposes(ready, done, g):
                pe.wait_ge(ready, g + 1)
                for t in range(G):
                    ins = nc.tensor.transpose(PS[:, 0, t * P:(t + 1) * P], ZT[:, t * D:(t + 1) * D], ID)
                ins.then_inc(done, 1)

            def mlp(c):
                lo, hi = c * GC, (c + 1) * GC

                def up(g):
                    pe.wait_ge(m_te, g + 1)
                    for n in range(4):
                        mm(bank(1 + n), W1[:, n * P:(n + 1) * P], XT, start=True, stop=True).then_inc(m_h, 1)

                def down(g):
                    pe.wait_ge(m_x, g + 1)
                    pe.wait_ge(m_he, g * 4 + 4)
                    for t in range(G):
                        for n in range(4):
                            ins = mm(PS[:, 5, t * D:(t + 1) * D], HT[:, n, t * P:(t + 1) * P],
                                     W2[:, n * D:(n + 1) * D], start=(n == 0), stop=(n == 3))
                    ins.then_inc(m_o, 1)

                transposes(m_z, m_t, lo)
                up(lo)
                with pe.Fori(lo, hi - 1) as g:
                    transposes(m_z, m_t, g + 1)
                    down(g)
                    up(g + 1)
                down(hi - 1)

            def route(c):
                lo, hi = c * GC, (c + 1) * GC

                def rest(g):
                    pe.wait_ge(r_te, g + 1)
                    for n in range(4):
                        ins = mm(bank(1 + n, 1, 0, EI), SGW[:, n, :], XT, start=True, stop=True)
                        if n % 2:
                            ins.then_inc(r_gu, 1)
                    for t in range(G):
                        ins = mm(PS[:, 7, t * E:(t + 1) * E], XT[:, t * P:(t + 1) * P], GWT[:], start=True, stop=True)
                    ins.then_inc(r_l, 1)

                def down(g):
                    pe.wait_ge(r_h, g * 2 + 2)
                    for t in range(G):
                        for n in range(2):
                            ins = mm(PS[:, 5, t * D:(t + 1) * D], SHH[:, n, t * P:(t + 1) * P], SDW[:, n, :],
                                     start=(n == 0), stop=(n == 1))
                    ins.then_inc(r_o, 1)

                transposes(r_z, r_t, lo)
                rest(lo)
                with pe.Fori(lo, hi - 1) as g:
                    transposes(r_z, r_t, g + 1)
                    down(g)
                    rest(g + 1)
                down(hi - 1)
                pe.wait_ge(t_sel, 2 * c + 2)
                flat = lambda x: x[:, :, :].rearrange("p t e -> p (t e)")
                for j in range(2):
                    mm(PS[:, 5 + j, :], UPB[:], flat(SELB)[:, 512 * j:512 * (j + 1)], start=True, stop=False)
                    mm(PS[:, 5 + j, :], ONB[:], flat(CSB)[:, 512 * j:512 * (j + 1)], start=False, stop=True)
                mm(PS[:, 7, 0:E], ONB[:], SELB[:, TC - 1, :], start=True, stop=False)
                mm(PS[:, 7, 0:E], ONB[:], CSB[:, TC - 1, :], start=False, stop=True).then_inc(t_rank, 1)

            def experts(c):
                o = c * SS

                def T(i, r):
                    pe.wait_ge(e_ld[r], i * 4 + (4 * o + 16 - 4 * r))
                    for t in range(G):
                        ins = nc.tensor.transpose(PS[:, 0, t * P:(t + 1) * P], XB[r][:, t, 0:D], ID)
                    ins.then_inc(e_t, 1)

                def slot_expert(i, t):
                    return pe.value_load(TER[0:1, one(i * G + (c * SLOTS + t))], min_val=0, max_val=E - 1)

                def gu(i, r):
                    e = [slot_expert(i, t) for t in range(G)]
                    pe.wait_ge(e_te, o + i + 1)
                    for t in range(G):
                        ins = mm(gu_bank[r % 2][:, t, 0:2 * EI], EXT[:, t * P:(t + 1) * P], WGU[:, e[t], :],
                                 start=True, stop=True)
                    ins.then_inc(e_gu, 1)

                def hT(i):
                    pe.wait_ge(e_h, o + i + 2)
                    for t in range(G):
                        ins = nc.tensor.transpose(PS[0:EI, 5, t * P:(t + 1) * P], EH[:, t, :], ID)
                    ins.then_inc(e_ht, 1)

                def down(i, u):
                    e = [slot_expert(i, t) for t in range(G)]
                    pe.wait_ge(e_hte, o + i + 1)
                    if not isinstance(i, int) or i + o >= 2:
                        pe.wait_ge(e_ye, o + i - 1)
                    for t in range(G):
                        ins = mm(PS[:, 6 + u, t * D:(t + 1) * D], EHT[u][:, t * P:(t + 1) * P], WD[:, e[t], :],
                                 start=True, stop=True)
                    ins.then_inc(e_y, 1)

                T(0, 0)
                gu(0, 0)
                T(1, 1)
                gu(1, 1)
                hT(0)
                T(2, 2)

                def body(i, r):
                    gu(i + 1, (r + 1) % 4)
                    hT(i)
                    down(i - 1, (r - 1) % 2)
                    T(i + 2, (r + 2) % 4)
                body(1, 1)
                body(2, 2)
                with pe.Fori(0, (SS - 8) // 4) as q:
                    for r in range(4):
                        body(q * 4 + (3 + r), (3 + r) % 4)
                i = 3 + (SS - 8)
                while i + 2 < SS:
                    body(i, i % 4)
                    i += 1
                gu(SS - 1, 3)
                hT(SS - 2)
                down(SS - 3, 1)
                hT(SS - 1)
                down(SS - 2, 0)
                down(SS - 1, 1)

            for c in range(CHUNKS):
                if c == 0:
                    pass
                attention(c)
                if c == 0:
                    pe.wait_ge(ld_m, 32)
                mlp(c)
                if c == 0:
                    pe.wait_ge(ld_r, 48)
                route(c)
            pe.wait_ge(t_ter, 16 * CHUNKS)
            pe.wait_ge(ld_wgu, 16)
            pe.wait_ge(ld_wd, 16)
            pe.sem_inc(e_ht, 1)
            for c in range(CHUNKS):
                experts(c)
            layer2_pe(pe)


_OUT = "out"


def kernel(**inputs):
    import concourse.bacc as bacc
    from concourse.bass_utils import run_bass_kernel_spmd as run

    i = {k: np.asarray(v) for k, v in inputs.items()}
    t = np.ascontiguousarray
    rows = lambda *names: [np.broadcast_to(v.reshape(1, -1), (P, v.size)) for v in names]
    col = lambda v, n=P: v.reshape(n, -1)

    def padded(v):
        out = np.zeros((P, 1), np.float32)
        out[:v.size, 0] = v
        return out
    gates = np.stack([i["g_xattn"][0], i["g_ffn"][0], i["g_xattn"][1], i["g_ffn"][1]])
    con = np.zeros((P, C_HOT), np.float32)
    con[:, C_ID:C_ID + P] = np.eye(P)
    con[:, C_UP:C_UP + P] = np.triu(np.ones((P, P)), 1)
    con[:, C_LOW:C_LOW + 64] = np.tril(np.ones((NG, NG)), -1).reshape(-1)
    con[:, C_STEP:C_STEP + TC] = P * np.arange(TC)
    con[:, C_SLOT] = 2 * np.arange(P)
    con[:, C_SLOT + 1] = 2 * np.arange(P) + 1
    hot = np.zeros((48, E1, P), np.float32)
    for e in range(E1):
        hot[e::E1, e, :] = 1.0
    arrays = {
        "x": t(i["x"].transpose(1, 0, 2)),
        "ctx": t(i["ctx_1024"].transpose(1, 0, 2)),
        "wq": t(i["L0_xattn_wq"]),
        "wk": t(i["L0_xattn_wk"]),
        "wvT": t(i["L0_xattn_wv"].reshape(D, H, DH).transpose(2, 1, 0)),
        "wo": t(i["L0_xattn_wo"].reshape(H, DH, D).transpose(1, 0, 2)),
        "w1": t(i["L0_xattn_w1"]),
        "w2": t(i["L0_xattn_w2"].reshape(4, P, D).transpose(1, 0, 2).reshape(P, MLP)),
        "gwT": t(i["L0_ffn_gate_w"].T),
        "wgu": t(np.concatenate([i["L0_ffn_Wg"], i["L0_ffn_Wu"]], 1).transpose(2, 0, 1)),
        "wd": t(i["L0_ffn_Wd"].transpose(2, 0, 1)),
        "sgu": t(np.stack([i["L0_ffn_Sg"][:EI], i["L0_ffn_Su"][:EI], i["L0_ffn_Sg"][EI:], i["L0_ffn_Su"][EI:]])
                 .transpose(2, 0, 1)),
        "sd": t(i["L0_ffn_Sd"].reshape(D, 2, EI).transpose(2, 1, 0)),
        "wqT1": t(i["L1_xattn_Wq"].T),
        "wkT1": t(i["L1_xattn_Wk"].T),
        "wvT1": t(i["L1_xattn_Wv"].T),
        "gw1": t(i["L1_ffn_gate_w"].T),
        "w1e": t(i["L1_ffn_mlp1_w"][:, ::2].transpose(2, 0, 1)),
        "w2e": t(i["L1_ffn_mlp2_w"].transpose(2, 0, 1)),
        "b2s": t(np.concatenate([i["L1_ffn_mlp2_b"]] * 3)),
        "vec": t(np.concatenate([
            col(i["L0_xattn_ln1_g"]), col(i["L0_xattn_ln1_b"]), col(i["L0_xattn_ln2_g"]), col(i["L0_xattn_ln2_b"]),
            i["L0_xattn_b1"].reshape(4, P).T, col(i["L1_ffn_scale"]), i["L1_ffn_mlp1_b"][:, ::2].T,
            padded(i["L1_xattn_bq"]), padded(i["L1_xattn_bk"]), *rows(gates)], 1)),
        "rows": t(np.concatenate(rows(
            i["L0_xattn_ln1_g"], i["L0_xattn_ln1_b"], i["L0_xattn_bo"], i["L0_xattn_b2"], i["L1_xattn_bv"],
            i["L0_ffn_gate_bias"], i["L1_ffn_gate_b"]), 1)),
        "con": con,
        "hot": hot.reshape(48, E1 * P),
    }
    nc = bacc.Bacc("TRN2", target_bir_lowering=False, num_devices=1)
    a = {k: nc.dram_tensor("in_" + k, v.shape, mybir.dt.from_np(v.dtype), kind="ExternalInput").ap()
         for k, v in arrays.items()}
    a[_OUT] = nc.dram_tensor(_OUT, (P, B, D), F32, kind="ExternalOutput").ap()
    build(nc, a)
    r = run(nc, [{"in_" + k: v for k, v in arrays.items()}], core_ids=[0])
    return t(r.results[0][_OUT].transpose(1, 0, 2))
```

```python
import math
from contextlib import ExitStack

import numpy as np

import concourse.bass as bass
from concourse import mybir

F32 = mybir.dt.float32
BF16 = mybir.dt.bfloat16
I32 = mybir.dt.int32
U32 = mybir.dt.uint32
ALU = mybir.AluOpType
ACT = mybir.ActivationFunctionType
AX_X = mybir.AxisListType.X

P = 128
D = 128
B = 32
NC_CTX = 77
H, DH = 16, 64
INNER = H * DH
MLP = 512
E, NG, EI = 64, 8, 88
TOPK, TOPG = 8, 4
E1, K1 = 16, 4
QK = 32
EPS = 1e-5
CHUNKS = 2
TC = B // CHUNKS
G = 4
GC = TC // G
SLOTS = TC * P * TOPK // P + E
SS = SLOTS // G
ROW = D + E
BIG = 65536.0
GONE = -1e30
LIMIT, ALPHA = 7.0, 1.702

V_LN1G, V_LN1B, V_LN2G, V_LN2B, V_B1, V_SCALE, V_BM1 = 0, 1, 2, 3, 4, 8, 9
V_BQ, V_BK, V_GATES, V_END = 25, 26, 27, 31
R_LN1G, R_LN1B, R_BO, R_B2, R_BV, R_GBIAS, R_GB1, R_END = 0, 128, 256, 384, 512, 640, 704, 720
C_ID, C_UP, C_LOW, C_STEP, C_SLOT, C_HOT, C_END = 0, 128, 256, 320, 336, 338, 338 + E1 * P


class Steps:

    def __init__(self, sem, eng):
        self.sem, self.eng, self.base, self.k = sem, eng, 0, 0

    def done(self, ins):
        ins.then_inc(self.sem, 1)
        self.k += 1

    def wait(self):
        self.eng.wait_ge(self.sem, self.base + self.k)

    def step(self, ins):
        self.done(ins)
        self.wait()

    def loop(self, lo, hi, body, per):
        start = self.base + self.k
        with self.eng.Fori(lo, hi) as i:
            self.base, self.k = (i - lo) * per + start, 0
            body(i)
            assert self.k == per, self.k
        self.base, self.k = start + (hi - lo) * per, 0


def build(nc, a):
    one = lambda i: bass.ds(i, 1)
    ctx = ExitStack()
    with ctx:
        def sb(name, shape, dt=F32):
            return ctx.enter_context(nc.sbuf_tensor("sb_" + name, shape, dt))

        def sem(name):
            return ctx.enter_context(nc.semaphore(name))

        X = sb("X", [P, B, D])
        Yf = sb("Y", [P, B * D])
        Y = Yf[:, :].rearrange("p (b d) -> p b d", b=B)
        XR = sb("XR", [P, TC, ROW])
        WGU = sb("WGU", [P, E, 2 * EI])
        RW_ = sb("RW", [P, E * D])
        WD = RW_[0:EI, :].rearrange("p (e d) -> p e d", e=E)
        CTX = RW_[0:NC_CTX, 0:B * D].rearrange("p (b d) -> p b d", b=B)
        WVT = RW_[0:DH, B * D:B * D + H * D].rearrange("p (h d) -> p h d", h=H)
        WO = RW_[0:DH, B * D + H * D:B * D + 2 * H * D].rearrange("p (h d) -> p h d", h=H)
        AW = sb("AW", [P, 4096])
        WQ, WK = AW[:, 0:1024], AW[:, 1024:2048]
        WH = AW[:, 2048:4096].rearrange("p (h d) -> p h d", h=H)
        A1 = sb("A1", [P, 7 * 1024])
        RT5 = sb("RT5", [P, 5 * 1024])
        W1 = sb("W1", [P, MLP])
        W2 = sb("W2", [P, MLP])
        VEC = sb("VEC", [P, V_END])
        ROWS = sb("ROWS", [P, R_END])
        CON = sb("CON", [P, C_HOT])
        TG = sb("TG", [P, 4])
        GWT = sb("GWT", [P, E])
        SGW = sb("SGW", [P, 4, EI])
        SDW = sb("SDW", [EI, 2, D])
        UPB = sb("UPB", [P, P], BF16)
        ONB = sb("ONB", [P, P], BF16)
        SELB = sb("SELB", [P, TC, E], BF16)
        CSB = sb("CSB", [P, TC, E], BF16)
        POS = sb("POS", [P, B * TOPK], U32)
        TE = sb("TE", [P, CHUNKS, 2], I32)
        TER = sb("TER", [1, CHUNKS * SLOTS], I32)
        ZT = sb("ZT", [P, G * D])
        BS = sb("BS", [P, TC, 6])
        BSC = sb("BSC", [P, TC, 6])
        ST = sb("ST", [P, 6, TC])
        BSX = sb("BSX", [P, TC, 6])
        STX = sb("STX", [P, 3, TC])
        STC = sb("STC", [NC_CTX, 3, TC])
        N2 = sb("N2", [P, 2 * H])
        RN = sb("RN", [P, 2 * H])
        NT = sb("NT", [P, 4, E])
        PS = ctx.enter_context(nc.psum_tensor("PS", [P, 8, 512], F32))

        ID = CON[:, C_ID:C_ID + P]
        SQQ, SQK, QN, KN, QT, PB, GB = (A1[:, 1024 * i:1024 * (i + 1)] for i in range(7))
        ZC, VN = RT5[0:NC_CTX, 1024:1024 + D], RT5[0:NC_CTX, 1152:1152 + D]
        QNT, KNT = RT5[:, 1280:1280 + D], RT5[:, 1408:1408 + NC_CTX]
        ZERO = RT5[:, 0:ROW]
        HT = A1[:, 0:2048].rearrange("p (c n) -> p c n", c=4)
        XT = A1[:, 2048:2560]
        TMP = A1[:, 2560:3072]
        SIL = A1[0:EI, 3072:4096].rearrange("p (c n) -> p c n", c=2)
        SHH = A1[0:EI, 4096:5120].rearrange("p (c n) -> p c n", c=2)
        RS, RC, RA, RB, RK = (RT5[:, 1024 * i:1024 * (i + 1)] for i in range(5))
        XB = [A1[:, 768 * i:768 * (i + 1)].rearrange("p (t n) -> p t n", t=G) for i in range(4)]
        EXT = A1[:, 3072:3584]
        ESI = A1[:, 3584:3584 + G * EI].rearrange("p (t n) -> p t n", t=G)
        EH = A1[:, 4096:4096 + G * EI].rearrange("p (t n) -> p t n", t=G)
        EHT = [A1[0:EI, 4608 + 512 * i:5120 + 512 * i] for i in range(2)]
        YB = [A1[:, 5632 + 512 * i:6144 + 512 * i].rearrange("p (t n) -> p t n", t=G) for i in range(2)]
        W1E = RT5[:, 0:2048].rearrange("p (e n) -> p e n", e=E1)
        W2E = RT5[:, 2048:4096].rearrange("p (e n) -> p e n", e=E1)
        LW = RT5[:, 4096:5120]
        WQT, WKT, WVT1, GW1 = LW[:, 0:32], LW[:, 32:64], LW[:, 64:192], LW[:, 192:208]
        B2S = LW[0:48, 208:336]
        HOT = XR[:, :, :].rearrange("p t n -> p (t n)")[:, 0:E1 * P // 2].bitcast(BF16)
        HOTF = AW[:, 0:2048]
        GBUF = [Yf[:, 1024 * i:1024 * (i + 1)] for i in range(4)]
        CG = AW[0:NC_CTX, 0:512].rearrange("p (t n) -> p t n", t=G)
        CT = AW[:, 512:512 + G * NC_CTX]
        KP = AW[0:QK, 1024:1024 + G * NC_CTX]
        VP = AW[0:NC_CTX, 1536:2048].rearrange("p (t n) -> p t n", t=G)
        QP = AW[0:QK, 2048:2560]
        ZS = AW[0:NC_CTX, 2560:3072]
        HM = [A1[:, 512 * i:512 * (i + 1)] for i in range(2)]
        SG = [A1[:, 1024 + 512 * i:1536 + 512 * i] for i in range(2)]
        XTL = A1[:, 2048:2560]
        SX = [A1[:, 3072 + 512 * i:3584 + 512 * i] for i in range(2)]
        AT = A1[:, 4096:4608]
        RED = A1[:, 6656:6656 + D]
        LB = WGU[:, :, :].rearrange("p e n -> p (e n)")
        TT, ZB = LB[:, 0:2048], LB[:, 2048:4096]
        RTF = LB[0:48, 4096:6144]
        RTB = LB[:, 6144:7168].bitcast(BF16)
        GL, GO = (LB[:, 7168 + 320 * i:7488 + 320 * i].rearrange("p (t e) -> p t e", t=TC) for i in range(2))
        GM8 = LB[:, 7808:7936].rearrange("p (t e) -> p t e", t=TC)
        GD, GSA, GSB, GSEL = (LB[:, 7936 + 256 * i:8192 + 256 * i] for i in range(4))
        R48 = LB[:, 8960:9728].rearrange("p (t j e) -> p t j e", t=TC, j=3)
        HIB = LB[:, 9728:9856].bitcast(BF16).rearrange("p (t e) -> p t e", t=TC)
        GSUM = LB[:, 9856:9856 + TC]

        xs = [nc.dram_tensor(f"sorted_rows{c}", [SLOTS * P, ROW], F32).ap() for c in range(CHUNKS)]
        ys = [nc.dram_tensor(f"sorted_out{c}", [SLOTS * P, D], F32).ap() for c in range(CHUNKS)]
        te_d = nc.dram_tensor("slot_experts", [CHUNKS, SLOTS], I32).ap()

        ld_c, ld_x, ld_w, ld_m, ld_r, ld_wgu, ld_wd, ld_l, ld_hot = (sem(n) for n in (
            "ld_const", "ld_tokens", "ld_attn", "ld_mlp", "ld_route", "ld_wgu", "ld_wd", "ld_layer2", "ld_hot"))
        zeroed = sem("zeroed")
        dstep, astep = sem("dve_step"), sem("act_step")
        gates, wh_mm, wh_ok = sem("gates"), sem("wh_mm"), sem("wh_ok")
        cbf = sem("const_bf16")
        a_z, a_vn, a_t, a_qk, a_q, a_k, a_sq, a_n2, a_rt, a_qn, a_kn = (sem("attn_" + n) for n in (
            "z", "vn", "zT", "zT_out", "q", "k", "squares", "sums", "roots", "qn", "kn"))
        a_qt, a_qte, a_p, a_pe, a_g, a_ge, a_o, a_y = (sem("attn_" + n) for n in (
            "qT", "qT_out", "p", "p_out", "g", "g_out", "o", "y"))
        m_z, m_t, m_te, m_h, m_he, m_o, m_x = (sem("mlp_" + n) for n in (
            "z", "zT", "zT_out", "h", "gelu", "o", "x"))
        r_z, r_zc, r_t, r_te, r_l, r_le, r_gu, r_si, r_h, r_o, r_x = (sem("rt_" + n) for n in (
            "z", "z_row", "zT", "zT_out", "logit", "logit_out", "gu", "silu", "h", "o", "x"))
        t_s, t_sel, t_rank, t_pos, t_te, t_ted, t_ter, t_rw = (sem("tab_" + n) for n in (
            "sigmoid", "chosen", "ranks", "pos", "slots", "slots_dram", "slots_row", "rows"))
        p_cp, p_sc = sem("pool_copy"), [sem(f"scatter{i}") for i in range(2)]
        e_ld = [sem(f"ex_load{i}") for i in range(4)]
        e_t, e_te, e_gu, e_si, e_h, e_ht, e_hte, e_y, e_ye = (sem("ex_" + n) for n in (
            "xT", "xT_out", "gu", "silu", "h", "hT", "hT_out", "y", "y_out"))
        e_st = [sem(f"ex_store{i}") for i in range(2)]
        l_g = [sem(f"l2_gather{i}") for i in range(4)]
        l_red, l_cg, l_fin, l_out = sem("l2_reduced"), sem("l2_ctx"), sem("l2_final"), sem("l2_stored")
        l_dve = sem("l2_hot")
        l_h, l_hm, l_sg, l_sx, l_bc, l_y = (sem("l2_" + n) for n in ("h", "hmin", "glu", "weighted", "bcast", "y"))
        n_z, n_t, n_te, n_q, n_qe, n_ct, n_cte, n_kv, n_kpe, n_vpe, n_s, n_se, n_sh, n_o = (sem("l2f_" + n) for n in (
            "z", "zT", "zT_out", "q", "q_out", "ctxT", "ctxT_out", "kv", "k_out", "v_out", "scores", "tanh",
            "sigmoid", "o"))
        n_x, n_z2, n_t2, n_t2e, n_g, n_d, n_de, n_r, n_rt, n_rte, n_acce, n_f = (sem("l2r_" + n) for n in (
            "x", "z", "zT", "zT_out", "gate", "diff", "silu", "weights", "wT", "wT_out", "sum_out", "sumT"))

        block = ctx.enter_context(nc.Block())

        def bank(n, k=1, p0=0, p1=P):
            return PS[p0:p1, n:n + k, :].rearrange("p a n -> p (a n)")

        gu_bank = [PS[:, 1 + 2 * u:3 + 2 * u, :].rearrange("p a (c n) -> p (a c) n", c=2) for u in range(2)]

        def chunk_tiles(c):
            return c * TC, (c + 1) * TC

        def slot_experts(eng, c, i):
            return nc.values_load_multi_w_load_instructions(
                TER[0:1, bass.ds(i * G + c * SLOTS, G)], engines=[eng.engine], min_val=0, max_val=E - 1,
                skip_runtime_bounds_check_because="the table holds the lesser of a count and E - 1")[1]

        NGR = B // G

        def t3(x, n=G):
            return x.rearrange("p (t e) -> p t e", t=n)

        def layer2_act(act):
            def attention(c):
                lo, hi = c * GC, (c + 1) * GC

                def projections(g):
                    act.wait_ge(n_t, g + 1)
                    nc.scalar.activation(XTL, bank(0), ACT.Copy).then_inc(n_te, 1)
                    act.wait_ge(n_ct, g + 1)
                    nc.scalar.activation(CT, bank(1)[:, 0:G * NC_CTX], ACT.Copy).then_inc(n_cte, 1)
                    act.wait_ge(n_q, g + 1)
                    nc.scalar.activation(QP, bank(2, 1, 0, QK), ACT.Identity,
                                         bias=VEC[0:QK, V_BQ:V_BQ + 1]).then_inc(n_qe, 1)
                    act.wait_ge(n_kv, g + 1)
                    nc.scalar.activation(KP, bank(3, 1, 0, QK)[:, 0:G * NC_CTX], ACT.Identity,
                                         bias=VEC[0:QK, V_BK:V_BK + 1]).then_inc(n_kpe, 1)

                def scores(g):
                    act.wait_ge(n_s, g + 1)
                    nc.scalar.activation(ZS, bank(5, 1, 0, NC_CTX), ACT.Tanh,
                                         scale=0.5 / math.sqrt(QK)).then_inc(n_se, 1)

                projections(lo)
                with act.Fori(lo, hi - 1) as g:
                    scores(g)
                    projections(g + 1)
                scores(hi - 1)

            def route(c):
                for i in range(GC):
                    act.wait_ge(n_t2, c * GC + i + 1)
                    nc.scalar.activation(TT[:, i * 512:(i + 1) * 512], bank(i), ACT.Identity,
                                         scale=VEC[:, V_SCALE:V_SCALE + 1]).then_inc(n_t2e, 1)
                act.wait_ge(n_d, c + 1)
                nc.scalar.activation(GSA, GD, ACT.Silu)
                nc.scalar.activation(GSB, GD, ACT.Silu, scale=-1.0).then_inc(n_de, 1)
                for i in range(GC):
                    act.wait_ge(n_rt, c * GC + i + 1)
                    nc.scalar.activation(RTF[:, i * 512:(i + 1) * 512], bank(i, 1, 0, 48), ACT.Copy)
                    nc.scalar.activation(RTB[0:48, i * 512:(i + 1) * 512], bank(i, 1, 0, 48), ACT.Copy).then_inc(n_rte, 1)

            def experts(c):
                lo, hi = c * GC, (c + 1) * GC

                def sums(g):
                    act.wait_ge(l_y, g * E1 + (E1 + 2))
                    nc.scalar.activation(AT, PS[:, one(g % 2 + 4), :].rearrange("p a n -> p (a n)"),
                                         ACT.Copy).then_inc(n_acce, 1)

                def group(g, first=False):
                    for e in range(E1):
                        act.wait_ge(l_hm, g * E1 + (e + 3))
                        act.wait_ge(l_sx, g * E1 + (e + 1))
                        nc.scalar.activation(SG[e % 2], HM[e % 2], ACT.Silu, scale=ALPHA).then_inc(l_sg, 1)
                        if e == 1 and not first:
                            sums(g - 1)

                group(lo, True)
                with act.Fori(lo + 1, hi) as g:
                    group(g)
                sums(hi - 1)

            act.sem_inc(l_sg, 2)
            for c in range(CHUNKS):
                attention(c)
                route(c)
                experts(c)

        def layer2_dve(dve, S, bn, mean_rstd, second_norm, gathered):
            v = nc.vector
            mean, rstd, var, both, t1, t2 = (ST[:, i, :] for i in range(6))
            sh = [P, TC, D]

            def attention(c):
                lo, hi = c * GC, (c + 1) * GC
                mean_rstd(BS, mean, rstd, var, t1)

                def z(g):
                    for t in range(G):
                        i = (g - lo) * G + t
                        ins = v.tensor_scalar(ZT[:, t * D:(t + 1) * D], X[:, g * G + t, :], mean[:, one(i)],
                                              rstd[:, one(i)], ALU.subtract, ALU.mult)
                    ins.then_inc(n_z, 1)

                def values(g):
                    dve.wait_ge(n_kv, g + 1)
                    v.tensor_tensor(VP, bank(4, 1, 0, NC_CTX).rearrange("p (t n) -> p t n", t=G),
                                    ROWS[0:NC_CTX, R_BV:R_BV + D].unsqueeze(1).to_broadcast([NC_CTX, G, D]),
                                    ALU.add).then_inc(n_vpe, 1)

                def sigmoid(g):
                    dve.wait_ge(n_se, g + 1)
                    v.tensor_scalar(ZS, ZS, 0.5, 0.5, ALU.mult, ALU.add).then_inc(n_sh, 1)

                def x(g):
                    dve.wait_ge(n_o, g + 1)
                    tiles = bass.ds(g * G, G)
                    v.scalar_tensor_tensor(X[:, tiles, :], t3(bank(6)), TG[:, 2:3], X[:, tiles, :], ALU.mult,
                                           ALU.add).then_inc(n_x, 1)
                    dve.wait_ge(n_x, g + 1)
                    bn(X, BS, ([(g - lo) * G + t for t in range(G)], [g * G + t for t in range(G)]))

                z(lo)
                values(lo)
                dve.wait_ge(n_t, lo + 1)
                z(lo + 1)
                def body(g):
                    sigmoid(g)
                    dve.wait_ge(n_t, g + 2)
                    z(g + 2)
                    x(g)
                    values(g + 1)
                S.loop(lo, hi - 2, body, 1)
                sigmoid(hi - 2)
                x(hi - 2)
                values(hi - 1)
                sigmoid(hi - 1)
                x(hi - 1)
                S.wait()

            def route(c):
                lo, hi = c * GC, (c + 1) * GC
                mean_rstd(BS, mean, rstd, var, t1)
                second_norm(var, rstd, both, t1, t2)
                with dve.Fori(lo, hi) as g:
                    for t in range(G):
                        i = (g - lo) * G + t
                        ins = v.tensor_scalar(t3(ZB, TC)[:, i, :], X[:, g * G + t, :], mean[:, one(i)],
                                              both[:, one(i)], ALU.subtract, ALU.mult)
                    ins.then_inc(n_z2, 1)
                S.step(v.tensor_scalar(t1, rstd, TG[:, 3:4], None, ALU.mult))
                S.step(v.tensor_tensor(t2, t1, mean, ALU.mult))
                S.done(v.tensor_scalar(t1, t1, 1.0, None, ALU.add))
                dve.wait_ge(n_z2, hi)
                S.wait()
                xc = X[:, c * TC:(c + 1) * TC, :]
                S.step(v.tensor_tensor(xc, xc, t1.unsqueeze(2).to_broadcast(sh), ALU.mult))
                S.done(v.tensor_tensor(xc, xc, t2.unsqueeze(2).to_broadcast(sh), ALU.subtract))
                dve.wait_ge(n_g, c + 1)
                S.step(v.tensor_tensor(GL[:, :, 0:E1], t3(bank(7)[:, 0:TC * E1], TC),
                                       ROWS[:, R_GB1:R_GB1 + E1].unsqueeze(1).to_broadcast([P, TC, E1]), ALU.add))
                for t in range(TC):
                    ins = v.max(GM8[:, t, :], GL[:, t, 0:E1])
                S.step(ins)
                S.step(v.tensor_tensor(t3(GD, TC), GL[:, :, 0:E1], GM8[:, :, 0:1].to_broadcast([P, TC, E1]),
                                       ALU.subtract))
                v.tensor_scalar(GD, GD, -1.0, None, ALU.add).then_inc(n_d, 1)
                S.step(v.memset(GM8[:, :, K1:8], GONE))
                for t in range(TC):
                    ins = v.match_replace(GO[:, t, :], GM8[:, t, :], GL[:, t, :], 2 * GONE)
                S.step(ins)
                S.done(v.tensor_scalar(t3(GSEL, TC), GO[:, :, 0:E1], 2 * GONE, None, ALU.is_equal))
                dve.wait_ge(n_de, c + 1)
                S.step(v.reciprocal(GSB, GSB))
                S.step(v.tensor_tensor(GSA, GSA, GSB, ALU.mult))
                S.step(v.tensor_tensor(GSA, GSA, GSEL, ALU.mult))
                S.step(v.tensor_reduce(GSUM, t3(GSA, TC), AX_X, ALU.add))
                S.step(v.reciprocal(GSUM, GSUM))
                S.step(v.tensor_tensor(t3(GSA, TC), t3(GSA, TC), GSUM.unsqueeze(2).to_broadcast([P, TC, E1]), ALU.mult))
                S.step(v.tensor_copy(HIB, t3(GSA, TC)))
                S.step(v.tensor_copy(R48[:, :, 0, :], HIB))
                S.step(v.tensor_tensor(t3(GSA, TC), t3(GSA, TC), R48[:, :, 0, :], ALU.subtract))
                S.step(v.tensor_copy(HIB, t3(GSA, TC)))
                S.step(v.tensor_copy(R48[:, :, 1, :], HIB))
                v.tensor_tensor(R48[:, :, 2, :], t3(GSA, TC), R48[:, :, 1, :], ALU.subtract).then_inc(n_r, 1)

            def experts(c):
                lo, hi = c * GC, (c + 1) * GC

                def x(g):
                    dve.wait_ge(n_f, g + 1)
                    tiles = bass.ds(g * G, G)
                    v.scalar_tensor_tensor(X[:, tiles, :], t3(bank(7)), TG[:, 3:4], X[:, tiles, :], ALU.mult, ALU.add).then_inc(l_fin, 1)

                def group(g, first=False):
                    for e in range(E1 + 2):
                        if e < E1:
                            dve.wait_ge(l_h, g * E1 + (e + 1))
                            dve.wait_ge(l_sg, g * E1 + (e + 1))
                            v.tensor_scalar(HM[e % 2], bank(e % 2), VEC[:, V_BM1 + e:V_BM1 + e + 1], LIMIT,
                                            ALU.add, ALU.min).then_inc(l_hm, 1)
                        if e >= 2:
                            k = e - 2
                            dve.wait_ge(l_sg, g * E1 + (k + 3))
                            dve.wait_ge(l_bc, g * E1 + (k + 1))
                            dve.wait_ge(l_y, g * E1 + (k + 1))
                            v.scalar_tensor_tensor(SX[k % 2], SG[k % 2], (LIMIT + 1.0) / ALPHA, bank(2 + k % 2),
                                                   ALU.mult, ALU.mult).then_inc(l_sx, 1)
                        if e == 5 and not first:
                            x(g - 1)
                        if c + 1 < CHUNKS and e >= 6 and e % 3 == 0 and e < 18:
                            r = e // 3 - 2
                            gathered(g * 4 + (TC + r), r, (c + 1) * TC)

                gathers = 2 * G if c + 1 < CHUNKS else 0
                group(lo, True)
                S.loop(lo + 1, hi, group, gathers)
                x(hi - 1)

            dve.wait_ge(ld_hot, 16)
            v.tensor_copy(HOT, HOTF).then_inc(l_dve, 1)
            dve.wait_ge(ld_l, 16 * 7)
            dve.sem_inc(l_hm, 2)
            dve.sem_inc(l_sx, 2)
            for i in range(2):
                dve.wait_ge(e_st[i], 16 * (SS // 2) * CHUNKS)
            S.done(v.memset(RTB, 0.0))
            S.done(v.memset(GL[:, :, E1:E1 + 4], GONE))
            for c in range(CHUNKS):
                attention(c)
                route(c)
                experts(c)

        def layer2_pe(pe):
            mm = nc.tensor.matmul

            def attention(c):
                lo, hi = c * GC, (c + 1) * GC

                def projections(g, first=False):
                    pe.wait_ge(n_z, g + 1)
                    for t in range(G):
                        ins = nc.tensor.transpose(PS[:, 0, t * P:(t + 1) * P], ZT[:, t * D:(t + 1) * D], ID)
                    ins.then_inc(n_t, 1)
                    pe.wait_ge(l_cg, g * 16 + 16)
                    for t in range(G):
                        ins = nc.tensor.transpose(PS[:, 1, t * NC_CTX:(t + 1) * NC_CTX], CG[:, t, :],
                                                  ID[0:NC_CTX, 0:NC_CTX])
                    ins.then_inc(n_ct, 1)
                    pe.wait_ge(n_te, g + 1)
                    mm(bank(2, 1, 0, QK), WQT, XTL, start=True, stop=True).then_inc(n_q, 1)
                    pe.wait_ge(n_cte, g + 1)
                    mm(bank(3, 1, 0, QK)[:, 0:G * NC_CTX], WKT, CT, start=True, stop=True)
                    if not first:
                        pe.wait_ge(n_vpe, g)
                    for t in range(G):
                        ins = mm(PS[0:NC_CTX, 4, t * D:(t + 1) * D], CT[:, t * NC_CTX:(t + 1) * NC_CTX], WVT1,
                                 start=True, stop=True)
                    ins.then_inc(n_kv, 1)

                def scores(g):
                    pe.wait_ge(n_qe, g + 1)
                    pe.wait_ge(n_kpe, g + 1)
                    for t in range(G):
                        ins = mm(PS[0:NC_CTX, 5, t * P:(t + 1) * P], KP[:, t * NC_CTX:(t + 1) * NC_CTX],
                                 QP[:, t * P:(t + 1) * P], start=True, stop=True)
                    ins.then_inc(n_s, 1)

                def out(g):
                    pe.wait_ge(n_sh, g + 1)
                    pe.wait_ge(n_vpe, g + 1)
                    for t in range(G):
                        ins = mm(PS[:, 6, t * D:(t + 1) * D], ZS[:, t * P:(t + 1) * P], VP[:, t, :],
                                 start=True, stop=True)
                    ins.then_inc(n_o, 1)

                projections(lo, lo == 0)
                with pe.Fori(lo, hi - 1) as g:
                    scores(g)
                    projections(g + 1)
                    out(g)
                scores(hi - 1)
                out(hi - 1)

            def route(c):
                for i in range(GC):
                    pe.wait_ge(n_z2, c * GC + i + 1)
                    for t in range(G):
                        ins = nc.tensor.transpose(PS[:, i, t * P:(t + 1) * P], t3(ZB, TC)[:, i * G + t, :], ID)
                    ins.then_inc(n_t2, 1)
                for i in range(GC):
                    pe.wait_ge(n_t2e, c * GC + i + 1)
                    for t in range(i * G, (i + 1) * G):
                        ins = mm(PS[:, 7, t * E1:(t + 1) * E1], TT[:, t * P:(t + 1) * P], GW1, start=True, stop=True)
                ins.then_inc(n_g, 1)
                pe.wait_ge(n_r, c + 1)
                for i in range(GC):
                    for t in range(G):
                        ins = nc.tensor.transpose(PS[0:48, i, t * P:(t + 1) * P],
                                                  R48[:, i * G + t, :, :].rearrange("p j e -> p (j e)"), ID)
                    ins.then_inc(n_rt, 1)

            def experts(c):
                lo, hi = c * GC, (c + 1) * GC

                def acc(g):
                    return PS[:, one(g % 2 + 4), :].rearrange("p a n -> p (a n)")

                def cols(x, g):
                    return x[:, bass.ds((g - lo) * 512, 512)]

                def sums(g):
                    pe.wait_ge(n_acce, g + 1)
                    for t in range(G):
                        ins = nc.tensor.transpose(PS[:, 7, t * P:(t + 1) * P], AT[:, t * P:(t + 1) * P], ID)
                    ins.then_inc(n_f, 1)

                def group(g, first=False):
                    for e in range(E1 + 3):
                        if e < E1:
                            pe.wait_ge(l_hm, g * E1 + (e + 1))
                            mm(bank(e % 2), W1E[:, e, :], cols(TT, g), start=True, stop=True).then_inc(l_h, 1)
                        if e == 0:
                            mm(acc(g), B2S, cols(RTF, g), start=True, stop=False)
                        if 2 <= e < E1 + 2:
                            k = e - 2
                            pe.wait_ge(l_sx, g * E1 + (k + 1))
                            mm(bank(2 + k % 2), HOT[:, k * P:(k + 1) * P], cols(RTB, g), start=True,
                               stop=True).then_inc(l_bc, 1)
                        if e >= 3:
                            k = e - 3
                            pe.wait_ge(l_sx, g * E1 + (k + 3))
                            mm(acc(g), W2E[:, k, :], SX[k % 2], start=False, stop=(k == E1 - 1)).then_inc(l_y, 1)
                        if e == 2 and not first:
                            sums(g - 1)

                pe.wait_ge(n_rte, hi)
                group(lo, True)
                with pe.Fori(lo + 1, hi) as g:
                    group(g)
                sums(hi - 1)

            pe.wait_ge(ld_l, 16 * 7)
            pe.wait_ge(l_dve, 1)
            pe.sem_inc(l_y, 2)
            for c in range(CHUNKS):
                attention(c)
                route(c)
                experts(c)

        @block.sync
        def _(sp):
            for dst, name in ((CON, "con"), (VEC, "vec"), (ROWS, "rows")):
                sp.dma_start(dst[:], a[name]).then_inc(ld_c, 16)
            sp.dma_start(X[:, :, :], a["x"]).then_inc(ld_x, 16)
            sp.dma_start(CTX, a["ctx"]).then_inc(ld_x, 16)
            sp.dma_start(WVT, a["wvT"]).then_inc(ld_w, 16)
            sp.dma_start(WO, a["wo"]).then_inc(ld_w, 16)
            sp.dma_start(WQ, a["wq"]).then_inc(ld_w, 16)
            sp.dma_start(WK, a["wk"]).then_inc(ld_w, 16)
            sp.dma_start(W1[:], a["w1"]).then_inc(ld_m, 16)
            sp.dma_start(W2[:], a["w2"]).then_inc(ld_m, 16)
            sp.dma_start(GWT[:], a["gwT"]).then_inc(ld_r, 16)
            sp.dma_start(SGW[:, :, :], a["sgu"]).then_inc(ld_r, 16)
            sp.dma_start(SDW[:, :, :], a["sd"]).then_inc(ld_r, 16)
            sp.wait_ge(cbf, 1)
            for c in range(CHUNKS):
                z = ZERO.unsqueeze(1).to_broadcast([P, SLOTS, ROW])
                sp.dma_start(xs[c].rearrange("(s p) n -> p s n", p=P), z).then_inc(zeroed, 16)
            sp.dma_start(WGU[:, :, :], a["wgu"]).then_inc(ld_wgu, 16)

            for c in range(CHUNKS):
                sp.wait_ge(t_te, c + 1)
                sp.dma_start(te_d[c].rearrange("(p k) -> p k", k=2), TE[0:SLOTS // 2, c, :]).then_inc(t_ted, 16)
                sp.wait_ge(t_ted, 16 * (c + 1))
                sp.dma_start(TER[0:1, c * SLOTS:(c + 1) * SLOTS], te_d[c:c + 1, :]).then_inc(t_ter, 16)
            sp.wait_ge(a_y, B + 1)
            sp.dma_start(WD, a["wd"]).then_inc(ld_wd, 16)
            sp.wait_ge(t_rw, CHUNKS)
            for dst, name in ((W1E, "w1e"), (W2E, "w2e"), (WQT, "wqT1"), (WKT, "wkT1"), (WVT1, "wvT1"),
                              (GW1, "gw1"), (B2S, "b2s")):
                sp.dma_start(dst, a[name]).then_inc(ld_l, 16)
            sp.dma_start(HOTF, a["hot"]).then_inc(ld_hot, 16)

            def rows_of(t, step):
                return t[bass.ds(step * (G * P), G * P), :].rearrange("(p t) n -> p t n", p=P)

            for c in range(CHUNKS):
                o = c * SS
                for i in range(2):
                    sp.wait_ge(p_sc[i], 16 * TOPK * (TC // 2) * (c + 1))

                def load(i, r):
                    sp.dma_start(XB[r][:, :, :], rows_of(xs[c], i)).then_inc(e_ld[r], 16)

                def store(i, r):
                    sp.wait_ge(e_ye, o + i + 1)
                    sp.dma_start(rows_of(ys[c], i), YB[r % 2][:, :, :]).then_inc(e_st[r % 2], 16)

                if c == 0:
                    sp.wait_ge(r_x, B // G)
                for i in range(4):
                    if c:
                        sp.wait_ge(e_h, o - 4 + i + 2)
                    load(i, i)
                with sp.Fori(0, SS // 4 - 1) as q:
                    for r in range(4):
                        sp.wait_ge(e_h, q * 4 + (o + r + 2))
                        load(q * 4 + (r + 4), r)
                        store(q * 4 + r, r)
                for r in range(4):
                    store(SS - 4 + r, r)
            sp.wait_ge(l_dve, 1)
            sp.dma_start(CG[:, :, :], a["ctx"][:, 0:G, :]).then_inc(l_cg, 16)
            for c in range(CHUNKS):
                lo, hi = c * GC, (c + 1) * GC
                with sp.Fori(lo + 1, hi + 1 if hi < NGR else hi) as g:
                    sp.wait_ge(n_ct, g)
                    sp.dma_start(CG[:, :, :], a["ctx"][:, bass.ds(g * G, G), :]).then_inc(l_cg, 16)
                with sp.Fori(lo, hi) as g:
                    sp.wait_ge(l_fin, g + 1)
                    sp.dma_start(a["out"][:, bass.ds(g * G, G), :], X[:, bass.ds(g * G, G), :]).then_inc(l_out, 16)
            sp.wait_ge(l_out, 16 * NGR)

        @block.gpsimd
        def _(pool):
            def rows(c):
                if c:
                    for i in range(2):
                        pool.wait_ge(p_sc[i], 16 * TOPK * (TC // 2) * c)
                with pool.Fori(c * GC, (c + 1) * GC) as g:
                    pool.wait_ge(r_z, g + 1)
                    dst = XR[:, bass.ds(g * G - c * TC, G), 0:D]
                    nc.gpsimd.tensor_copy(dst, ZT[:, :].rearrange("p (t d) -> p t d", t=G)).then_inc(r_zc, 1)

            def scatter(c):
                pool.wait_ge(t_rw, c + 1)
                pool.wait_ge(r_zc, (c + 1) * GC)
                pool.wait_ge(zeroed, 16 * CHUNKS)
                lo, _ = chunk_tiles(c)
                for t in range(TC):
                    b = lo + t
                    for k in range(TOPK):
                        pool.indirect_dma_start(
                            out=xs[c], in_=XR[:, t, :], in_offset=None,
                            out_offset=bass.IndirectOffsetOnAxis(ap=POS[:, b * TOPK + k:b * TOPK + k + 1], axis=0),
                        ).then_inc(p_sc[t % 2], 16)

            def gather(c):
                lo, hi = chunk_tiles(c)
                for i in range(2):
                    pool.wait_ge(e_st[i], 16 * (SS // 2) * (c + 1))
                for b in range(lo, hi):
                    r = b % 4
                    if b >= 4:
                        pool.wait_ge(l_red, b - 3)
                    for k in range(TOPK):
                        pool.indirect_dma_start(
                            out=GBUF[r][:, k * D:(k + 1) * D], out_offset=None, in_=ys[c],
                            in_offset=bass.IndirectOffsetOnAxis(ap=POS[:, b * TOPK + k:b * TOPK + k + 1], axis=0),
                        ).then_inc(l_g[r], 16)

            for c in range(CHUNKS):
                rows(c)
                scatter(c)
            for c in range(CHUNKS):
                gather(c)

        @block.scalar
        def _(act):
            S = Steps(astep, act)
            act.wait_ge(ld_c, 48)
            nc.scalar.activation(TG[:], VEC[:, V_GATES:V_GATES + 4], ACT.Tanh).then_inc(gates, 1)
            for i in range(4):
                act.wait_ge(wh_mm, i + 1)
                nc.scalar.activation(AW[:, 2048 + 512 * i:2560 + 512 * i], bank(1 + i), ACT.Copy).then_inc(wh_ok, 1)

            def attention(c):
                lo, hi = chunk_tiles(c)

                def qk_in(b):
                    act.wait_ge(a_t, b + 1)
                    nc.scalar.activation(QNT, PS[:, 0, 0:P], ACT.Identity,
                                         bias=VEC[:, V_LN1B:V_LN1B + 1], scale=VEC[:, V_LN1G:V_LN1G + 1])
                    nc.scalar.activation(KNT, PS[:, 0, P:P + NC_CTX], ACT.Identity,
                                         bias=VEC[:, V_LN1B:V_LN1B + 1],
                                         scale=VEC[:, V_LN1G:V_LN1G + 1]).then_inc(a_qk, 1)

                def q_sq(b):
                    act.wait_ge(a_q, b + 1)
                    nc.scalar.activation(SQQ, bank(1, 2), ACT.Square).then_inc(a_sq, 1)

                def k_sq(b):
                    act.wait_ge(a_k, b + 1)
                    nc.scalar.activation(SQK[0:NC_CTX, :], bank(3, 2, 0, NC_CTX), ACT.Square).then_inc(a_sq, 1)

                def roots(b, j):
                    act.wait_ge(a_n2, b * 2 + (1 + j))
                    h = slice(j * H, (j + 1) * H)
                    nc.scalar.activation(RN[:, h], N2[:, h], ACT.Sqrt).then_inc(a_rt, 1)

                def out2(ready, done, dst, b):
                    act.wait_ge(ready, b + 1)
                    nc.scalar.activation(dst, bank(5, 2), ACT.Copy).then_inc(done, 1)

                def g_out(b, j):
                    act.wait_ge(a_g, b * 2 + (1 + j))
                    nc.scalar.activation(GB[:, 512 * j:512 * (j + 1)], bank(5 + j), ACT.Copy).then_inc(a_ge, 1)

                qk_in(lo)
                q_sq(lo)
                roots(lo, 0)
                k_sq(lo)
                roots(lo, 1)
                with act.Fori(lo, hi - 1) as b:
                    qk_in(b + 1)
                    out2(a_qt, a_qte, QT, b)
                    q_sq(b + 1)
                    out2(a_p, a_pe, PB, b)
                    roots(b + 1, 0)
                    k_sq(b + 1)
                    g_out(b, 0)
                    roots(b + 1, 1)
                    g_out(b, 1)
                out2(a_qt, a_qte, QT, hi - 1)
                out2(a_p, a_pe, PB, hi - 1)
                g_out(hi - 1, 0)
                g_out(hi - 1, 1)

            def mlp(c):
                lo, hi = c * GC, (c + 1) * GC

                def z_out(g):
                    act.wait_ge(m_t, g + 1)
                    nc.scalar.activation(XT, bank(0), ACT.Identity, bias=VEC[:, V_LN2B:V_LN2B + 1],
                                         scale=VEC[:, V_LN2G:V_LN2G + 1]).then_inc(m_te, 1)

                def gelu(g):
                    for n in range(4):
                        act.wait_ge(m_h, g * 4 + (n + 1))
                        nc.scalar.activation(HT[:, n, :], bank(1 + n), ACT.Gelu,
                                             bias=VEC[:, V_B1 + n:V_B1 + n + 1]).then_inc(m_he, 1)

                z_out(lo)
                gelu(lo)
                with act.Fori(lo, hi - 1) as g:
                    z_out(g + 1)
                    gelu(g + 1)

            def route(c):
                lo, hi = c * GC, (c + 1) * GC

                def z_out(g):
                    act.wait_ge(r_t, g + 1)
                    nc.scalar.activation(XT, bank(0), ACT.Copy).then_inc(r_te, 1)

                def silus(g):
                    for n in range(2):
                        act.wait_ge(r_gu, g * 2 + (n + 1))
                        nc.scalar.activation(SIL[:, n, :], bank(1 + 2 * n, 1, 0, EI), ACT.Silu).then_inc(r_si, 1)

                z_out(lo)
                silus(lo)
                with act.Fori(lo, hi - 1) as g:
                    z_out(g + 1)
                    silus(g + 1)
                act.wait_ge(r_le, (c + 1) * GC)
                nc.scalar.activation(RS, RS, ACT.Sigmoid).then_inc(t_s, 1)

            def experts(c):
                o = c * SS

                def x_out(i):
                    act.wait_ge(e_t, o + i + 1)
                    nc.scalar.activation(EXT, bank(0), ACT.Copy).then_inc(e_te, 1)

                def silu(i, u):
                    act.wait_ge(e_gu, o + i + 1)
                    act.wait_ge(e_h, o + i + 1)
                    nc.scalar.activation(ESI, gu_bank[u][:, :, 0:EI], ACT.Silu).then_inc(e_si, 1)

                def y_out(i, u, first=False):
                    act.wait_ge(e_y, o + i + 1)
                    if not first:
                        act.wait_ge(e_st[u], i * 8 + (16 * (o // 2) - 8 * u))
                    nc.scalar.activation(YB[u][:, :, :].rearrange("p t n -> p (t n)"), bank(6 + u),
                                         ACT.Copy).then_inc(e_ye, 1)

                x_out(0)
                silu(0, 0)
                x_out(1)
                silu(1, 1)
                x_out(2)

                def body(i, r, first=False):
                    x_out(i + 2)
                    silu(i + 1, (r + 1) % 2)
                    y_out(i - 1, (r - 1) % 2, first)

                body(1, 1, c == 0)
                body(2, 2, c == 0)
                with act.Fori(0, (SS - 8) // 4) as q:
                    for r in range(4):
                        body(q * 4 + (3 + r), 3 + r)
                i = 3 + (SS - 8)
                while i + 2 < SS:
                    body(i, i % 4)
                    i += 1
                silu(SS - 1, 1)
                y_out(SS - 3, 1)
                y_out(SS - 2, 0)
                y_out(SS - 1, 1)

            for c in range(CHUNKS):
                attention(c)
                mlp(c)
                route(c)
            for c in range(CHUNKS):
                experts(c)
            layer2_act(act)

        @block.vector
        def _(dve):
            v = nc.vector
            S = Steps(dstep, dve)
            v.memset(ZERO, 0.0)
            S.done(v.memset(N2[:], 1.0))
            S.done(v.memset(ONB[:], 1.0))
            S.done(v.memset(NT[:, 3, :], 1.0))
            dve.wait_ge(ld_c, 48)
            v.tensor_copy(UPB[:], CON[:, C_UP:C_UP + P]).then_inc(cbf, 1)
            dve.sem_inc(a_y, 1)
            dve.sem_inc(m_x, 1)
            dve.wait_ge(ld_x, 32)
            dve.wait_ge(gates, 1)

            def rsqrt(dst, src, tmp):
                S.step(v.tensor_scalar(tmp.bitcast(I32), src.bitcast(I32), 1, None, ALU.logical_shift_right))
                S.step(v.tensor_scalar(dst.bitcast(I32), tmp.bitcast(I32), -1, 0x5F3759DF, ALU.mult, ALU.add))
                for _ in range(3):
                    S.step(v.scalar_tensor_tensor(tmp, dst, -0.5, dst, ALU.mult, ALU.mult))
                    S.step(v.tensor_tensor(tmp, tmp, src, ALU.mult))
                    S.step(v.scalar_tensor_tensor(dst, tmp, 1.5, dst, ALU.add, ALU.mult))

            def mean_rstd(stats, mean, rstd, var, t1):
                f = lambda k: stats[:, :, k]
                S.step(v.tensor_tensor(mean, f(1), f(4), ALU.add))
                S.done(v.tensor_scalar(mean, mean, 0.5, None, ALU.mult))
                S.step(v.tensor_tensor(t1, f(1), f(4), ALU.subtract))
                S.done(v.tensor_tensor(var, f(2), f(5), ALU.add))
                S.step(v.scalar_tensor_tensor(t1, t1, 0.25, t1, ALU.mult, ALU.mult))
                S.step(v.scalar_tensor_tensor(var, var, 1.0 / D, t1, ALU.mult, ALU.add))
                S.step(v.tensor_scalar(var, var, EPS, None, ALU.add))
                rsqrt(rstd, var, t1)

            def second_norm(var, rstd, both, t1, t2):
                S.step(v.tensor_scalar(t2, var, -EPS, None, ALU.add))
                S.step(v.tensor_tensor(t2, t2, rstd, ALU.mult))
                S.step(v.tensor_tensor(t2, t2, rstd, ALU.mult))
                S.step(v.tensor_scalar(t2, t2, EPS, None, ALU.add))
                rsqrt(both, t2, t1)
                S.step(v.tensor_tensor(both, both, rstd, ALU.mult))

            def bn(src, dst, places):
                v.memset(NT[:, 2, 0:1], 0.0)
                for i, j in zip(*places):
                    ins = v.bn_stats(dst[:, i, :], src[:, j, :])
                S.done(ins)

            mean, rstd, var, both, t1, t2 = (ST[:, i, :] for i in range(6))
            k = slice(0, NC_CTX)

            def attention_stats(c):
                lo, _ = chunk_tiles(c)

                def four(q):
                    for j in range(G):
                        v.bn_stats(BSX[:, q * G + j, :], X[:, q * G + (lo + j), :])
                        ins = v.bn_stats(BSC[k, q * G + j, :], CTX[:, q * G + (lo + j), :])
                    S.done(ins)
                S.loop(0, TC // G, four, 1)
                S.wait()
                mean_rstd(BSX, STX[:, 0, :], STX[:, 1, :], var, t1)
                second_norm(var, STX[:, 1, :], STX[:, 2, :], t1, t2)
                mean_rstd(BSC[k], STC[:, 0, :], STC[:, 1, :], STC[:, 2, :], t1[k])

            def attention(c):
                lo, hi = chunk_tiles(c)
                meanx, rstdx, bothx = (STX[:, i, :] for i in range(3))
                meanc, rstdc = (STC[:, i, :] for i in range(2))

                def z(b):
                    i = b - lo
                    v.tensor_scalar(ZT[:, 0:D], X[:, b, :], meanx[:, one(i)], bothx[:, one(i)], ALU.subtract, ALU.mult)
                    v.tensor_scalar(ZC, CTX[:, b, :], meanc[:, one(i)], rstdc[:, one(i)],
                                    ALU.subtract, ALU.mult).then_inc(a_z, 1)

                def next_z(b):
                    dve.wait_ge(a_t, b)
                    z(b)

                def residual(b):
                    i = b - lo
                    S.step(v.tensor_scalar(Y[:, b, :], X[:, b, :], meanx[:, one(i)], rstdx[:, one(i)],
                                           ALU.subtract, ALU.mult))
                    S.done(v.tensor_tensor(Y[:, b, :], Y[:, b, :], ROWS[:, R_BO:R_BO + D], ALU.add))

                def vn(b):
                    i = b - lo
                    S.step(v.tensor_scalar(VN, CTX[:, b, :], meanc[:, one(i)], rstdc[:, one(i)],
                                           ALU.subtract, ALU.mult))
                    S.step(v.tensor_tensor(VN, VN, ROWS[k, R_LN1G:R_LN1G + D], ALU.mult))
                    v.tensor_tensor(VN, VN, ROWS[k, R_LN1B:R_LN1B + D], ALU.add).then_inc(a_vn, 1)

                def normalise(b, j, n, squares, src, dst, done):
                    h = slice(j * H, (j + 1) * H)
                    dve.wait_ge(a_sq, b * 2 + (1 + j))
                    v.tensor_reduce(N2[0:n, h], squares.rearrange("p (h d) -> p h d", h=H), AX_X,
                                    ALU.add).then_inc(a_n2, 1)
                    dve.wait_ge(a_rt, b * 2 + (1 + j))
                    S.step(v.tensor_scalar(RN[0:n, h], RN[0:n, h], 1e-12, None, ALU.max))
                    S.step(v.reciprocal(RN[0:n, h], RN[0:n, h]))
                    v.tensor_tensor(dst.rearrange("p (h d) -> p h d", h=H), src.rearrange("p (h d) -> p h d", h=H),
                                    RN[0:n, h].unsqueeze(2).to_broadcast([n, H, DH]), ALU.mult).then_inc(done, 1)

                def queries(b):
                    normalise(b, 0, P, SQQ, bank(1, 2), QN, a_qn)

                def keys(b):
                    normalise(b, 1, NC_CTX, SQK[k, :], bank(3, 2, 0, NC_CTX), KN[k, :], a_kn)

                def y(b):
                    dve.wait_ge(a_o, b + 1)
                    v.tensor_tensor(Y[:, b, :], bank(7)[:, 0:D], Y[:, b, :], ALU.add).then_inc(a_y, 1)
                    dve.wait_ge(a_y, b + 2)
                    bn(Y, BS, ([b - lo], [b]))

                z(lo)
                vn(lo)
                queries(lo)
                keys(lo)
                next_z(lo + 1)

                def body(b, last=False):
                    if not last:
                        next_z(b + 2)
                    residual(b)
                    queries(b + 1)
                    dve.wait_ge(a_p, b + 1)
                    vn(b + 1)
                    keys(b + 1)
                    y(b)
                S.loop(lo, hi - 2, body, 9)
                body(hi - 2, True)
                residual(hi - 1)
                S.wait()
                y(hi - 1)
                S.wait()

            def mlp(c):
                lo, hi = c * GC, (c + 1) * GC
                mean_rstd(BS, mean, rstd, var, t1)

                def z(g):
                    for t in range(G):
                        i = (g - lo) * G + t
                        ins = v.tensor_scalar(ZT[:, t * D:(t + 1) * D], Y[:, g * G + t, :], mean[:, one(i)],
                                              rstd[:, one(i)], ALU.subtract, ALU.mult)
                    ins.then_inc(m_z, 1)

                def x(g):
                    dve.wait_ge(m_o, g + 1)
                    tiles = bass.ds(g * G, G)
                    tmp = TMP.rearrange("p (t d) -> p t d", t=G)
                    S.step(v.tensor_tensor(tmp, bank(5).rearrange("p (t d) -> p t d", t=G), Y[:, tiles, :], ALU.add))
                    S.step(v.tensor_tensor(tmp, tmp, ROWS[:, R_B2:R_B2 + D].unsqueeze(1).to_broadcast([P, G, D]),
                                           ALU.add))
                    v.scalar_tensor_tensor(X[:, tiles, :], tmp, TG[:, 0:1], X[:, tiles, :], ALU.mult,
                                           ALU.add).then_inc(m_x, 1)
                    dve.wait_ge(m_x, g + 2)
                    bn(X, BS, ([(g - lo) * G + t for t in range(G)], [g * G + t for t in range(G)]))

                z(lo)
                dve.wait_ge(m_t, lo + 1)
                z(lo + 1)
                if c + 1 < CHUNKS:
                    attention_stats(c + 1)

                def body(g):
                    dve.wait_ge(m_t, g + 2)
                    z(g + 2)
                    x(g)
                S.loop(lo, hi - 2, body, 3)
                x(hi - 2)
                x(hi - 1)
                S.wait()

            def route(c):
                lo, hi = c * GC, (c + 1) * GC
                if c:
                    for i in range(2):
                        dve.wait_ge(p_sc[i], 16 * TOPK * (TC // 2) * c)
                else:
                    dve.wait_ge(zeroed, 16 * CHUNKS)
                mean_rstd(BS, mean, rstd, var, t1)

                def z(g):
                    for t in range(G):
                        i = (g - lo) * G + t
                        ins = v.tensor_scalar(ZT[:, t * D:(t + 1) * D], X[:, g * G + t, :], mean[:, one(i)],
                                              rstd[:, one(i)], ALU.subtract, ALU.mult)
                    ins.then_inc(r_z, 1)

                def rest(g):
                    dve.wait_ge(r_l, g + 1)
                    v.tensor_copy(RS.rearrange("p (g n) -> p g n", g=GC)[:, g - lo, :], bank(7)[:, 0:G * E],
                                  ).then_inc(r_le, 1)
                    for n in range(2):
                        dve.wait_ge(r_si, g * 2 + (n + 1))
                        v.tensor_tensor(SHH[:, n, :], SIL[:, n, :], bank(2 + 2 * n, 1, 0, EI), ALU.mult).then_inc(r_h, 1)
                    dve.wait_ge(r_o, g + 1)
                    v.scalar_tensor_tensor(X[:, bass.ds(g * G, G), :], bank(5).rearrange("p (t d) -> p t d", t=G),
                                           TG[:, 1:2], X[:, bass.ds(g * G, G), :], ALU.mult, ALU.add).then_inc(r_x, 1)

                z(lo)
                with dve.Fori(lo, hi - 1) as g:
                    dve.wait_ge(r_t, g + 1)
                    dve.wait_ge(r_zc, g + 1)
                    z(g + 1)
                    rest(g)
                rest(hi - 1)
                dve.wait_ge(r_zc, hi)
                tables(c)

            def tables(c):
                t3 = lambda x, n=TC: x.rearrange("p (t e) -> p t e", t=n)
                C = t3(RC)
                dve.wait_ge(t_s, c + 1)
                S.step(v.tensor_tensor(C, t3(RS), ROWS[:, R_GBIAS:R_GBIAS + E].unsqueeze(1).to_broadcast([P, TC, E]),
                                       ALU.add))
                c8 = RC.rearrange("p (n w) -> p n w", w=8)
                N = TC * NG
                hi0 = RA[:, 0:512].rearrange("p (n w) -> p n w", w=4)
                lo0 = RA[:, 512:1024].rearrange("p (n w) -> p n w", w=4)
                hi1 = RB[:, 0:256].rearrange("p (n w) -> p n w", w=2)
                lo1 = RB[:, 256:512].rearrange("p (n w) -> p n w", w=2)
                m1 = RB[:, 512:768].rearrange("p (n w) -> p n w", w=2)
                S.done(v.tensor_tensor(hi0, c8[:, :, 0:4], c8[:, :, 4:8], ALU.max))
                S.step(v.tensor_tensor(lo0, c8[:, :, 0:4], c8[:, :, 4:8], ALU.min))
                S.done(v.tensor_tensor(hi1, hi0[:, :, 0:2], hi0[:, :, 2:4], ALU.max))
                S.done(v.tensor_tensor(m1, hi0[:, :, 0:2], hi0[:, :, 2:4], ALU.min))
                S.step(v.tensor_tensor(lo1, lo0[:, :, 0:2], lo0[:, :, 2:4], ALU.max))
                S.step(v.tensor_tensor(lo1, lo1, m1, ALU.max))
                gs, gl, gm = RK[:, 0:N], RK[:, N:2 * N], RK[:, 2 * N:3 * N]
                S.done(v.tensor_tensor(gs, hi1[:, :, 0], hi1[:, :, 1], ALU.max))
                S.done(v.tensor_tensor(gm, hi1[:, :, 0], hi1[:, :, 1], ALU.min))
                S.step(v.tensor_tensor(gl, lo1[:, :, 0], lo1[:, :, 1], ALU.max))
                S.step(v.tensor_tensor(gl, gl, gm, ALU.max))
                S.step(v.tensor_tensor(gs, gs, gl, ALU.add))
                sh = [P, TC, NG, NG]
                g3 = gs.rearrange("p (t g) -> p t g", t=TC)
                mine, other = g3.unsqueeze(3).to_broadcast(sh), g3.unsqueeze(2).to_broadcast(sh)
                ra, rb = (x.rearrange("p (t g j) -> p t g j", t=TC, g=NG) for x in (RA, RB))
                S.done(v.tensor_tensor(ra, other, mine, ALU.is_gt))
                S.step(v.tensor_tensor(rb, other, mine, ALU.is_equal))
                low = CON[:, C_LOW:C_LOW + 64].unsqueeze(1).to_broadcast([P, TC, 64])
                S.step(v.tensor_tensor(t3(RB), t3(RB), low, ALU.mult))
                S.step(v.tensor_tensor(RA, RA, RB, ALU.add))
                S.step(v.tensor_reduce(gl, RA.rearrange("p (n j) -> p n j", j=NG), AX_X, ALU.add))
                S.step(v.tensor_scalar(gl, gl, TOPG - 0.5, None, ALU.is_lt))
                S.step(v.tensor_tensor(c8, c8, gl.unsqueeze(2).to_broadcast([P, N, 8]), ALU.mult))
                m8 = RK[:, 0:TC * 8].rearrange("p (t k) -> p t k", t=TC)
                A = t3(RA)
                for t in range(TC):
                    ins = v.max(m8[:, t, :], C[:, t, :])
                S.step(ins)
                for t in range(TC):
                    ins = v.match_replace(A[:, t, :], m8[:, t, :], C[:, t, :], GONE)
                S.step(ins)
                S.step(v.tensor_scalar(RB, RA, GONE, None, ALU.is_equal))
                v.tensor_copy(SELB[:, :, :], t3(RB)).then_inc(t_sel, 1)
                S.done(v.memset(CSB[:, 0, :], 0.0))
                sel3 = t3(RB)
                for t in range(1, TC):
                    S.wait()
                    S.done(v.tensor_tensor(CSB[:, t, :], CSB[:, t - 1, :], sel3[:, t - 1, :], ALU.add))
                S.wait()
                v.memset(NT[:, 2, 0:1], 0.0).then_inc(t_sel, 1)
                S.step(v.tensor_tensor(RS, RS, RB, ALU.mult))
                sm = RK[:, 512:512 + TC]
                S.step(v.tensor_reduce(sm, t3(RS), AX_X, ALU.add))
                S.step(v.tensor_scalar(sm, sm, 1e-20, None, ALU.add))
                S.step(v.reciprocal(sm, sm))
                S.step(v.tensor_scalar(sm, sm, 2.5, None, ALU.mult))
                S.done(v.tensor_tensor(XR[:, :, D:ROW], t3(RS), sm.unsqueeze(2).to_broadcast([P, TC, E]), ALU.mult))
                dve.wait_ge(t_rank, c + 1)
                nt, end, base = NT[:, 0, :], NT[:, 1, :], NT[:, 2, :]
                S.step(v.tensor_copy(end, bank(7)[:, 0:E]))
                sh = [P, E, TC]
                big = RC.rearrange("p (e j) -> p e j", e=E)
                S.step(v.tensor_tensor(big, end.unsqueeze(2).to_broadcast(sh),
                                       CON[:, C_STEP:C_STEP + TC].unsqueeze(1).to_broadcast(sh), ALU.is_gt))
                S.step(v.tensor_reduce(nt, big, AX_X, ALU.add))
                S.step(v.tensor_tensor_scan(end, NT[:, 3, :], nt, 0.0, ALU.mult, ALU.add))
                S.step(v.tensor_tensor(base, end, nt, ALU.subtract))
                S.step(v.tensor_scalar(base, base, float(P), None, ALU.mult))
                n = SLOTS // 2
                for j in range(2):
                    w = RC[0:n, 64 * j:64 * j + 64]
                    S.done(v.tensor_scalar(w, end[0:n], CON[0:n, C_SLOT + j:C_SLOT + j + 1], None, ALU.is_le))
                S.wait()
                S.step(v.tensor_reduce(NT[0:n, 0, 0:2], RC[0:n, 0:128].rearrange("p (j e) -> p j e", j=2), AX_X, ALU.add))
                v.tensor_scalar(TE[0:n, c, :], NT[0:n, 0, 0:2], E - 1.0, None, ALU.min).then_inc(t_te, 1)
                S.step(v.tensor_tensor(t3(RA), bank(5, 2).rearrange("p (t e) -> p t e", t=TC),
                                       base.unsqueeze(1).to_broadcast([P, TC, E]), ALU.add))
                S.step(v.tensor_scalar(RA, RA, -1.0, BIG, ALU.mult, ALU.add))
                S.step(v.tensor_tensor(RA, RA, RB, ALU.mult))
                for t in range(TC):
                    ins = v.max(m8[:, t, :], t3(RA)[:, t, :])
                S.step(ins)
                pos = POS[:, c * TC * TOPK:(c + 1) * TC * TOPK]
                slot, r4 = (RC[:, 128 * i:128 * (i + 1)].bitcast(U32) for i in range(2))
                S.step(v.tensor_scalar(pos, RK[:, 0:TC * 8], -1.0, BIG, ALU.mult, ALU.add))
                S.done(v.tensor_scalar(slot, pos, 7, G - 1, ALU.logical_shift_right, ALU.bitwise_and))
                S.step(v.tensor_scalar(r4, pos, P - 1, 2, ALU.bitwise_and, ALU.logical_shift_left))
                S.step(v.tensor_tensor(slot, slot, r4, ALU.bitwise_or))
                S.step(v.tensor_scalar(pos, pos, 9, 9, ALU.logical_shift_right, ALU.logical_shift_left))
                v.tensor_tensor(pos, pos, slot, ALU.bitwise_or).then_inc(t_rw, 1)
                dve.wait_ge(t_rw, c + 1)

            def gathered(b, r, lo):
                dve.wait_ge(l_g[r], (b - r) * (4 * TOPK) + 16 * TOPK)
                S.step(v.tensor_reduce(RED, GBUF[r].rearrange("p (k d) -> p d k", k=TOPK), AX_X, ALU.add))
                v.scalar_tensor_tensor(X[:, b, :], RED, TG[:, 1:2], X[:, b, :], ALU.mult, ALU.add).then_inc(l_red, 1)
                dve.wait_ge(l_red, b + 1)
                bn(X, BS, ([b - lo], [b]))

            def experts(c):
                o = c * SS

                def h(i, r):
                    e = slot_experts(dve, c, i)
                    dve.wait_ge(e_si, o + i + 1)
                    dve.wait_ge(e_ht, o + i + 1)
                    for t in range(G):
                        ins = v.scalar_tensor_tensor(EH[:, t, :], ESI[:, t, :], XB[r][:, t, one(e[t] + D)],
                                                     gu_bank[r % 2][:, t, EI:2 * EI], ALU.mult, ALU.mult)
                    ins.then_inc(e_h, 1)

                def hT_out(i, r):
                    dve.wait_ge(e_ht, o + i + 2)
                    v.tensor_copy(EHT[r % 2], bank(5, 1, 0, EI)).then_inc(e_hte, 1)

                h(0, 0)

                def body(i, r):
                    hT_out(i, r)
                    h(i + 1, (r + 1) % 4)
                done = 0
                if c:
                    done = GC * 8
                    start = (c - 1) * TC
                    def steps8(q):
                        for r in range(8):
                            body(q * 8 + r, r % 4)
                            if r % 2:
                                gathered(q * 4 + (start + r // 2), r // 2, start)
                    S.loop(0, GC, steps8, 8)
                with dve.Fori(done // 4, SS // 4 - 1) as q:
                    for r in range(4):
                        body(q * 4 + r, r)
                for i in range(SS - 4, SS - 1):
                    body(i, i % 4)
                hT_out(SS - 1, 3)

            attention_stats(0)
            for c in range(CHUNKS):
                attention(c)
                mlp(c)
                route(c)
            dve.sem_inc(e_h, 1)
            dve.wait_ge(t_ter, 16 * CHUNKS)
            for c in range(CHUNKS):
                experts(c)
            layer2_dve(dve, S, bn, mean_rstd, second_norm, gathered)

        @block.tensor
        def _(pe):
            mm = nc.tensor.matmul
            pe.wait_ge(ld_c, 48)
            pe.wait_ge(ld_w, 64)
            for i in range(4):
                for j in range(4):
                    h = 4 * i + j
                    ins = mm(PS[:, 1 + i, j * D:(j + 1) * D], WVT[:, h, :], WO[:, h, :], start=True, stop=True)
                ins.then_inc(wh_mm, 1)
            pe.wait_ge(wh_ok, 4)

            def attention(c):
                lo, hi = chunk_tiles(c)

                def T(b):
                    pe.wait_ge(a_z, b + 1)
                    nc.tensor.transpose(PS[:, 0, 0:P], ZT[:, 0:D], ID)
                    nc.tensor.transpose(PS[:, 0, P:P + NC_CTX], ZC, ID[0:NC_CTX, 0:NC_CTX]).then_inc(a_t, 1)

                def q(b):
                    pe.wait_ge(a_qk, b + 1)
                    for j in range(2):
                        ins = mm(PS[:, 1 + j, :], QNT, WQ[:, 512 * j:512 * (j + 1)], start=True, stop=True)
                    ins.then_inc(a_q, 1)

                def k(b):
                    for j in range(2):
                        ins = mm(PS[0:NC_CTX, 3 + j, :], KNT, WK[:, 512 * j:512 * (j + 1)], start=True, stop=True)
                    ins.then_inc(a_k, 1)

                def qT(b):
                    pe.wait_ge(a_qn, b + 1)
                    for j in range(8):
                        ins = nc.tensor.transpose(bank(5, 2)[:, j * P:(j + 1) * P], QN[:, j * P:(j + 1) * P], ID)
                    ins.then_inc(a_qt, 1)

                def p(b):
                    pe.wait_ge(a_qte, b + 1)
                    pe.wait_ge(a_kn, b + 1)
                    pe.wait_ge(a_vn, b + 1)
                    for j in range(2):
                        ins = mm(PS[:, 5 + j, :], VN, KN[0:NC_CTX, 512 * j:512 * (j + 1)], start=True, stop=True)
                    ins.then_inc(a_p, 1)

                def g(b):
                    pe.wait_ge(a_pe, b + 1)
                    for h in range(H):
                        r = DH * (h % 2)
                        ins = mm(PS[r:r + DH, 5 + h // 8, (h // 2 % 4) * D:(h // 2 % 4 + 1) * D],
                                 PB[:, h * DH:(h + 1) * DH], WH[:, h, :], start=True, stop=True)
                        if h % 8 == 7:
                            ins.then_inc(a_g, 1)

                def o(b):
                    pe.wait_ge(a_y, b + 1)
                    for j in range(8):
                        if j % 4 == 0:
                            pe.wait_ge(a_ge, b * 2 + (1 + j // 4))
                        ins = mm(PS[:, 7, 0:D], QT[:, j * P:(j + 1) * P], GB[:, j * D:(j + 1) * D],
                                 start=(j == 0), stop=(j == 7))
                    ins.then_inc(a_o, 1)

                T(lo)
                q(lo)
                k(lo)
                with pe.Fori(lo, hi - 1) as b:
                    T(b + 1)
                    qT(b)
                    q(b + 1)
                    p(b)
                    k(b + 1)
                    g(b)
                    o(b)
                qT(hi - 1)
                p(hi - 1)
                g(hi - 1)
                o(hi - 1)

            def transposes(ready, done, g):
                pe.wait_ge(ready, g + 1)
                for t in range(G):
                    ins = nc.tensor.transpose(PS[:, 0, t * P:(t + 1) * P], ZT[:, t * D:(t + 1) * D], ID)
                ins.then_inc(done, 1)

            def mlp(c):
                lo, hi = c * GC, (c + 1) * GC

                def up(g):
                    pe.wait_ge(m_te, g + 1)
                    for n in range(4):
                        mm(bank(1 + n), W1[:, n * P:(n + 1) * P], XT, start=True, stop=True).then_inc(m_h, 1)

                def down(g):
                    pe.wait_ge(m_x, g + 1)
                    pe.wait_ge(m_he, g * 4 + 4)
                    for t in range(G):
                        for n in range(4):
                            ins = mm(PS[:, 5, t * D:(t + 1) * D], HT[:, n, t * P:(t + 1) * P],
                                     W2[:, n * D:(n + 1) * D], start=(n == 0), stop=(n == 3))
                    ins.then_inc(m_o, 1)

                transposes(m_z, m_t, lo)
                up(lo)
                with pe.Fori(lo, hi - 1) as g:
                    transposes(m_z, m_t, g + 1)
                    down(g)
                    up(g + 1)
                down(hi - 1)

            def route(c):
                lo, hi = c * GC, (c + 1) * GC

                def rest(g):
                    pe.wait_ge(r_te, g + 1)
                    for n in range(4):
                        ins = mm(bank(1 + n, 1, 0, EI), SGW[:, n, :], XT, start=True, stop=True)
                        if n % 2:
                            ins.then_inc(r_gu, 1)
                    for t in range(G):
                        ins = mm(PS[:, 7, t * E:(t + 1) * E], XT[:, t * P:(t + 1) * P], GWT[:], start=True, stop=True)
                    ins.then_inc(r_l, 1)

                def down(g):
                    pe.wait_ge(r_h, g * 2 + 2)
                    for t in range(G):
                        for n in range(2):
                            ins = mm(PS[:, 5, t * D:(t + 1) * D], SHH[:, n, t * P:(t + 1) * P], SDW[:, n, :],
                                     start=(n == 0), stop=(n == 1))
                    ins.then_inc(r_o, 1)

                transposes(r_z, r_t, lo)
                rest(lo)
                with pe.Fori(lo, hi - 1) as g:
                    transposes(r_z, r_t, g + 1)
                    down(g)
                    rest(g + 1)
                down(hi - 1)
                pe.wait_ge(t_sel, 2 * c + 2)
                flat = lambda x: x[:, :, :].rearrange("p t e -> p (t e)")
                for j in range(2):
                    mm(PS[:, 5 + j, :], UPB[:], flat(SELB)[:, 512 * j:512 * (j + 1)], start=True, stop=False)
                    mm(PS[:, 5 + j, :], ONB[:], flat(CSB)[:, 512 * j:512 * (j + 1)], start=False, stop=True)
                mm(PS[:, 7, 0:E], ONB[:], SELB[:, TC - 1, :], start=True, stop=False)
                mm(PS[:, 7, 0:E], ONB[:], CSB[:, TC - 1, :], start=False, stop=True).then_inc(t_rank, 1)

            def experts(c):
                o = c * SS

                def T(i, r):
                    pe.wait_ge(e_ld[r], i * 4 + (4 * o + 16 - 4 * r))
                    for t in range(G):
                        ins = nc.tensor.transpose(PS[:, 0, t * P:(t + 1) * P], XB[r][:, t, 0:D], ID)
                    ins.then_inc(e_t, 1)

                def gu(i, r):
                    e = slot_experts(pe, c, i)
                    pe.wait_ge(e_te, o + i + 1)
                    for t in range(G):
                        ins = mm(gu_bank[r % 2][:, t, 0:2 * EI], EXT[:, t * P:(t + 1) * P], WGU[:, e[t], :],
                                 start=True, stop=True)
                    ins.then_inc(e_gu, 1)

                def hT(i):
                    pe.wait_ge(e_h, o + i + 2)
                    for t in range(G):
                        ins = nc.tensor.transpose(PS[0:EI, 5, t * P:(t + 1) * P], EH[:, t, :], ID)
                    ins.then_inc(e_ht, 1)

                def down(i, u):
                    e = slot_experts(pe, c, i)
                    pe.wait_ge(e_hte, o + i + 1)
                    if not isinstance(i, int) or i + o >= 2:
                        pe.wait_ge(e_ye, o + i - 1)
                    for t in range(G):
                        ins = mm(PS[:, 6 + u, t * D:(t + 1) * D], EHT[u][:, t * P:(t + 1) * P], WD[:, e[t], :],
                                 start=True, stop=True)
                    ins.then_inc(e_y, 1)

                T(0, 0)
                gu(0, 0)
                T(1, 1)
                gu(1, 1)
                hT(0)
                T(2, 2)

                def body(i, r):
                    gu(i + 1, (r + 1) % 4)
                    T(i + 2, (r + 2) % 4)
                    hT(i)
                    down(i - 1, (r - 1) % 2)
                body(1, 1)
                body(2, 2)
                with pe.Fori(0, (SS - 8) // 4) as q:
                    for r in range(4):
                        body(q * 4 + (3 + r), (3 + r) % 4)
                i = 3 + (SS - 8)
                while i + 2 < SS:
                    body(i, i % 4)
                    i += 1
                gu(SS - 1, 3)
                hT(SS - 2)
                down(SS - 3, 1)
                hT(SS - 1)
                down(SS - 2, 0)
                down(SS - 1, 1)

            for c in range(CHUNKS):
                if c == 0:
                    pass
                attention(c)
                if c == 0:
                    pe.wait_ge(ld_m, 32)
                mlp(c)
                if c == 0:
                    pe.wait_ge(ld_r, 48)
                route(c)
            pe.wait_ge(t_ter, 16 * CHUNKS)
            pe.wait_ge(ld_wgu, 16)
            pe.wait_ge(ld_wd, 16)
            pe.sem_inc(e_ht, 1)
            for c in range(CHUNKS):
                experts(c)
            layer2_pe(pe)


_OUT = "out"


def kernel(**inputs):
    import concourse.bacc as bacc
    from concourse.bass_utils import run_bass_kernel_spmd as run

    i = {k: np.asarray(v) for k, v in inputs.items()}
    t = np.ascontiguousarray
    rows = lambda *names: [np.broadcast_to(v.reshape(1, -1), (P, v.size)) for v in names]
    col = lambda v, n=P: v.reshape(n, -1)

    def padded(v):
        out = np.zeros((P, 1), np.float32)
        out[:v.size, 0] = v
        return out
    gates = np.stack([i["g_xattn"][0], i["g_ffn"][0], i["g_xattn"][1], i["g_ffn"][1]])
    con = np.zeros((P, C_HOT), np.float32)
    con[:, C_ID:C_ID + P] = np.eye(P)
    con[:, C_UP:C_UP + P] = np.triu(np.ones((P, P)), 1)
    con[:, C_LOW:C_LOW + 64] = np.tril(np.ones((NG, NG)), -1).reshape(-1)
    con[:, C_STEP:C_STEP + TC] = P * np.arange(TC)
    con[:, C_SLOT] = 2 * np.arange(P)
    con[:, C_SLOT + 1] = 2 * np.arange(P) + 1
    hot = np.zeros((P, E1, P), np.float32)
    for e in range(E1):
        hot[e:3 * E1:E1, e, :] = 1.0
    arrays = {
        "x": t(i["x"].transpose(1, 0, 2)),
        "ctx": t(i["ctx_1024"].transpose(1, 0, 2)),
        "wq": t(i["L0_xattn_wq"]),
        "wk": t(i["L0_xattn_wk"]),
        "wvT": t(i["L0_xattn_wv"].reshape(D, H, DH).transpose(2, 1, 0)),
        "wo": t(i["L0_xattn_wo"].reshape(H, DH, D).transpose(1, 0, 2)),
        "w1": t(i["L0_xattn_w1"]),
        "w2": t(i["L0_xattn_w2"].reshape(4, P, D).transpose(1, 0, 2).reshape(P, MLP)),
        "gwT": t(i["L0_ffn_gate_w"].T),
        "wgu": t(np.concatenate([i["L0_ffn_Wg"], i["L0_ffn_Wu"]], 1).transpose(2, 0, 1)),
        "wd": t(i["L0_ffn_Wd"].transpose(2, 0, 1)),
        "sgu": t(np.stack([i["L0_ffn_Sg"][:EI], i["L0_ffn_Su"][:EI], i["L0_ffn_Sg"][EI:], i["L0_ffn_Su"][EI:]])
                 .transpose(2, 0, 1)),
        "sd": t(i["L0_ffn_Sd"].reshape(D, 2, EI).transpose(2, 1, 0)),
        "wqT1": t(i["L1_xattn_Wq"].T),
        "wkT1": t(i["L1_xattn_Wk"].T),
        "wvT1": t(i["L1_xattn_Wv"].T),
        "gw1": t(i["L1_ffn_gate_w"].T),
        "w1e": t(i["L1_ffn_mlp1_w"][:, ::2].transpose(2, 0, 1)),
        "w2e": t(i["L1_ffn_mlp2_w"].transpose(2, 0, 1)),
        "b2s": t(np.concatenate([i["L1_ffn_mlp2_b"]] * 3)),
        "vec": t(np.concatenate([
            col(i["L0_xattn_ln1_g"]), col(i["L0_xattn_ln1_b"]), col(i["L0_xattn_ln2_g"]), col(i["L0_xattn_ln2_b"]),
            i["L0_xattn_b1"].reshape(4, P).T, col(i["L1_ffn_scale"]), i["L1_ffn_mlp1_b"][:, ::2].T,
            padded(i["L1_xattn_bq"]), padded(i["L1_xattn_bk"]), *rows(gates)], 1)),
        "rows": t(np.concatenate(rows(
            i["L0_xattn_ln1_g"], i["L0_xattn_ln1_b"], i["L0_xattn_bo"], i["L0_xattn_b2"], i["L1_xattn_bv"],
            i["L0_ffn_gate_bias"], i["L1_ffn_gate_b"]), 1)),
        "con": con,
        "hot": hot.reshape(P, E1 * P),
    }
    nc = bacc.Bacc("TRN2", target_bir_lowering=False, num_devices=1)
    a = {k: nc.dram_tensor("in_" + k, v.shape, mybir.dt.from_np(v.dtype), kind="ExternalInput").ap()
         for k, v in arrays.items()}
    a[_OUT] = nc.dram_tensor(_OUT, (P, B, D), F32, kind="ExternalOutput").ap()
    build(nc, a)
    r = run(nc, [{"in_" + k: v for k, v in arrays.items()}], core_ids=[0])
    return t(r.results[0][_OUT].transpose(1, 0, 2))
```

```python
import math
from contextlib import ExitStack

import numpy as np

import concourse.bass as bass
from concourse import mybir

F32 = mybir.dt.float32
BF16 = mybir.dt.bfloat16
I32 = mybir.dt.int32
U32 = mybir.dt.uint32
ALU = mybir.AluOpType
ACT = mybir.ActivationFunctionType
AX_X = mybir.AxisListType.X

P = 128
D = 128
B = 32
NC_CTX = 77
H, DH = 16, 64
MLP = 512
E, NG, EI = 64, 8, 88
TOPK, TOPG = 8, 4
E1, K1 = 16, 4
QK = 32
EPS = 1e-5
CHUNKS = 2
TC = B // CHUNKS
G = 4
GC = TC // G
SLOTS = TC * P * TOPK // P + E
SS = SLOTS // G
ROW = D + E
BIG = 65536.0
GONE = -1e30
LIMIT, ALPHA = 7.0, 1.702

V_LN1G, V_LN1B, V_LN2G, V_LN2B, V_B1, V_SCALE, V_BM1 = 0, 1, 2, 3, 4, 8, 9
V_BQ, V_BK, V_GATES, V_END = 25, 26, 27, 31
R_LN1G, R_LN1B, R_BO, R_B2, R_BV, R_GBIAS, R_GB1, R_END = 0, 128, 256, 384, 512, 640, 704, 720
C_ID, C_UP, C_STEP, C_SLOT, C_HOT = 0, 128, 256, 272, 274


class Steps:

    def __init__(self, sem, eng):
        self.sem, self.eng, self.base, self.k = sem, eng, 0, 0

    def done(self, ins):
        ins.then_inc(self.sem, 1)
        self.k += 1

    def wait(self):
        self.eng.wait_ge(self.sem, self.base + self.k)

    def step(self, ins):
        self.done(ins)
        self.wait()

    def loop(self, lo, hi, body, per):
        start = self.base + self.k
        with self.eng.Fori(lo, hi) as i:
            self.base, self.k = (i - lo) * per + start, 0
            body(i)
            assert self.k == per, self.k
        self.base, self.k = start + (hi - lo) * per, 0


def build(nc, a):
    one = lambda i: bass.ds(i, 1)
    ctx = ExitStack()
    with ctx:
        def sb(name, shape, dt=F32):
            return ctx.enter_context(nc.sbuf_tensor("sb_" + name, shape, dt))

        def sem(name):
            return ctx.enter_context(nc.semaphore(name))

        X = sb("X", [P, B, D])
        Yf = sb("Y", [P, B * D])
        Y = Yf[:, :].rearrange("p (b d) -> p b d", b=B)
        XR = sb("XR", [P, TC, ROW])
        WGU = sb("WGU", [P, E, 2 * EI])
        RW_ = sb("RW", [P, E * D])
        WD = RW_[0:EI, :].rearrange("p (e d) -> p e d", e=E)
        CTX = RW_[0:NC_CTX, 0:B * D].rearrange("p (b d) -> p b d", b=B)
        WVT = RW_[0:DH, B * D:B * D + H * D].rearrange("p (h d) -> p h d", h=H)
        WO = RW_[0:DH, B * D + H * D:B * D + 2 * H * D].rearrange("p (h d) -> p h d", h=H)
        AW = sb("AW", [P, 4096])
        WQ, WK = AW[:, 0:1024], AW[:, 1024:2048]
        WH = AW[:, 2048:4096].rearrange("p (h d) -> p h d", h=H)
        A1 = sb("A1", [P, 7 * 1024])
        RT5 = sb("RT5", [P, 5 * 1024])
        W1 = sb("W1", [P, MLP])
        W2 = sb("W2", [P, MLP])
        VEC = sb("VEC", [P, V_END])
        ROWS = sb("ROWS", [P, R_END])
        CON = sb("CON", [P, C_HOT])
        TG = sb("TG", [P, 4])
        GWT = sb("GWT", [P, E])
        SGW = sb("SGW", [P, 4, EI])
        SDW = sb("SDW", [EI, 2, D])
        UPB = sb("UPB", [P, P], BF16)
        ONB = sb("ONB", [P, P], BF16)
        SELB = sb("SELB", [P, TC, E], BF16)
        CSB = sb("CSB", [P, TC, E], BF16)
        POS = sb("POS", [P, B * TOPK], U32)
        TE = sb("TE", [P, CHUNKS, 2], I32)
        TER = sb("TER", [1, CHUNKS * SLOTS], I32)
        ZT = sb("ZT", [P, G * D])
        BS = sb("BS", [P, TC, 6])
        BSC = sb("BSC", [P, TC, 6])
        ST = sb("ST", [P, 7, TC])
        BSX = sb("BSX", [P, TC, 6])
        STX = sb("STX", [P, 3, TC])
        STC = sb("STC", [NC_CTX, 2, TC])
        N2 = sb("N2", [P, 2 * H])
        RN = sb("RN", [P, 2 * H])
        NT = sb("NT", [P, 4, E])
        PAUSE = sb("PAUSE", [P, 1])
        PS = ctx.enter_context(nc.psum_tensor("PS", [P, 8, 512], F32))

        ID = CON[:, C_ID:C_ID + P]
        SQQ, SQK, QN, KN, QT, PB, GB = (A1[:, 1024 * i:1024 * (i + 1)] for i in range(7))
        ZC, VN = RT5[0:NC_CTX, 1024:1024 + D], RT5[0:NC_CTX, 1152:1152 + D]
        QNT, KNT = RT5[:, 1280:1280 + D], RT5[:, 1408:1408 + NC_CTX]
        ZERO = RT5[:, 0:ROW]
        HT = A1[:, 0:2048].rearrange("p (c n) -> p c n", c=4)
        XT = A1[:, 2048:2560]
        TMP = A1[:, 2560:3072]
        SIL = A1[0:EI, 3072:4096].rearrange("p (c n) -> p c n", c=2)
        SHH = A1[0:EI, 4096:5120].rearrange("p (c n) -> p c n", c=2)
        RS, RC, RA, RB, RK = (RT5[:, 1024 * i:1024 * (i + 1)] for i in range(5))
        XB = [A1[:, 768 * i:768 * (i + 1)].rearrange("p (t n) -> p t n", t=G) for i in range(4)]
        EXT = A1[:, 3072:3584]
        ESI = A1[:, 3584:3584 + G * EI].rearrange("p (t n) -> p t n", t=G)
        EH = A1[:, 4096:4096 + G * EI].rearrange("p (t n) -> p t n", t=G)
        EHT = [A1[0:EI, 4608 + 512 * i:5120 + 512 * i] for i in range(2)]
        YB = [A1[:, 5632 + 512 * i:6144 + 512 * i].rearrange("p (t n) -> p t n", t=G) for i in range(2)]
        W1E = RT5[:, 0:2048].rearrange("p (e n) -> p e n", e=E1)
        W2E = RT5[:, 2048:4096].rearrange("p (e n) -> p e n", e=E1)
        LW = RT5[:, 4096:5120]
        WQT, WKT, WVT1, GW1 = LW[:, 0:32], LW[:, 32:64], LW[:, 64:192], LW[:, 192:208]
        B2S = LW[0:48, 208:336]
        HOT = XR[:, :, :].rearrange("p t n -> p (t n)")[:, 0:E1 * P // 2].bitcast(BF16)
        HOTF = XR[:, :, :].rearrange("p t n -> p (t n)")[:, E1 * P // 2:3 * E1 * P // 2]
        GBUF = [Yf[:, 1024 * i:1024 * (i + 1)] for i in range(4)]
        CG = AW[0:NC_CTX, 0:512].rearrange("p (t n) -> p t n", t=G)
        CT = AW[:, 512:512 + G * NC_CTX]
        KP = AW[0:QK, 1024:1024 + G * NC_CTX]
        VP = AW[0:NC_CTX, 1536:2048].rearrange("p (t n) -> p t n", t=G)
        QP = AW[0:QK, 2048:2560]
        ZS = AW[0:NC_CTX, 2560:3072]
        HM = [A1[:, 512 * i:512 * (i + 1)] for i in range(2)]
        SG = [A1[:, 1024 + 512 * i:1536 + 512 * i] for i in range(2)]
        XTL = A1[:, 2048:2560]
        SX = [A1[:, 3072 + 512 * i:3584 + 512 * i] for i in range(2)]
        AT = A1[:, 4096:4608]
        RED = A1[:, 6656:6656 + D]
        LB = WGU[:, :, :].rearrange("p e n -> p (e n)")
        TT, ZB = LB[:, 0:2048], LB[:, 2048:4096]
        RTF = LB[0:48, 4096:6144]
        RTB = LB[:, 6144:7168].bitcast(BF16)
        GL, GO = (LB[:, 7168 + 320 * i:7488 + 320 * i].rearrange("p (t e) -> p t e", t=TC) for i in range(2))
        GM8 = LB[:, 7808:7936].rearrange("p (t e) -> p t e", t=TC)
        GD, GSA, GSB, GSEL = (LB[:, 7936 + 256 * i:8192 + 256 * i] for i in range(4))
        R48 = LB[:, 8960:9728].rearrange("p (t j e) -> p t j e", t=TC, j=3)
        HIB = LB[:, 9728:9856].bitcast(BF16).rearrange("p (t e) -> p t e", t=TC)
        GSUM = LB[:, 9856:9856 + TC]

        xs = [nc.dram_tensor(f"sorted_rows{c}", [SLOTS * P, ROW], F32).ap() for c in range(CHUNKS)]
        ys = [nc.dram_tensor(f"sorted_out{c}", [SLOTS * P, D], F32).ap() for c in range(CHUNKS)]
        te_d = nc.dram_tensor("slot_experts", [CHUNKS, SLOTS], I32).ap()

        ld_c, ld_w, ld_m, ld_r, ld_wgu, ld_wd, ld_l, ld_hot = (sem(n) for n in (
            "ld_const", "ld_attn", "ld_mlp", "ld_route", "ld_wgu", "ld_wd", "ld_layer2", "ld_hot"))
        zeroed = sem("zeroed")
        ld_x = [sem(f"ld_tokens{i}") for i in range(CHUNKS)]
        dstep, astep = sem("dve_step"), sem("act_step")
        gates, wh_mm, wh_ok = sem("gates"), sem("wh_mm"), sem("wh_ok")
        cbf = sem("const_bf16")
        a_z, a_vn, a_t, a_qk, a_q, a_k, a_sq, a_n2, a_rt, a_qn, a_kn = (sem("attn_" + n) for n in (
            "z", "vn", "zT", "zT_out", "q", "k", "squares", "sums", "roots", "qn", "kn"))
        a_qt, a_qte, a_p, a_pe, a_g, a_ge, a_o, a_y = (sem("attn_" + n) for n in (
            "qT", "qT_out", "p", "p_out", "g", "g_out", "o", "y"))
        m_z, m_t, m_te, m_h, m_he, m_o, m_x = (sem("mlp_" + n) for n in (
            "z", "zT", "zT_out", "h", "gelu", "o", "x"))
        r_z, r_zc, r_t, r_te, r_l, r_le, r_gu, r_si, r_h, r_o, r_x = (sem("rt_" + n) for n in (
            "z", "z_row", "zT", "zT_out", "logit", "logit_out", "gu", "silu", "h", "o", "x"))
        t_s, t_sel, t_rank, t_rout, t_te, t_ted, t_ter, t_rw = (sem("tab_" + n) for n in (
            "sigmoid", "chosen", "ranks", "ranks_out", "slots", "slots_dram", "slots_row", "rows"))
        p_sc = [sem(f"scatter{i}") for i in range(2)]
        e_ld = [sem(f"ex_load{i}") for i in range(4)]
        e_t, e_te, e_gu, e_si, e_h, e_ht, e_hte, e_y, e_ye = (sem("ex_" + n) for n in (
            "xT", "xT_out", "gu", "silu", "h", "hT", "hT_out", "y", "y_out"))
        e_st = [sem(f"ex_store{i}") for i in range(2)]
        l_g = [sem(f"l2_gather{i}") for i in range(4)]
        l_red, l_cg, l_fin, l_out = sem("l2_reduced"), sem("l2_ctx"), sem("l2_final"), sem("l2_stored")
        l_dve = sem("l2_hot")
        l_h, l_hm, l_sg, l_sx, l_bc, l_y = (sem("l2_" + n) for n in ("h", "hmin", "glu", "weighted", "bcast", "y"))
        n_z, n_t, n_te, n_q, n_qe, n_ct, n_cte, n_kv, n_kpe, n_vpe, n_s, n_se, n_sh, n_o = (sem("l2f_" + n) for n in (
            "z", "zT", "zT_out", "q", "q_out", "ctxT", "ctxT_out", "kv", "k_out", "v_out", "scores", "tanh",
            "sigmoid", "o"))
        n_x, n_z2, n_t2, n_t2e, n_g, n_d, n_de, n_r, n_rt, n_rte, n_acce, n_f = (sem("l2r_" + n) for n in (
            "x", "z", "zT", "zT_out", "gate", "diff", "silu", "weights", "wT", "wT_out", "sum_out", "sumT"))

        block = ctx.enter_context(nc.Block())

        def bank(n, k=1, p0=0, p1=P):
            return PS[p0:p1, n:n + k, :].rearrange("p a n -> p (a n)")

        gu_bank = [PS[:, 1 + 2 * u:3 + 2 * u, :].rearrange("p a (c n) -> p (a c) n", c=2) for u in range(2)]

        def chunk_tiles(c):
            return c * TC, (c + 1) * TC

        def slot_experts(eng, c, i):
            return nc.values_load_multi_w_load_instructions(
                TER[0:1, bass.ds(i * G + c * SLOTS, G)], engines=[eng.engine], min_val=0, max_val=E - 1,
                skip_runtime_bounds_check_because="the table holds the lesser of a count and E - 1")[1]

        NGR = B // G
        RT_BANKS = (6, 5, 3, 2)

        def t3(x, n=G):
            return x.rearrange("p (t e) -> p t e", t=n)

        def layer2_act(act):
            def attention(c):
                lo, hi = c * GC, (c + 1) * GC

                def projections(g):
                    act.wait_ge(n_t, g + 1)
                    nc.scalar.activation(XTL, bank(0), ACT.Copy).then_inc(n_te, 1)
                    act.wait_ge(n_ct, g + 1)
                    nc.scalar.activation(CT, bank(1)[:, 0:G * NC_CTX], ACT.Copy).then_inc(n_cte, 1)
                    act.wait_ge(n_q, g + 1)
                    nc.scalar.activation(QP, bank(2, 1, 0, QK), ACT.Identity,
                                         bias=VEC[0:QK, V_BQ:V_BQ + 1]).then_inc(n_qe, 1)
                    act.wait_ge(n_kv, g + 1)
                    nc.scalar.activation(KP, bank(3, 1, 0, QK)[:, 0:G * NC_CTX], ACT.Identity,
                                         bias=VEC[0:QK, V_BK:V_BK + 1]).then_inc(n_kpe, 1)

                def scores(g):
                    act.wait_ge(n_s, g + 1)
                    nc.scalar.activation(ZS, bank(5, 1, 0, NC_CTX), ACT.Tanh,
                                         scale=0.5 / math.sqrt(QK)).then_inc(n_se, 1)

                projections(lo)
                with act.Fori(lo, hi - 1) as g:
                    scores(g)
                    projections(g + 1)
                scores(hi - 1)

            def route(c):
                for i in range(GC):
                    act.wait_ge(n_t2, c * GC + i + 1)
                    nc.scalar.activation(TT[:, i * 512:(i + 1) * 512], bank(i), ACT.Identity,
                                         scale=VEC[:, V_SCALE:V_SCALE + 1]).then_inc(n_t2e, 1)
                act.wait_ge(n_d, c + 1)
                nc.scalar.activation(GSA, GD, ACT.Silu)
                nc.scalar.activation(GSB, GD, ACT.Silu, scale=-1.0).then_inc(n_de, 1)
                for i in range(GC):
                    act.wait_ge(n_rt, c * GC + i + 1)
                    wT = bank(RT_BANKS[i], 1, 0, 48)
                    nc.scalar.activation(RTF[:, i * 512:(i + 1) * 512], wT, ACT.Copy)
                    nc.scalar.activation(RTB[0:48, i * 512:(i + 1) * 512], wT, ACT.Copy).then_inc(n_rte, 1)

            def experts(c):
                lo, hi = c * GC, (c + 1) * GC

                def sums(g):
                    act.wait_ge(l_y, g * E1 + (E1 + 2))
                    nc.scalar.activation(AT, PS[:, one(g % 2 + 4), :].rearrange("p a n -> p (a n)"),
                                         ACT.Copy).then_inc(n_acce, 1)

                def group(g, first=False):
                    for e in range(E1):
                        act.wait_ge(l_hm, g * E1 + (e + 3))
                        act.wait_ge(l_sx, g * E1 + (e + 1))
                        nc.scalar.activation(SG[e % 2], HM[e % 2], ACT.Silu, scale=ALPHA).then_inc(l_sg, 1)
                        if e == 1 and not first:
                            sums(g - 1)

                group(lo, True)
                with act.Fori(lo + 1, hi) as g:
                    group(g)
                sums(hi - 1)

            act.sem_inc(l_sg, 2)
            for c in range(CHUNKS):
                attention(c)
                route(c)
                experts(c)

        def layer2_dve(dve, S, bn, tile_stats, add_rows, add_to_x):
            v = nc.vector
            mean, rstd, both, t1, t2 = (ST[:, i, :] for i in range(5))
            sh = [P, TC, D]

            def attention(c):
                lo, hi = c * GC, (c + 1) * GC

                def z(g):
                    for t in range(G):
                        i = (g - lo) * G + t
                        ins = v.tensor_scalar(ZT[:, t * D:(t + 1) * D], X[:, g * G + t, :], mean[:, one(i)],
                                              rstd[:, one(i)], ALU.subtract, ALU.mult)
                    ins.then_inc(n_z, 1)

                def values(g):
                    dve.wait_ge(n_kv, g + 1)
                    v.tensor_tensor(VP, bank(4, 1, 0, NC_CTX).rearrange("p (t n) -> p t n", t=G),
                                    ROWS[0:NC_CTX, R_BV:R_BV + D].unsqueeze(1).to_broadcast([NC_CTX, G, D]),
                                    ALU.add).then_inc(n_vpe, 1)

                def sigmoid(g):
                    dve.wait_ge(n_se, g + 1)
                    v.tensor_scalar(ZS, ZS, 0.5, 0.5, ALU.mult, ALU.add).then_inc(n_sh, 1)

                def x(g):
                    dve.wait_ge(n_o, g + 1)
                    tiles = bass.ds(g * G, G)
                    v.scalar_tensor_tensor(X[:, tiles, :], t3(bank(6)), TG[:, 2:3], X[:, tiles, :], ALU.mult,
                                           ALU.add).then_inc(n_x, 1)
                    dve.wait_ge(n_x, g + 1)
                    bn(X, BS, ([(g - lo) * G + t for t in range(G)], [g * G + t for t in range(G)]))

                z(lo)
                values(lo)
                dve.wait_ge(n_t, lo + 1)
                z(lo + 1)
                if c == 0:
                    dve.wait_ge(ld_hot, 16)
                    v.tensor_copy(HOT, HOTF).then_inc(l_dve, 1)
                    S.done(v.memset(RTB, 0.0))
                    S.done(v.memset(GL[:, :, E1:E1 + 4], GONE))
                def body(g):
                    sigmoid(g)
                    dve.wait_ge(n_t, g + 2)
                    z(g + 2)
                    x(g)
                    values(g + 1)
                S.loop(lo, hi - 2, body, 1)
                sigmoid(hi - 2)
                x(hi - 2)
                values(hi - 1)
                sigmoid(hi - 1)
                dve.wait_ge(n_z, hi)
                tile_stats(slice(0, TC - G), True)
                x(hi - 1)

            def route(c):
                lo, hi = c * GC, (c + 1) * GC
                def z(g):
                    for t in range(G):
                        i = (g - lo) * G + t
                        ins = v.tensor_scalar(t3(ZB, TC)[:, i, :], X[:, g * G + t, :], mean[:, one(i)],
                                              both[:, one(i)], ALU.subtract, ALU.mult)
                    ins.then_inc(n_z2, 1)

                with dve.Fori(lo, hi - 1) as g:
                    z(g)
                tile_stats(slice(TC - G, TC), True)
                z(hi - 1)
                dve.wait_ge(n_g, c + 1)
                S.step(v.tensor_tensor(GL[:, :, 0:E1], t3(bank(7)[:, 0:TC * E1], TC),
                                       ROWS[:, R_GB1:R_GB1 + E1].unsqueeze(1).to_broadcast([P, TC, E1]), ALU.add))
                for t in range(TC):
                    ins = v.max(GM8[:, t, :], GL[:, t, 0:E1])
                S.step(ins)
                S.step(v.tensor_tensor(t3(GD, TC), GL[:, :, 0:E1], GM8[:, :, 0:1].to_broadcast([P, TC, E1]),
                                       ALU.subtract))
                v.tensor_scalar(GD, GD, -1.0, None, ALU.add).then_inc(n_d, 1)
                S.step(v.memset(GM8[:, :, K1:8], GONE))
                for t in range(TC):
                    ins = v.match_replace(GO[:, t, :], GM8[:, t, :], GL[:, t, :], 2 * GONE)
                S.step(ins)
                S.done(v.tensor_scalar(t3(GSEL, TC), GO[:, :, 0:E1], 2 * GONE, None, ALU.is_equal))
                dve.wait_ge(n_de, c + 1)
                S.step(v.reciprocal(GSB, GSB))
                S.step(v.tensor_tensor(GSA, GSA, GSB, ALU.mult))
                S.step(v.tensor_tensor(GSA, GSA, GSEL, ALU.mult))
                S.step(v.tensor_reduce(GSUM, t3(GSA, TC), AX_X, ALU.add))
                S.step(v.reciprocal(GSUM, GSUM))
                S.step(v.tensor_tensor(t3(GSA, TC), t3(GSA, TC), GSUM.unsqueeze(2).to_broadcast([P, TC, E1]), ALU.mult))
                S.step(v.tensor_copy(HIB, t3(GSA, TC)))
                S.step(v.tensor_copy(R48[:, :, 0, :], HIB))
                S.step(v.tensor_tensor(t3(GSA, TC), t3(GSA, TC), R48[:, :, 0, :], ALU.subtract))
                S.step(v.tensor_copy(HIB, t3(GSA, TC)))
                S.step(v.tensor_copy(R48[:, :, 1, :], HIB))
                v.tensor_tensor(R48[:, :, 2, :], t3(GSA, TC), R48[:, :, 1, :], ALU.subtract).then_inc(n_r, 1)
                dve.wait_ge(n_z2, hi)
                S.step(v.tensor_scalar(t1, rstd, TG[:, 3:4], None, ALU.mult))
                S.step(v.tensor_tensor(t2, t1, mean, ALU.mult))
                S.step(v.tensor_scalar(t1, t1, 1.0, None, ALU.add))
                xc = X[:, c * TC:(c + 1) * TC, :]
                S.step(v.tensor_tensor(xc, xc, t1.unsqueeze(2).to_broadcast(sh), ALU.mult))
                S.done(v.tensor_tensor(xc, xc, t2.unsqueeze(2).to_broadcast(sh), ALU.subtract))

            def experts(c):
                lo, hi = c * GC, (c + 1) * GC

                def x(g):
                    dve.wait_ge(n_f, g + 1)
                    tiles = bass.ds(g * G, G)
                    v.scalar_tensor_tensor(X[:, tiles, :], t3(bank(7)), TG[:, 3:4], X[:, tiles, :], ALU.mult, ALU.add).then_inc(l_fin, 1)

                def group(g, first=False):
                    for e in range(E1 + 2):
                        if e < E1:
                            dve.wait_ge(l_h, g * E1 + (e + 1))
                            dve.wait_ge(l_sg, g * E1 + (e + 1))
                            v.tensor_scalar(HM[e % 2], bank(e % 2), VEC[:, V_BM1 + e:V_BM1 + e + 1], LIMIT,
                                            ALU.add, ALU.min).then_inc(l_hm, 1)
                        if e >= 2:
                            k = e - 2
                            dve.wait_ge(l_sg, g * E1 + (k + 3))
                            dve.wait_ge(l_bc, g * E1 + (k + 1))
                            dve.wait_ge(l_y, g * E1 + (k + 1))
                            v.scalar_tensor_tensor(SX[k % 2], SG[k % 2], (LIMIT + 1.0) / ALPHA, bank(2 + k % 2),
                                                   ALU.mult, ALU.mult).then_inc(l_sx, 1)
                        if e == 5 and not first:
                            x(g - 1)
                        if c + 1 < CHUNKS and e >= 6 and e < 18:
                            r = e // 3 - 2
                            if e % 3 == 0:
                                add_rows(g * 4 + (TC + r), r)
                            if e % 3 == 1:
                                add_to_x(g * 4 + (TC + r), (c + 1) * TC)

                gathers = 2 * G if c + 1 < CHUNKS else 0
                group(lo, True)
                S.loop(lo + 1, hi, group, gathers)
                if gathers:
                    tile_stats(slice(0, TC))
                x(hi - 1)

            dve.wait_ge(ld_l, 16 * 7)
            dve.sem_inc(l_hm, 2)
            dve.sem_inc(l_sx, 2)
            for c in range(CHUNKS):
                attention(c)
                route(c)
                experts(c)

        def layer2_pe(pe):
            mm = nc.tensor.matmul

            def attention(c):
                lo, hi = c * GC, (c + 1) * GC

                def projections(g, first=False):
                    pe.wait_ge(n_z, g + 1)
                    for t in range(G):
                        ins = nc.tensor.transpose(PS[:, 0, t * P:(t + 1) * P], ZT[:, t * D:(t + 1) * D], ID)
                    ins.then_inc(n_t, 1)
                    pe.wait_ge(l_cg, g * 16 + 16)
                    for t in range(G):
                        ins = nc.tensor.transpose(PS[:, 1, t * NC_CTX:(t + 1) * NC_CTX], CG[:, t, :],
                                                  ID[0:NC_CTX, 0:NC_CTX])
                    ins.then_inc(n_ct, 1)
                    pe.wait_ge(n_te, g + 1)
                    mm(bank(2, 1, 0, QK), WQT, XTL, start=True, stop=True).then_inc(n_q, 1)
                    pe.wait_ge(n_cte, g + 1)
                    mm(bank(3, 1, 0, QK)[:, 0:G * NC_CTX], WKT, CT, start=True, stop=True)
                    if not first:
                        pe.wait_ge(n_vpe, g)
                    for t in range(G):
                        ins = mm(PS[0:NC_CTX, 4, t * D:(t + 1) * D], CT[:, t * NC_CTX:(t + 1) * NC_CTX], WVT1,
                                 start=True, stop=True)
                    ins.then_inc(n_kv, 1)

                def scores(g):
                    pe.wait_ge(n_qe, g + 1)
                    pe.wait_ge(n_kpe, g + 1)
                    for t in range(G):
                        ins = mm(PS[0:NC_CTX, 5, t * P:(t + 1) * P], KP[:, t * NC_CTX:(t + 1) * NC_CTX],
                                 QP[:, t * P:(t + 1) * P], start=True, stop=True)
                    ins.then_inc(n_s, 1)

                def out(g):
                    pe.wait_ge(n_sh, g + 1)
                    pe.wait_ge(n_vpe, g + 1)
                    for t in range(G):
                        ins = mm(PS[:, 6, t * D:(t + 1) * D], ZS[:, t * P:(t + 1) * P], VP[:, t, :],
                                 start=True, stop=True)
                    ins.then_inc(n_o, 1)

                projections(lo, lo == 0)
                with pe.Fori(lo, hi - 1) as g:
                    scores(g)
                    projections(g + 1)
                    out(g)
                scores(hi - 1)
                out(hi - 1)

            def route(c):
                def gate(i):
                    pe.wait_ge(n_t2e, c * GC + i + 1)
                    for t in range(i * G, (i + 1) * G):
                        ins = mm(PS[:, 7, t * E1:(t + 1) * E1], TT[:, t * P:(t + 1) * P], GW1, start=True, stop=True)
                    return ins

                for i in range(GC):
                    pe.wait_ge(n_z2, c * GC + i + 1)
                    for t in range(G):
                        ins = nc.tensor.transpose(PS[:, i, t * P:(t + 1) * P], t3(ZB, TC)[:, i * G + t, :], ID)
                    ins.then_inc(n_t2, 1)
                    if i:
                        gate(i - 1)
                gate(GC - 1).then_inc(n_g, 1)
                pe.wait_ge(l_dve, 1)
                pe.wait_ge(n_r, c + 1)
                for i in range(GC):
                    for t in range(G):
                        ins = nc.tensor.transpose(PS[0:48, RT_BANKS[i], t * P:(t + 1) * P],
                                                  R48[:, i * G + t, :, :].rearrange("p j e -> p (j e)"), ID)
                    ins.then_inc(n_rt, 1)

            def experts(c):
                lo, hi = c * GC, (c + 1) * GC

                def acc(g):
                    return PS[:, one(g % 2 + 4), :].rearrange("p a n -> p (a n)")

                def cols(x, g):
                    return x[:, bass.ds((g - lo) * 512, 512)]

                def sums(g):
                    pe.wait_ge(n_acce, g + 1)
                    for t in range(G):
                        ins = nc.tensor.transpose(PS[:, 7, t * P:(t + 1) * P], AT[:, t * P:(t + 1) * P], ID)
                    ins.then_inc(n_f, 1)

                def group(g, first=False):
                    pe.wait_ge(n_rte, g + 1)
                    for e in range(E1 + 3):
                        if e == 2 and first:
                            pe.wait_ge(n_rte, hi)
                        if e < E1:
                            pe.wait_ge(l_hm, g * E1 + (e + 1))
                            mm(bank(e % 2), W1E[:, e, :], cols(TT, g), start=True, stop=True).then_inc(l_h, 1)
                        if e == 0:
                            mm(acc(g), B2S, cols(RTF, g), start=True, stop=False)
                        if 2 <= e < E1 + 2:
                            k = e - 2
                            pe.wait_ge(l_sx, g * E1 + (k + 1))
                            mm(bank(2 + k % 2), HOT[:, k * P:(k + 1) * P], cols(RTB, g), start=True,
                               stop=True).then_inc(l_bc, 1)
                        if e >= 3:
                            k = e - 3
                            pe.wait_ge(l_sx, g * E1 + (k + 3))
                            mm(acc(g), W2E[:, k, :], SX[k % 2], start=False, stop=(k == E1 - 1)).then_inc(l_y, 1)
                        if e == 2 and not first:
                            sums(g - 1)

                group(lo, True)
                with pe.Fori(lo + 1, hi) as g:
                    group(g)
                sums(hi - 1)

            pe.wait_ge(ld_l, 16 * 7)
            pe.sem_inc(l_y, 2)
            for c in range(CHUNKS):
                attention(c)
                route(c)
                experts(c)

        @block.sync
        def _(sp):
            sp.dma_start(X[:, 0:TC, :], a["x"][:, 0:TC, :]).then_inc(ld_x[0], 16)
            sp.dma_start(CTX[:, 0:TC, :], a["ctx"][:, 0:TC, :]).then_inc(ld_x[0], 16)
            for dst, name in ((CON, "con"), (VEC, "vec"), (ROWS, "rows")):
                sp.dma_start(dst[:], a[name]).then_inc(ld_c, 16)
            sp.dma_start(WVT, a["wvT"]).then_inc(ld_w, 16)
            sp.dma_start(WO, a["wo"]).then_inc(ld_w, 16)
            sp.dma_start(WQ, a["wq"]).then_inc(ld_w, 16)
            sp.dma_start(WK, a["wk"]).then_inc(ld_w, 16)
            for c in range(1, CHUNKS):
                lo, hi = chunk_tiles(c)
                sp.dma_start(X[:, lo:hi, :], a["x"][:, lo:hi, :]).then_inc(ld_x[c], 16)
                sp.dma_start(CTX[:, lo:hi, :], a["ctx"][:, lo:hi, :]).then_inc(ld_x[c], 16)
            sp.dma_start(W1[:], a["w1"]).then_inc(ld_m, 16)
            sp.dma_start(W2[:], a["w2"]).then_inc(ld_m, 16)
            sp.dma_start(GWT[:], a["gwT"]).then_inc(ld_r, 16)
            sp.dma_start(SGW[:, :, :], a["sgu"]).then_inc(ld_r, 16)
            sp.dma_start(SDW[:, :, :], a["sd"]).then_inc(ld_r, 16)
            sp.wait_ge(cbf, 1)
            for c in range(CHUNKS):
                z = ZERO.unsqueeze(1).to_broadcast([P, SLOTS, ROW])
                sp.dma_start(xs[c].rearrange("(s p) n -> p s n", p=P), z).then_inc(zeroed, 16)
            sp.dma_start(WGU[:, :, :], a["wgu"]).then_inc(ld_wgu, 16)

            sp.wait_ge(a_y, B + 1)
            sp.dma_start(WD, a["wd"]).then_inc(ld_wd, 16)
            def rows_of(t, step):
                return t[bass.ds(step * (G * P), G * P), :].rearrange("(p t) n -> p t n", p=P)

            for c in range(CHUNKS):
                o = c * SS
                for i in range(2):
                    sp.wait_ge(p_sc[i], 16 * TOPK * (TC // 2) * (c + 1))

                def load(i, r):
                    sp.dma_start(XB[r][:, :, :], rows_of(xs[c], i)).then_inc(e_ld[r], 16)

                def store(i, r):
                    sp.wait_ge(e_ye, o + i + 1)
                    sp.dma_start(rows_of(ys[c], i), YB[r % 2][:, :, :]).then_inc(e_st[r % 2], 16)

                if c == 0:
                    sp.wait_ge(r_x, B // G)
                for i in range(4):
                    if c:
                        sp.wait_ge(e_h, o - 4 + i + 2)
                    load(i, i)
                if c == CHUNKS - 1:
                    sp.dma_start(HOTF, a["hot"]).then_inc(ld_hot, 16)

                def four(q):
                    for r in range(4):
                        sp.wait_ge(e_h, q * 4 + (o + r + 2))
                        load(q * 4 + (r + 4), r)
                        store(q * 4 + r, r)

                done = 0
                if c == 0:
                    for q, more in enumerate(((), ((W1E, "w1e"),), ((W2E, "w2e"),), ((WQT, "wqT1"), (WKT, "wkT1"),
                                              (WVT1, "wvT1"), (GW1, "gw1"), (B2S, "b2s")))):
                        four(q)
                        if q == 1:
                            sp.wait_ge(t_rw, CHUNKS)
                        for dst, name in more:
                            sp.dma_start(dst, a[name]).then_inc(ld_l, 16)
                    done = 4
                with sp.Fori(done, SS // 4 - 1) as q:
                    four(q)
                for r in range(4):
                    store(SS - 4 + r, r)
            sp.dma_start(CG[:, :, :], a["ctx"][:, 0:G, :]).then_inc(l_cg, 16)
            for c in range(CHUNKS):
                lo, hi = c * GC, (c + 1) * GC
                with sp.Fori(lo + 1, hi + 1 if hi < NGR else hi) as g:
                    sp.wait_ge(n_ct, g)
                    sp.dma_start(CG[:, :, :], a["ctx"][:, bass.ds(g * G, G), :]).then_inc(l_cg, 16)
                with sp.Fori(lo, hi) as g:
                    sp.wait_ge(l_fin, g + 1)
                    sp.dma_start(a["out"][:, bass.ds(g * G, G), :], X[:, bass.ds(g * G, G), :]).then_inc(l_out, 16)
            sp.wait_ge(l_out, 16 * NGR)

        @block.gpsimd
        def _(pool):
            def rows(c):
                if c:
                    for i in range(2):
                        pool.wait_ge(p_sc[i], 16 * TOPK * (TC // 2) * c)
                with pool.Fori(c * GC, (c + 1) * GC) as g:
                    pool.wait_ge(r_z, g + 1)
                    dst = XR[:, bass.ds(g * G - c * TC, G), 0:D]
                    nc.gpsimd.tensor_copy(dst, ZT[:, :].rearrange("p (t d) -> p t d", t=G)).then_inc(r_zc, 1)

            def scatter(c):
                pool.wait_ge(t_rw, c + 1)
                pool.wait_ge(r_zc, (c + 1) * GC)
                pool.wait_ge(zeroed, 16 * CHUNKS)
                lo, _ = chunk_tiles(c)
                for t in range(TC):
                    b = lo + t
                    if t == 0:
                        pool.dma_start(te_d[c].rearrange("(p k) -> p k", k=2),
                                       TE[0:SLOTS // 2, c, :]).then_inc(t_ted, 16)
                    if t == 2:
                        pool.wait_ge(t_ted, 16 * (c + 1))
                        pool.dma_start(TER[0:1, c * SLOTS:(c + 1) * SLOTS], te_d[c:c + 1, :]).then_inc(t_ter, 16)
                    for k in range(TOPK):
                        pool.indirect_dma_start(
                            out=xs[c], in_=XR[:, t, :], in_offset=None,
                            out_offset=bass.IndirectOffsetOnAxis(ap=POS[:, b * TOPK + k:b * TOPK + k + 1], axis=0),
                        ).then_inc(p_sc[t % 2], 16)

            def gather(c):
                lo, hi = chunk_tiles(c)
                for i in range(2):
                    pool.wait_ge(e_st[i], 16 * (SS // 2) * (c + 1))
                for b in range(lo, hi):
                    r = b % 4
                    if b >= 4:
                        pool.wait_ge(l_red, b - 3)
                    for k in range(TOPK):
                        pool.indirect_dma_start(
                            out=GBUF[r][:, k * D:(k + 1) * D], out_offset=None, in_=ys[c],
                            in_offset=bass.IndirectOffsetOnAxis(ap=POS[:, b * TOPK + k:b * TOPK + k + 1], axis=0),
                        ).then_inc(l_g[r], 16)

            for c in range(CHUNKS):
                rows(c)
                scatter(c)
            for c in range(CHUNKS):
                gather(c)

        @block.scalar
        def _(act):
            S = Steps(astep, act)
            act.wait_ge(ld_c, 48)
            nc.scalar.activation(TG[:], VEC[:, V_GATES:V_GATES + 4], ACT.Tanh).then_inc(gates, 1)
            for i in range(4):
                act.wait_ge(wh_mm, i + 1)
                nc.scalar.activation(AW[:, 2048 + 512 * i:2560 + 512 * i], bank(1 + i), ACT.Copy).then_inc(wh_ok, 1)

            def attention(c):
                lo, hi = chunk_tiles(c)

                def qk_in(b):
                    act.wait_ge(a_t, b + 1)
                    nc.scalar.activation(QNT, PS[:, 0, 0:P], ACT.Identity,
                                         bias=VEC[:, V_LN1B:V_LN1B + 1], scale=VEC[:, V_LN1G:V_LN1G + 1])
                    nc.scalar.activation(KNT, PS[:, 0, P:P + NC_CTX], ACT.Identity,
                                         bias=VEC[:, V_LN1B:V_LN1B + 1],
                                         scale=VEC[:, V_LN1G:V_LN1G + 1]).then_inc(a_qk, 1)

                def q_sq(b):
                    act.wait_ge(a_q, b + 1)
                    nc.scalar.activation(SQQ, bank(1, 2), ACT.Square).then_inc(a_sq, 1)

                def k_sq(b):
                    act.wait_ge(a_k, b + 1)
                    nc.scalar.activation(SQK[0:NC_CTX, :], bank(3, 2, 0, NC_CTX), ACT.Square).then_inc(a_sq, 1)

                def roots(b, j):
                    act.wait_ge(a_n2, b * 2 + (1 + j))
                    h = slice(j * H, (j + 1) * H)
                    nc.scalar.activation(RN[:, h], N2[:, h], ACT.Sqrt).then_inc(a_rt, 1)

                def out2(ready, done, dst, b):
                    act.wait_ge(ready, b + 1)
                    nc.scalar.activation(dst, bank(5, 2), ACT.Copy).then_inc(done, 1)

                def g_out(b, j):
                    act.wait_ge(a_g, b * 2 + (1 + j))
                    nc.scalar.activation(GB[:, 512 * j:512 * (j + 1)], bank(5 + j), ACT.Copy).then_inc(a_ge, 1)

                qk_in(lo)
                q_sq(lo)
                roots(lo, 0)
                k_sq(lo)
                roots(lo, 1)
                with act.Fori(lo, hi - 1) as b:
                    qk_in(b + 1)
                    out2(a_qt, a_qte, QT, b)
                    q_sq(b + 1)
                    out2(a_p, a_pe, PB, b)
                    roots(b + 1, 0)
                    k_sq(b + 1)
                    g_out(b, 0)
                    g_out(b, 1)
                    roots(b + 1, 1)
                out2(a_qt, a_qte, QT, hi - 1)
                out2(a_p, a_pe, PB, hi - 1)
                g_out(hi - 1, 0)
                g_out(hi - 1, 1)

            def mlp(c):
                lo, hi = c * GC, (c + 1) * GC

                def z_out(g):
                    act.wait_ge(m_t, g + 1)
                    nc.scalar.activation(XT, bank(0), ACT.Identity, bias=VEC[:, V_LN2B:V_LN2B + 1],
                                         scale=VEC[:, V_LN2G:V_LN2G + 1]).then_inc(m_te, 1)

                def gelu(g):
                    for n in range(4):
                        act.wait_ge(m_h, g * 4 + (n + 1))
                        nc.scalar.activation(HT[:, n, :], bank(1 + n), ACT.Gelu,
                                             bias=VEC[:, V_B1 + n:V_B1 + n + 1]).then_inc(m_he, 1)

                z_out(lo)
                gelu(lo)
                with act.Fori(lo, hi - 1) as g:
                    z_out(g + 1)
                    gelu(g + 1)

            def route(c):
                lo, hi = c * GC, (c + 1) * GC

                def z_out(g):
                    act.wait_ge(r_t, g + 1)
                    nc.scalar.activation(XT, bank(0), ACT.Copy).then_inc(r_te, 1)

                def silus(g):
                    for n in range(2):
                        act.wait_ge(r_gu, g * 2 + (n + 1))
                        nc.scalar.activation(SIL[:, n, :], bank(1 + 2 * n, 1, 0, EI), ACT.Silu).then_inc(r_si, 1)

                z_out(lo)
                silus(lo)
                with act.Fori(lo, hi - 1) as g:
                    z_out(g + 1)
                    silus(g + 1)
                act.wait_ge(r_le, (c + 1) * GC)
                nc.scalar.activation(RS, RS, ACT.Sigmoid).then_inc(t_s, 1)
                act.wait_ge(t_rank, c + 1)
                nc.scalar.activation(RA, bank(5, 2), ACT.Copy)
                nc.scalar.activation(NT[:, 1, :], bank(7)[:, 0:E], ACT.Copy).then_inc(t_rout, 1)

            def experts(c):
                o = c * SS

                def x_out(i):
                    act.wait_ge(e_t, o + i + 1)
                    nc.scalar.activation(EXT, bank(0), ACT.Copy).then_inc(e_te, 1)

                def silu(i, u):
                    act.wait_ge(e_gu, o + i + 1)
                    act.wait_ge(e_h, o + i + 1)
                    nc.scalar.activation(ESI, gu_bank[u][:, :, 0:EI], ACT.Silu).then_inc(e_si, 1)

                def hT_out(i, u):
                    act.wait_ge(e_ht, o + i + 2)
                    nc.scalar.activation(EHT[u], bank(5, 1, 0, EI), ACT.Copy).then_inc(e_hte, 1)

                def y_out(i, u, first=False):
                    act.wait_ge(e_y, o + i + 1)
                    if not first:
                        act.wait_ge(e_st[u], i * 8 + (16 * (o // 2) - 8 * u))
                    nc.scalar.activation(YB[u][:, :, :].rearrange("p t n -> p (t n)"), bank(6 + u),
                                         ACT.Copy).then_inc(e_ye, 1)

                x_out(0)
                silu(0, 0)
                x_out(1)
                silu(1, 1)
                x_out(2)
                hT_out(0, 0)

                def body(i, r, first=False):
                    x_out(i + 2)
                    silu(i + 1, (r + 1) % 2)
                    hT_out(i, r % 2)
                    y_out(i - 1, (r - 1) % 2, first)

                body(1, 1, c == 0)
                body(2, 2, c == 0)
                with act.Fori(0, (SS - 8) // 4) as q:
                    for r in range(4):
                        body(q * 4 + (3 + r), 3 + r)
                i = 3 + (SS - 8)
                while i + 2 < SS:
                    body(i, i % 4)
                    i += 1
                silu(SS - 1, 1)
                hT_out(SS - 2, 0)
                y_out(SS - 3, 1)
                hT_out(SS - 1, 1)
                y_out(SS - 2, 0)
                y_out(SS - 1, 1)

            for c in range(CHUNKS):
                attention(c)
                mlp(c)
                route(c)
            for c in range(CHUNKS):
                experts(c)
            layer2_act(act)

        @block.vector
        def _(dve):
            v = nc.vector
            S = Steps(dstep, dve)
            v.memset(ZERO, 0.0)
            S.done(v.memset(N2[:], 1.0))
            S.done(v.memset(ONB[:], 1.0))
            S.done(v.memset(NT[:, 3, :], 1.0))
            dve.sem_inc(a_y, 1)
            dve.sem_inc(m_x, 1)
            dve.wait_ge(ld_x[0], 32)

            def rsqrt(dst, src, tmp):
                S.step(v.tensor_scalar(tmp.bitcast(I32), src.bitcast(I32), 1, None, ALU.logical_shift_right))
                S.step(v.tensor_scalar(dst.bitcast(I32), tmp.bitcast(I32), -1, 0x5F3759DF, ALU.mult, ALU.add))
                for _ in range(3):
                    S.step(v.scalar_tensor_tensor(tmp, dst, -0.5, dst, ALU.mult, ALU.mult))
                    S.step(v.tensor_tensor(tmp, tmp, src, ALU.mult))
                    S.step(v.scalar_tensor_tensor(dst, tmp, 1.5, dst, ALU.add, ALU.mult))

            def norms(stats, mean, inv, work, twice=False):
                f = lambda k: stats[:, :, k]
                n = 2 if twice else 1
                w, t = work[:, 0:2], work[:, 2:4]
                S.done(v.tensor_tensor(mean, f(1), f(4), ALU.add))
                S.done(v.tensor_tensor(t[:, 0], f(1), f(4), ALU.subtract))
                S.step(v.tensor_tensor(w[:, 1], f(2), f(5), ALU.add))
                S.done(v.tensor_scalar(mean, mean, 0.5, None, ALU.mult))
                S.step(v.scalar_tensor_tensor(t[:, 0], t[:, 0], 0.25, t[:, 0], ALU.mult, ALU.mult))
                S.step(v.scalar_tensor_tensor(w[:, 1], w[:, 1], 1.0 / D, t[:, 0], ALU.mult, ALU.add))
                S.step(v.tensor_scalar(w[:, 0], w[:, 1], EPS, None, ALU.add))
                if twice:
                    S.step(v.scalar_tensor_tensor(w[:, 1], w[:, 0], EPS, w[:, 1], ALU.mult, ALU.add))
                rsqrt(inv[:, 0:n], w[:, 0:n], t[:, 0:n])

            def bn(src, dst, places):
                v.memset(PAUSE[:], 0.0)
                for i, j in zip(*places):
                    ins = v.bn_stats(dst[:, i, :], src[:, j, :])
                S.done(ins)

            mean, rstd = ST[:, 0, :], ST[:, 1, :]
            k = slice(0, NC_CTX)

            def tile_stats(tiles, rms=False):
                S.wait()
                norms(BS[:, tiles, :], mean[:, tiles], ST[:, 1:3, tiles], ST[:, 3:7, tiles], rms)

            def first_stats():
                def four(q):
                    for j in range(G):
                        v.bn_stats(BSX[:, q * G + j, :], X[:, q * G + j, :])
                        ins = v.bn_stats(BSC[k, q * G + j, :], CTX[:, q * G + j, :])
                    S.done(ins)
                S.loop(0, TC // G, four, 1)

            def attention_stats():
                S.wait()
                norms(BSX, STX[:, 0, :], STX[:, 1:3, :], ST[:, 3:7, :], True)
                norms(BSC[k], STC[:, 0, :], STC[:, 1:2, :], ST[k, 3:7, :])

            def attention(c):
                lo, hi = chunk_tiles(c)
                meanx, rstdx, bothx = (STX[:, i, :] for i in range(3))
                meanc, rstdc = (STC[:, i, :] for i in range(2))

                def z(b):
                    i = b - lo
                    v.tensor_scalar(ZT[:, 0:D], X[:, b, :], meanx[:, one(i)], bothx[:, one(i)], ALU.subtract, ALU.mult)
                    v.tensor_scalar(ZC, CTX[:, b, :], meanc[:, one(i)], rstdc[:, one(i)],
                                    ALU.subtract, ALU.mult).then_inc(a_z, 1)

                def next_z(b):
                    dve.wait_ge(a_t, b)
                    z(b)

                def next_stats(b):
                    v.bn_stats(BSX[:, b - lo, :], X[:, b + TC, :])
                    S.done(v.bn_stats(BSC[k, b - lo, :], CTX[:, b + TC, :]))

                def residual(b):
                    i = b - lo
                    S.step(v.tensor_scalar(Y[:, b, :], X[:, b, :], meanx[:, one(i)], rstdx[:, one(i)],
                                           ALU.subtract, ALU.mult))
                    S.done(v.tensor_tensor(Y[:, b, :], Y[:, b, :], ROWS[:, R_BO:R_BO + D], ALU.add))

                def vn(b):
                    i = b - lo
                    S.step(v.tensor_scalar(VN, CTX[:, b, :], meanc[:, one(i)], rstdc[:, one(i)],
                                           ALU.subtract, ALU.mult))
                    S.step(v.tensor_tensor(VN, VN, ROWS[k, R_LN1G:R_LN1G + D], ALU.mult))
                    v.tensor_tensor(VN, VN, ROWS[k, R_LN1B:R_LN1B + D], ALU.add).then_inc(a_vn, 1)

                def normalise(b, j, n, squares, src, dst, done):
                    h = slice(j * H, (j + 1) * H)
                    dve.wait_ge(a_sq, b * 2 + (1 + j))
                    v.tensor_reduce(N2[0:n, h], squares.rearrange("p (h d) -> p h d", h=H), AX_X,
                                    ALU.add).then_inc(a_n2, 1)
                    dve.wait_ge(a_rt, b * 2 + (1 + j))
                    S.step(v.tensor_scalar(RN[0:n, h], RN[0:n, h], 1e-12, None, ALU.max))
                    S.step(v.reciprocal(RN[0:n, h], RN[0:n, h]))
                    v.tensor_tensor(dst.rearrange("p (h d) -> p h d", h=H), src.rearrange("p (h d) -> p h d", h=H),
                                    RN[0:n, h].unsqueeze(2).to_broadcast([n, H, DH]), ALU.mult).then_inc(done, 1)

                def queries(b):
                    normalise(b, 0, P, SQQ, bank(1, 2), QN, a_qn)

                def keys(b):
                    normalise(b, 1, NC_CTX, SQK[k, :], bank(3, 2, 0, NC_CTX), KN[k, :], a_kn)

                def y(b):
                    dve.wait_ge(a_o, b + 1)
                    v.tensor_tensor(Y[:, b, :], bank(7)[:, 0:D], Y[:, b, :], ALU.add).then_inc(a_y, 1)
                    dve.wait_ge(a_y, b + 2)
                    bn(Y, BS, ([b - lo], [b]))

                z(lo)
                vn(lo)
                if c:
                    chosen_scores()
                    weights()
                    slot_counts(c - 1)
                    slot_table(c - 1)
                    positions()
                    eight_positions()
                    rows_of_positions(c - 1)
                queries(lo)
                keys(lo)
                next_z(lo + 1)

                def body(b, last=False):
                    if not last:
                        next_z(b + 2)
                    if c + 1 < CHUNKS:
                        next_stats(b)
                    residual(b)
                    queries(b + 1)
                    dve.wait_ge(a_p, b + 1)
                    vn(b + 1)
                    keys(b + 1)
                    if last:
                        residual(b + 1)
                        if c:
                            dve.wait_ge(r_z, c * GC)
                        tile_stats(slice(0, TC - 2))
                    y(b)
                if c + 1 < CHUNKS:
                    dve.wait_ge(ld_x[c + 1], 32)
                S.loop(lo, hi - 2, body, 10 if c + 1 < CHUNKS else 9)
                body(hi - 2, True)
                if c + 1 < CHUNKS:
                    next_stats(hi - 1)
                y(hi - 1)

            def mlp(c):
                lo, hi = c * GC, (c + 1) * GC

                def z(g):
                    for t in range(G):
                        i = (g - lo) * G + t
                        ins = v.tensor_scalar(ZT[:, t * D:(t + 1) * D], Y[:, g * G + t, :], mean[:, one(i)],
                                              rstd[:, one(i)], ALU.subtract, ALU.mult)
                    ins.then_inc(m_z, 1)

                def x(g):
                    dve.wait_ge(m_o, g + 1)
                    tiles = bass.ds(g * G, G)
                    tmp = TMP.rearrange("p (t d) -> p t d", t=G)
                    S.step(v.tensor_tensor(tmp, bank(5).rearrange("p (t d) -> p t d", t=G), Y[:, tiles, :], ALU.add))
                    S.step(v.tensor_tensor(tmp, tmp, ROWS[:, R_B2:R_B2 + D].unsqueeze(1).to_broadcast([P, G, D]),
                                           ALU.add))
                    v.scalar_tensor_tensor(X[:, tiles, :], tmp, TG[:, 0:1], X[:, tiles, :], ALU.mult,
                                           ALU.add).then_inc(m_x, 1)
                    dve.wait_ge(m_x, g + 2)
                    bn(X, BS, ([(g - lo) * G + t for t in range(G)], [g * G + t for t in range(G)]))

                z(lo)
                dve.wait_ge(m_t, lo + 1)
                z(lo + 1)
                tile_stats(slice(TC - 2, TC))
                if c + 1 < CHUNKS:
                    attention_stats()

                def body(g):
                    dve.wait_ge(m_t, g + 2)
                    z(g + 2)
                    x(g)
                S.loop(lo, hi - 2, body, 3)
                x(hi - 2)
                dve.wait_ge(m_z, hi)
                tile_stats(slice(0, TC - G))
                x(hi - 1)

            def route(c):
                lo, hi = c * GC, (c + 1) * GC
                if c:
                    for i in range(2):
                        dve.wait_ge(p_sc[i], 16 * TOPK * (TC // 2) * c)
                else:
                    dve.wait_ge(zeroed, 16 * CHUNKS)

                def z(g):
                    for t in range(G):
                        i = (g - lo) * G + t
                        ins = v.tensor_scalar(ZT[:, t * D:(t + 1) * D], X[:, g * G + t, :], mean[:, one(i)],
                                              rstd[:, one(i)], ALU.subtract, ALU.mult)
                    ins.then_inc(r_z, 1)

                def rest(g):
                    dve.wait_ge(r_l, g + 1)
                    v.tensor_copy(RS.rearrange("p (g n) -> p g n", g=GC)[:, g - lo, :], bank(7)[:, 0:G * E],
                                  ).then_inc(r_le, 1)
                    for n in range(2):
                        dve.wait_ge(r_si, g * 2 + (n + 1))
                        v.tensor_tensor(SHH[:, n, :], SIL[:, n, :], bank(2 + 2 * n, 1, 0, EI), ALU.mult).then_inc(r_h, 1)
                    dve.wait_ge(r_o, g + 1)
                    v.scalar_tensor_tensor(X[:, bass.ds(g * G, G), :], bank(5).rearrange("p (t d) -> p t d", t=G),
                                           TG[:, 1:2], X[:, bass.ds(g * G, G), :], ALU.mult, ALU.add).then_inc(r_x, 1)

                z(lo)
                tile_stats(slice(TC - G, TC))
                with dve.Fori(lo, hi - 1) as g:
                    dve.wait_ge(r_t, g + 1)
                    dve.wait_ge(r_zc, g + 1)
                    z(g + 1)
                    rest(g)
                rest(hi - 1)
                dve.wait_ge(r_zc, hi)
                choose(c)

            def choose(c):
                t3 = lambda x, n=TC: x.rearrange("p (t e) -> p t e", t=n)
                C = t3(RC)
                dve.wait_ge(t_s, c + 1)
                S.step(v.tensor_tensor(C, t3(RS), ROWS[:, R_GBIAS:R_GBIAS + E].unsqueeze(1).to_broadcast([P, TC, E]),
                                       ALU.add))
                c8 = RC.rearrange("p (n w) -> p n w", w=8)
                N = TC * NG
                hi0 = RA[:, 0:512].rearrange("p (n w) -> p n w", w=4)
                lo0 = RA[:, 512:1024].rearrange("p (n w) -> p n w", w=4)
                hi1 = RB[:, 0:256].rearrange("p (n w) -> p n w", w=2)
                lo1 = RB[:, 256:512].rearrange("p (n w) -> p n w", w=2)
                m1 = RB[:, 512:768].rearrange("p (n w) -> p n w", w=2)
                S.done(v.tensor_tensor(hi0, c8[:, :, 0:4], c8[:, :, 4:8], ALU.max))
                S.step(v.tensor_tensor(lo0, c8[:, :, 0:4], c8[:, :, 4:8], ALU.min))
                S.done(v.tensor_tensor(hi1, hi0[:, :, 0:2], hi0[:, :, 2:4], ALU.max))
                S.done(v.tensor_tensor(m1, hi0[:, :, 0:2], hi0[:, :, 2:4], ALU.min))
                S.step(v.tensor_tensor(lo1, lo0[:, :, 0:2], lo0[:, :, 2:4], ALU.max))
                S.step(v.tensor_tensor(lo1, lo1, m1, ALU.max))
                g12, gout = (RK[:, 192 * i:192 * (i + 1)].rearrange("p (t g) -> p t g", t=TC) for i in range(2))
                g8, gl, gm = (RK[:, 384 + 128 * i:512 + 128 * i] for i in range(3))
                pair = lambda x, i: x[:, :, i].rearrange("p (t g) -> p t g", t=TC)
                gl3, gm3, g83 = (x.rearrange("p (t g) -> p t g", t=TC) for x in (gl, gm, g8))
                S.done(v.memset(g12[:, :, NG:NG + TOPG], GONE))
                S.done(v.tensor_tensor(g12[:, :, 0:NG], pair(hi1, 0), pair(hi1, 1), ALU.max))
                S.done(v.tensor_tensor(gm3, pair(hi1, 0), pair(hi1, 1), ALU.min))
                S.step(v.tensor_tensor(gl3, pair(lo1, 0), pair(lo1, 1), ALU.max))
                S.step(v.tensor_tensor(gl, gl, gm, ALU.max))
                S.step(v.tensor_tensor(g12[:, :, 0:NG], g12[:, :, 0:NG], gl3, ALU.add))
                for t in range(TC):
                    ins = v.max(g83[:, t, :], g12[:, t, 0:NG])
                S.step(ins)
                S.step(v.memset(g83[:, :, TOPG:NG], GONE))
                for t in range(TC):
                    ins = v.match_replace(gout[:, t, :], g83[:, t, :], g12[:, t, :], 2 * GONE)
                S.step(ins)
                S.step(v.tensor_scalar(gl3, gout[:, :, 0:NG], 2 * GONE, None, ALU.is_equal))
                S.step(v.tensor_tensor(c8, c8, gl.unsqueeze(2).to_broadcast([P, N, 8]), ALU.mult))
                m8 = RK[:, 0:TC * 8].rearrange("p (t k) -> p t k", t=TC)
                A = t3(RA)
                for t in range(TC):
                    ins = v.max(m8[:, t, :], C[:, t, :])
                S.step(ins)
                for t in range(TC):
                    ins = v.match_replace(A[:, t, :], m8[:, t, :], C[:, t, :], GONE)
                S.step(ins)
                v.tensor_scalar(SELB[:, :, :], A, GONE, None, ALU.is_equal).then_inc(t_sel, 1)
                S.done(v.memset(CSB[:, 0, :], 0.0))
                dve.wait_ge(t_sel, 2 * c + 1)
                for t in range(1, TC):
                    S.wait()
                    ins = v.tensor_tensor(CSB[:, t, :], CSB[:, t - 1, :], SELB[:, t - 1, :], ALU.add)
                    if t < TC - 1:
                        S.done(ins)
                ins.then_inc(t_sel, 1)

            t16 = lambda x: x.rearrange("p (t e) -> p t e", t=TC)

            def chosen_scores():
                sm = RK[:, 512:512 + TC]
                S.step(v.tensor_tensor(t16(RS), t16(RS), SELB[:, :, :], ALU.mult))
                S.step(v.tensor_reduce(sm, t16(RS), AX_X, ALU.add))
                S.step(v.tensor_scalar(sm, sm, 1e-20, None, ALU.add))
                S.step(v.reciprocal(sm, sm))
                S.done(v.tensor_scalar(sm, sm, 2.5, None, ALU.mult))

            def weights():
                sm = RK[:, 512:512 + TC]
                S.wait()
                S.done(v.tensor_tensor(XR[:, :, D:ROW], t16(RS), sm.unsqueeze(2).to_broadcast([P, TC, E]), ALU.mult))

            nt, end, base = (NT[:, i, :] for i in range(3))

            def slot_counts(c):
                dve.wait_ge(t_rout, c + 1)
                S.wait()
                sh = [P, E, TC]
                big = RS.rearrange("p (e j) -> p e j", e=E)
                S.step(v.tensor_tensor(big, end.unsqueeze(2).to_broadcast(sh),
                                       CON[:, C_STEP:C_STEP + TC].unsqueeze(1).to_broadcast(sh), ALU.is_gt))
                S.done(v.tensor_reduce(nt, big, AX_X, ALU.add))

            def slot_table(c):
                S.wait()
                S.step(v.tensor_tensor_scan(end, NT[:, 3, :], nt, 0.0, ALU.mult, ALU.add))
                S.step(v.tensor_tensor(base, end, nt, ALU.subtract))
                S.done(v.tensor_scalar(base, base, -float(P), BIG, ALU.mult, ALU.add))
                n = SLOTS // 2
                for j in range(2):
                    w = RS[0:n, 64 * j:64 * j + 64]
                    S.done(v.tensor_scalar(w, end[0:n], CON[0:n, C_SLOT + j:C_SLOT + j + 1], None, ALU.is_le))
                S.wait()
                S.step(v.tensor_reduce(NT[0:n, 0, 0:2], RS[0:n, 0:128].rearrange("p (j e) -> p j e", j=2), AX_X, ALU.add))
                v.tensor_scalar(TE[0:n, c, :], NT[0:n, 0, 0:2], E - 1.0, None, ALU.min).then_inc(t_te, 1)

            def positions():
                S.wait()
                S.step(v.tensor_tensor(t16(RA), base.unsqueeze(1).to_broadcast([P, TC, E]), t16(RA), ALU.subtract))
                S.done(v.tensor_tensor(t16(RA), t16(RA), SELB[:, :, :], ALU.mult))

            def eight_positions():
                S.wait()
                for t in range(TC):
                    ins = v.max(t16(RK[:, 0:TC * 8])[:, t, :], t16(RA)[:, t, :])
                S.done(ins)

            def rows_of_positions(c):
                pos = POS[:, c * TC * TOPK:(c + 1) * TC * TOPK]
                slot, r4 = (RS[:, 128 * i:128 * (i + 1)].bitcast(U32) for i in range(2))
                S.wait()
                S.step(v.tensor_scalar(pos, RK[:, 0:TC * 8], -1.0, BIG, ALU.mult, ALU.add))
                S.done(v.tensor_scalar(slot, pos, 7, G - 1, ALU.logical_shift_right, ALU.bitwise_and))
                S.step(v.tensor_scalar(r4, pos, P - 1, 2, ALU.bitwise_and, ALU.logical_shift_left))
                S.step(v.tensor_tensor(slot, slot, r4, ALU.bitwise_or))
                S.step(v.tensor_scalar(pos, pos, 9, 9, ALU.logical_shift_right, ALU.logical_shift_left))
                v.tensor_tensor(pos, pos, slot, ALU.bitwise_or).then_inc(t_rw, 1)
                dve.wait_ge(t_rw, c + 1)

            def add_rows(b, r):
                dve.wait_ge(l_g[r], (b - r) * (4 * TOPK) + 16 * TOPK)
                S.done(v.tensor_reduce(RED, GBUF[r].rearrange("p (k d) -> p d k", k=TOPK), AX_X, ALU.add))

            def add_to_x(b, lo):
                S.wait()
                v.scalar_tensor_tensor(X[:, b, :], RED, TG[:, 1:2], X[:, b, :], ALU.mult, ALU.add).then_inc(l_red, 1)
                dve.wait_ge(l_red, b + 1)
                bn(X, BS, ([b - lo], [b]))

            def experts(c):
                o = c * SS

                dve.wait_ge(t_ter, 16 * (c + 1))

                def h(i, r):
                    e = slot_experts(dve, c, i)
                    dve.wait_ge(e_si, o + i + 1)
                    dve.wait_ge(e_ht, o + i + 1)
                    for t in range(G):
                        ins = v.scalar_tensor_tensor(EH[:, t, :], ESI[:, t, :], XB[r][:, t, one(e[t] + D)],
                                                     gu_bank[r % 2][:, t, EI:2 * EI], ALU.mult, ALU.mult)
                    ins.then_inc(e_h, 1)

                h(0, 0)

                def body(i, r):
                    h(i + 1, (r + 1) % 4)
                done = 0
                if not c:
                    last = CHUNKS - 1
                    done = 8
                    body(0, 0)
                    chosen_scores()
                    body(1, 1)
                    weights()
                    body(2, 2)
                    slot_counts(last)
                    body(3, 3)
                    slot_table(last)
                    body(4, 0)
                    positions()
                    body(5, 1)
                    eight_positions()
                    body(6, 2)
                    rows_of_positions(last)
                    body(7, 3)
                else:
                    done = 3 * 12
                    start = (c - 1) * TC

                    def twelve(q):
                        for r in range(12):
                            body(q * 12 + r, r % 4)
                            if r % 3 == 1:
                                add_rows(q * 4 + (start + r // 3), r // 3)
                            if r % 3 == 2:
                                add_to_x(q * 4 + (start + r // 3), start)
                    S.loop(0, 3, twelve, 8)
                    b = start + 12
                    for i in range(done, SS - 4):
                        body(i, i % 4)
                        if i % 3 == 1:
                            add_rows(b, b % 4)
                        if i % 3 == 2:
                            add_to_x(b, start)
                            b += 1
                    done = SS - 4
                if done < SS - 4:
                    with dve.Fori(done // 4, SS // 4 - 1) as q:
                        for r in range(4):
                            body(q * 4 + r, r)
                if c:
                    body(SS - 4, 0)
                    add_to_x(b, start)
                    body(SS - 3, 1)
                    add_rows(b + 1, (b + 1) % 4)
                    body(SS - 2, 2)
                    add_to_x(b + 1, start)
                    tile_stats(slice(0, TC))
                else:
                    for i in range(SS - 4, SS - 1):
                        body(i, i % 4)

            first_stats()
            attention_stats()
            dve.wait_ge(ld_c, 48)
            v.tensor_copy(UPB[:], CON[:, C_UP:C_UP + P]).then_inc(cbf, 1)
            dve.wait_ge(gates, 1)
            for c in range(CHUNKS):
                attention(c)
                mlp(c)
                route(c)
            dve.sem_inc(e_h, 1)
            for c in range(CHUNKS):
                experts(c)
            layer2_dve(dve, S, bn, tile_stats, add_rows, add_to_x)

        @block.tensor
        def _(pe):
            mm = nc.tensor.matmul
            pe.wait_ge(ld_c, 48)
            pe.wait_ge(ld_w, 64)
            for i in range(4):
                for j in range(4):
                    h = 4 * i + j
                    ins = mm(PS[:, 1 + i, j * D:(j + 1) * D], WVT[:, h, :], WO[:, h, :], start=True, stop=True)
                ins.then_inc(wh_mm, 1)
            pe.wait_ge(wh_ok, 4)

            def attention(c):
                lo, hi = chunk_tiles(c)

                def T(b):
                    pe.wait_ge(a_z, b + 1)
                    nc.tensor.transpose(PS[:, 0, 0:P], ZT[:, 0:D], ID)
                    nc.tensor.transpose(PS[:, 0, P:P + NC_CTX], ZC, ID[0:NC_CTX, 0:NC_CTX]).then_inc(a_t, 1)

                def q(b):
                    pe.wait_ge(a_qk, b + 1)
                    for j in range(2):
                        ins = mm(PS[:, 1 + j, :], QNT, WQ[:, 512 * j:512 * (j + 1)], start=True, stop=True)
                    ins.then_inc(a_q, 1)

                def k(b):
                    for j in range(2):
                        ins = mm(PS[0:NC_CTX, 3 + j, :], KNT, WK[:, 512 * j:512 * (j + 1)], start=True, stop=True)
                    ins.then_inc(a_k, 1)

                def qT(b):
                    pe.wait_ge(a_qn, b + 1)
                    for j in range(8):
                        ins = nc.tensor.transpose(bank(5, 2)[:, j * P:(j + 1) * P], QN[:, j * P:(j + 1) * P], ID)
                    ins.then_inc(a_qt, 1)

                def p(b):
                    pe.wait_ge(a_qte, b + 1)
                    pe.wait_ge(a_kn, b + 1)
                    pe.wait_ge(a_vn, b + 1)
                    for j in range(2):
                        ins = mm(PS[:, 5 + j, :], VN, KN[0:NC_CTX, 512 * j:512 * (j + 1)], start=True, stop=True)
                    ins.then_inc(a_p, 1)

                def g(b):
                    pe.wait_ge(a_pe, b + 1)
                    for h in range(H):
                        r = DH * (h % 2)
                        ins = mm(PS[r:r + DH, 5 + h // 8, (h // 2 % 4) * D:(h // 2 % 4 + 1) * D],
                                 PB[:, h * DH:(h + 1) * DH], WH[:, h, :], start=True, stop=True)
                        if h % 8 == 7:
                            ins.then_inc(a_g, 1)

                def o(b):
                    pe.wait_ge(a_y, b + 1)
                    for j in range(8):
                        if j % 4 == 0:
                            pe.wait_ge(a_ge, b * 2 + (1 + j // 4))
                        ins = mm(PS[:, 7, 0:D], QT[:, j * P:(j + 1) * P], GB[:, j * D:(j + 1) * D],
                                 start=(j == 0), stop=(j == 7))
                    ins.then_inc(a_o, 1)

                T(lo)
                q(lo)
                k(lo)
                with pe.Fori(lo, hi - 1) as b:
                    T(b + 1)
                    qT(b)
                    q(b + 1)
                    p(b)
                    k(b + 1)
                    g(b)
                    o(b)
                qT(hi - 1)
                p(hi - 1)
                g(hi - 1)
                o(hi - 1)

            def transposes(ready, done, g):
                pe.wait_ge(ready, g + 1)
                for t in range(G):
                    ins = nc.tensor.transpose(PS[:, 0, t * P:(t + 1) * P], ZT[:, t * D:(t + 1) * D], ID)
                ins.then_inc(done, 1)

            def mlp(c):
                lo, hi = c * GC, (c + 1) * GC

                def up(g):
                    pe.wait_ge(m_te, g + 1)
                    for n in range(4):
                        mm(bank(1 + n), W1[:, n * P:(n + 1) * P], XT, start=True, stop=True).then_inc(m_h, 1)

                def down(g):
                    pe.wait_ge(m_x, g + 1)
                    pe.wait_ge(m_he, g * 4 + 4)
                    for t in range(G):
                        for n in range(4):
                            ins = mm(PS[:, 5, t * D:(t + 1) * D], HT[:, n, t * P:(t + 1) * P],
                                     W2[:, n * D:(n + 1) * D], start=(n == 0), stop=(n == 3))
                    ins.then_inc(m_o, 1)

                transposes(m_z, m_t, lo)
                up(lo)
                with pe.Fori(lo, hi - 1) as g:
                    transposes(m_z, m_t, g + 1)
                    down(g)
                    up(g + 1)
                down(hi - 1)

            def route(c):
                lo, hi = c * GC, (c + 1) * GC

                def rest(g):
                    pe.wait_ge(r_te, g + 1)
                    for n in range(4):
                        ins = mm(bank(1 + n, 1, 0, EI), SGW[:, n, :], XT, start=True, stop=True)
                        if n % 2:
                            ins.then_inc(r_gu, 1)
                    for t in range(G):
                        ins = mm(PS[:, 7, t * E:(t + 1) * E], XT[:, t * P:(t + 1) * P], GWT[:], start=True, stop=True)
                    ins.then_inc(r_l, 1)

                def down(g):
                    pe.wait_ge(r_h, g * 2 + 2)
                    for t in range(G):
                        for n in range(2):
                            ins = mm(PS[:, 5, t * D:(t + 1) * D], SHH[:, n, t * P:(t + 1) * P], SDW[:, n, :],
                                     start=(n == 0), stop=(n == 1))
                    ins.then_inc(r_o, 1)

                transposes(r_z, r_t, lo)
                rest(lo)
                with pe.Fori(lo, hi - 1) as g:
                    transposes(r_z, r_t, g + 1)
                    down(g)
                    rest(g + 1)
                down(hi - 1)
                pe.wait_ge(t_sel, 2 * c + 2)
                flat = lambda x: x[:, :, :].rearrange("p t e -> p (t e)")
                for j in range(2):
                    mm(PS[:, 5 + j, :], UPB[:], flat(SELB)[:, 512 * j:512 * (j + 1)], start=True, stop=False)
                    mm(PS[:, 5 + j, :], ONB[:], flat(CSB)[:, 512 * j:512 * (j + 1)], start=False, stop=True)
                mm(PS[:, 7, 0:E], ONB[:], SELB[:, TC - 1, :], start=True, stop=False)
                mm(PS[:, 7, 0:E], ONB[:], CSB[:, TC - 1, :], start=False, stop=True).then_inc(t_rank, 1)
                pe.wait_ge(t_rout, c + 1)

            def experts(c):
                o = c * SS
                pe.wait_ge(t_ter, 16 * (c + 1))

                def T(i, r):
                    pe.wait_ge(e_ld[r], i * 4 + (4 * o + 16 - 4 * r))
                    for t in range(G):
                        ins = nc.tensor.transpose(PS[:, 0, t * P:(t + 1) * P], XB[r][:, t, 0:D], ID)
                    ins.then_inc(e_t, 1)

                def gu(i, r):
                    e = slot_experts(pe, c, i)
                    pe.wait_ge(e_te, o + i + 1)
                    for t in range(G):
                        ins = mm(gu_bank[r % 2][:, t, 0:2 * EI], EXT[:, t * P:(t + 1) * P], WGU[:, e[t], :],
                                 start=True, stop=True)
                    ins.then_inc(e_gu, 1)

                def hT(i):
                    pe.wait_ge(e_h, o + i + 2)
                    if not isinstance(i, int) or i + o >= 1:
                        pe.wait_ge(e_hte, o + i)
                    for t in range(G):
                        ins = nc.tensor.transpose(PS[0:EI, 5, t * P:(t + 1) * P], EH[:, t, :], ID)
                    ins.then_inc(e_ht, 1)

                def down(i, u):
                    e = slot_experts(pe, c, i)
                    pe.wait_ge(e_hte, o + i + 1)
                    if not isinstance(i, int) or i + o >= 2:
                        pe.wait_ge(e_ye, o + i - 1)
                    for t in range(G):
                        ins = mm(PS[:, 6 + u, t * D:(t + 1) * D], EHT[u][:, t * P:(t + 1) * P], WD[:, e[t], :],
                                 start=True, stop=True)
                    ins.then_inc(e_y, 1)

                T(0, 0)
                gu(0, 0)
                T(1, 1)
                gu(1, 1)
                hT(0)
                T(2, 2)

                def body(i, r):
                    gu(i + 1, (r + 1) % 4)
                    T(i + 2, (r + 2) % 4)
                    hT(i)
                    down(i - 1, (r - 1) % 2)
                body(1, 1)
                body(2, 2)
                with pe.Fori(0, (SS - 8) // 4) as q:
                    for r in range(4):
                        body(q * 4 + (3 + r), (3 + r) % 4)
                i = 3 + (SS - 8)
                while i + 2 < SS:
                    body(i, i % 4)
                    i += 1
                gu(SS - 1, 3)
                hT(SS - 2)
                down(SS - 3, 1)
                hT(SS - 1)
                down(SS - 2, 0)
                down(SS - 1, 1)

            for c in range(CHUNKS):
                attention(c)
                if c == 0:
                    pe.wait_ge(ld_m, 32)
                mlp(c)
                if c == 0:
                    pe.wait_ge(ld_r, 48)
                route(c)
            pe.wait_ge(ld_wgu, 16)
            pe.wait_ge(ld_wd, 16)
            pe.sem_inc(e_ht, 1)
            for c in range(CHUNKS):
                experts(c)
            layer2_pe(pe)


_OUT = "out"


def kernel(**inputs):
    import concourse.bacc as bacc
    from concourse.bass_utils import run_bass_kernel_spmd as run

    i = {k: np.asarray(v) for k, v in inputs.items()}
    t = np.ascontiguousarray
    rows = lambda *names: [np.broadcast_to(v.reshape(1, -1), (P, v.size)) for v in names]
    col = lambda v, n=P: v.reshape(n, -1)

    def padded(v):
        out = np.zeros((P, 1), np.float32)
        out[:v.size, 0] = v
        return out
    gates = np.stack([i["g_xattn"][0], i["g_ffn"][0], i["g_xattn"][1], i["g_ffn"][1]])
    con = np.zeros((P, C_HOT), np.float32)
    con[:, C_ID:C_ID + P] = np.eye(P)
    con[:, C_UP:C_UP + P] = np.triu(np.ones((P, P)), 1)
    con[:, C_STEP:C_STEP + TC] = P * np.arange(TC)
    con[:, C_SLOT] = 2 * np.arange(P)
    con[:, C_SLOT + 1] = 2 * np.arange(P) + 1
    hot = np.zeros((P, E1, P), np.float32)
    for e in range(E1):
        hot[e:3 * E1:E1, e, :] = 1.0
    arrays = {
        "x": t(i["x"].transpose(1, 0, 2)),
        "ctx": t(i["ctx_1024"].transpose(1, 0, 2)),
        "wq": t(i["L0_xattn_wq"]),
        "wk": t(i["L0_xattn_wk"]),
        "wvT": t(i["L0_xattn_wv"].reshape(D, H, DH).transpose(2, 1, 0)),
        "wo": t(i["L0_xattn_wo"].reshape(H, DH, D).transpose(1, 0, 2)),
        "w1": t(i["L0_xattn_w1"]),
        "w2": t(i["L0_xattn_w2"].reshape(4, P, D).transpose(1, 0, 2).reshape(P, MLP)),
        "gwT": t(i["L0_ffn_gate_w"].T),
        "wgu": t(np.concatenate([i["L0_ffn_Wg"], i["L0_ffn_Wu"]], 1).transpose(2, 0, 1)),
        "wd": t(i["L0_ffn_Wd"].transpose(2, 0, 1)),
        "sgu": t(np.stack([i["L0_ffn_Sg"][:EI], i["L0_ffn_Su"][:EI], i["L0_ffn_Sg"][EI:], i["L0_ffn_Su"][EI:]])
                 .transpose(2, 0, 1)),
        "sd": t(i["L0_ffn_Sd"].reshape(D, 2, EI).transpose(2, 1, 0)),
        "wqT1": t(i["L1_xattn_Wq"].T),
        "wkT1": t(i["L1_xattn_Wk"].T),
        "wvT1": t(i["L1_xattn_Wv"].T),
        "gw1": t(i["L1_ffn_gate_w"].T),
        "w1e": t(i["L1_ffn_mlp1_w"][:, ::2].transpose(2, 0, 1)),
        "w2e": t(i["L1_ffn_mlp2_w"].transpose(2, 0, 1)),
        "b2s": t(np.concatenate([i["L1_ffn_mlp2_b"]] * 3)),
        "vec": t(np.concatenate([
            col(i["L0_xattn_ln1_g"]), col(i["L0_xattn_ln1_b"]), col(i["L0_xattn_ln2_g"]), col(i["L0_xattn_ln2_b"]),
            i["L0_xattn_b1"].reshape(4, P).T, col(i["L1_ffn_scale"]), i["L1_ffn_mlp1_b"][:, ::2].T,
            padded(i["L1_xattn_bq"]), padded(i["L1_xattn_bk"]), *rows(gates)], 1)),
        "rows": t(np.concatenate(rows(
            i["L0_xattn_ln1_g"], i["L0_xattn_ln1_b"], i["L0_xattn_bo"], i["L0_xattn_b2"], i["L1_xattn_bv"],
            i["L0_ffn_gate_bias"], i["L1_ffn_gate_b"]), 1)),
        "con": con,
        "hot": hot.reshape(P, E1 * P),
    }
    nc = bacc.Bacc("TRN2", target_bir_lowering=False, num_devices=1)
    a = {k: nc.dram_tensor("in_" + k, v.shape, mybir.dt.from_np(v.dtype), kind="ExternalInput").ap()
         for k, v in arrays.items()}
    a[_OUT] = nc.dram_tensor(_OUT, (P, B, D), F32, kind="ExternalOutput").ap()
    build(nc, a)
    r = run(nc, [{"in_" + k: v for k, v in arrays.items()}], core_ids=[0])
    return t(r.results[0][_OUT].transpose(1, 0, 2))
```
